# Optimizing a Trainium2 kernel written in Bass

```python
import numpy as np
import jax
import jax.numpy as jnp

def _softmax(x, axis=-1):
    return jax.nn.softmax(x, axis=axis)

def _gelu(x):
    return jax.nn.gelu(x, approximate=True)

def _silu(x):
    return jax.nn.silu(x)

def _sigmoid(x):
    return jax.nn.sigmoid(x)

def _layernorm(x, axis=-1, eps=1e-05):
    m = jnp.mean(x, axis=axis, keepdims=True)
    v = jnp.var(x, axis=axis, keepdims=True)
    return (x - m) / jnp.sqrt(v + eps)

def _scatter_add(tgt, idx, src, axis=0):
    return tgt.at[idx].add(src)

def _segment_sum(src, seg, n):
    return jax.ops.segment_sum(src, seg, n)
kernel_name = 'mk_recurrent_d1_jaxref_r4_a97195'

def setup_inputs(seed: int=0):
    np.random.seed(seed)
    _w = jnp.asarray

    def _L0_attn_setup():
        import jax, jax.numpy as jnp
        import numpy as np
        LN_EPS = 1e-05
        ATTN_EPS = 1e-05

        def _ln(x, w, b):
            mu = x.mean(-1, keepdims=True)
            var = ((x - mu) ** 2).mean(-1, keepdims=True)
            return (x - mu) * jax.lax.rsqrt(var + LN_EPS) * w + b

        def _build_mask(heads, l):
            h2 = heads // 2
            slopes = 2.0 ** jnp.linspace(0.0, -8.0, h2)
            idx = jnp.arange(l)
            decay = -jnp.maximum(idx[:, None] - idx[None, :], 0).astype(jnp.float32)
            alibi = jnp.exp(slopes[:, None, None] * decay)
            return jnp.concatenate([alibi, jnp.ones((heads - h2, l, l), dtype=jnp.float32)], axis=0)
        key = jax.random.key(seed)
        ks = jax.random.split(key, 8)
        b, l, d_model = (2, 512, 256)
        heads, exp = (16, 2)
        d_exp = d_model * exp
        d_head = d_exp // heads
        depth = 12
        f32 = jnp.float32
        inp = {'x': jax.random.normal(ks[0], (b, l, d_model), dtype=f32), 'in_ln_w': jnp.ones((d_model,), f32), 'in_ln_b': jnp.zeros((d_model,), f32), 'q_ln_w': jnp.ones((d_model,), f32), 'q_ln_b': jnp.zeros((d_model,), f32), 'k_ln_w': jnp.ones((d_model,), f32), 'k_ln_b': jnp.zeros((d_model,), f32), 'out_ln_w': jnp.ones((d_model,), f32), 'out_ln_b': jnp.zeros((d_model,), f32), 'W_in': jax.random.normal(ks[1], (d_model, 2 * d_exp), f32) * 0.02, 'W_out': jax.random.normal(ks[2], (d_exp, d_model), f32) * (0.02 / np.sqrt(2 * depth)), 'Wq': jax.random.normal(ks[3], (d_model, d_exp), f32) * 0.02, 'bq': jax.random.normal(ks[4], (d_exp,), f32) * 0.02, 'Wk': jax.random.normal(ks[5], (d_model, d_exp), f32) * 0.02, 'bk': jax.random.normal(ks[6], (d_exp,), f32) * 0.02, 'smear_factor': jnp.linspace(-6.0, 6.0, heads).astype(f32), 'log_scale': jnp.full((heads,), 0.25 * np.log(d_head), f32)}
        return inp
    _L0_attn_in = _L0_attn_setup()

    def _L0_ffn_setup():
        import jax, jax.numpy as jnp
        import numpy as np
        DIM = 256
        DEPTH = 2
        HEADS = 8
        DIM_HEAD = 64
        WINDOW = 128
        INNER = HEADS * DIM_HEAD
        HID = int(DIM * 4 * 2 / 3)
        B, N = (2, 2048)
        QK_SCALE = 8.0

        def shift_token(t):
            t1, t2 = jnp.split(t, 2, axis=-1)
            t2 = jnp.pad(t2, ((0, 0), (1, 0), (0, 0)))[:, :-1]
            return jnp.concatenate([t1, t2], axis=-1)

        def l2norm(t):
            return t / jnp.clip(jnp.linalg.norm(t, axis=-1, keepdims=True), 1e-12)

        def rotate_half(x):
            x1, x2 = jnp.split(x, 2, axis=-1)
            return jnp.concatenate([-x2, x1], axis=-1)

        def rotary_xpos(q, k):
            n = q.shape[-2]
            half_idx = jnp.arange(0, DIM_HEAD, 2, dtype=jnp.float32)
            inv_freq = 1.0 / 10000.0 ** (half_idx / DIM_HEAD)
            t = jnp.arange(n, dtype=jnp.float32)
            freqs = t[:, None] * inv_freq[None, :]
            freqs = jnp.concatenate([freqs, freqs], axis=-1)
            base = (half_idx + 0.4 * DIM_HEAD) / (1.4 * DIM_HEAD)
            power = (t - n // 2) / float(WINDOW // 2)
            scale = base[None, :] ** power[:, None]
            scale = jnp.concatenate([scale, scale], axis=-1)
            cos, sin = (jnp.cos(freqs), jnp.sin(freqs))
            q = q * cos * scale + rotate_half(q) * sin * scale
            k = k * cos / scale + rotate_half(k) * sin / scale
            return (q, k)

        def local_attention(q, k, v):
            b, h, n, d = q.shape
            w = n // WINDOW
            bq = q.reshape(b, h, w, WINDOW, d) * QK_SCALE
            bk = k.reshape(b, h, w, WINDOW, d)
            bv = v.reshape(b, h, w, WINDOW, d)

            def look_around(t):
                p = jnp.pad(t, ((0, 0), (0, 0), (1, 0), (0, 0), (0, 0)))
                return jnp.concatenate([p[:, :, :w], p[:, :, 1:]], axis=3)
            bk, bv = (look_around(bk), look_around(bv))
            bt = jnp.arange(n).reshape(w, WINDOW)
            btp = jnp.pad(bt, ((1, 0), (0, 0)), constant_values=-1)
            btk = jnp.concatenate([btp[:w], btp[1:]], axis=1)
            sim = jnp.einsum('bhwid,bhwjd->bhwij', bq, bk)
            i = bt[:, :, None]
            j = btk[:, None, :]
            mask = (i < j) | (i > j + WINDOW) | (j == -1)
            sim = jnp.where(mask, -jnp.finfo(sim.dtype).max, sim)
            attn = jax.nn.softmax(sim, axis=-1)
            out = jnp.einsum('bhwij,bhwjd->bhwid', attn, bv)
            return out.reshape(b, h, n, d)

        def _layer(x, wqkv, qs, ksc, wo, lg, lb, w1, b1, w2, b2):
            b, n, _ = x.shape
            h = shift_token(x)
            qkv = h @ wqkv
            q, k, v = jnp.split(qkv, 3, axis=-1)
            to_heads = lambda t: t.reshape(b, n, HEADS, DIM_HEAD).transpose(0, 2, 1, 3)
            q, k, v = (to_heads(q), to_heads(k), to_heads(v))
            q = l2norm(q) * qs
            k = l2norm(k) * ksc
            q, k = rotary_xpos(q, k)
            o = local_attention(q, k, v)
            o = o.transpose(0, 2, 1, 3).reshape(b, n, INNER)
            x = x + o @ wo
            h = shift_token(x)
            mu = h.mean(-1, keepdims=True)
            var = h.var(-1, keepdims=True)
            h = (h - mu) / jnp.sqrt(var + 1e-05) * lg + lb
            h = h @ w1 + b1
            a, g = jnp.split(h, 2, axis=-1)
            h = a * jax.nn.gelu(g, approximate=False)
            x = x + h @ w2 + b2
            return x
        key = jax.random.key(seed)
        ks = jax.random.split(key, 6)
        return {'x': jax.random.normal(ks[0], (B, N, DIM), jnp.float32), 'wqkv': jax.random.normal(ks[1], (DEPTH, DIM, 3 * INNER), jnp.float32) * 0.02, 'q_scale': jnp.ones((DEPTH, DIM_HEAD), jnp.float32), 'k_scale': jnp.ones((DEPTH, DIM_HEAD), jnp.float32), 'wo': jax.random.normal(ks[2], (DEPTH, INNER, DIM), jnp.float32) * 0.02, 'ln_g': jnp.ones((DEPTH, DIM), jnp.float32), 'ln_b': jnp.zeros((DEPTH, DIM), jnp.float32), 'w1': jax.random.normal(ks[3], (DEPTH, DIM, 2 * HID), jnp.float32) * 0.02, 'b1': jnp.zeros((DEPTH, 2 * HID), jnp.float32), 'w2': jax.random.normal(ks[4], (DEPTH, HID, DIM), jnp.float32) * 0.02, 'b2': jnp.zeros((DEPTH, DIM), jnp.float32)}
    _L0_ffn_in = _L0_ffn_setup()
    _d = {'L0_attn_x': _L0_attn_in['x'], 'L0_attn_in_ln_w': _L0_attn_in['in_ln_w'], 'L0_attn_in_ln_b': _L0_attn_in['in_ln_b'], 'L0_attn_q_ln_w': _L0_attn_in['q_ln_w'], 'L0_attn_q_ln_b': _L0_attn_in['q_ln_b'], 'L0_attn_k_ln_w': _L0_attn_in['k_ln_w'], 'L0_attn_k_ln_b': _L0_attn_in['k_ln_b'], 'L0_attn_out_ln_w': _L0_attn_in['out_ln_w'], 'L0_attn_out_ln_b': _L0_attn_in['out_ln_b'], 'L0_attn_W_in': _L0_attn_in['W_in'], 'L0_attn_W_out': _L0_attn_in['W_out'], 'L0_attn_Wq': _L0_attn_in['Wq'], 'L0_attn_bq': _L0_attn_in['bq'], 'L0_attn_Wk': _L0_attn_in['Wk'], 'L0_attn_bk': _L0_attn_in['bk'], 'L0_attn_smear_factor': _L0_attn_in['smear_factor'], 'L0_attn_log_scale': _L0_attn_in['log_scale'], 'L0_ffn_wqkv': _L0_ffn_in['wqkv'], 'L0_ffn_q_scale': _L0_ffn_in['q_scale'], 'L0_ffn_k_scale': _L0_ffn_in['k_scale'], 'L0_ffn_wo': _L0_ffn_in['wo'], 'L0_ffn_ln_g': _L0_ffn_in['ln_g'], 'L0_ffn_ln_b': _L0_ffn_in['ln_b'], 'L0_ffn_w1': _L0_ffn_in['w1'], 'L0_ffn_b1': _L0_ffn_in['b1'], 'L0_ffn_w2': _L0_ffn_in['w2'], 'L0_ffn_b2': _L0_ffn_in['b2']}
    _x0 = _d['L0_attn_x']
    _d['L0_attn_x'] = jax.random.normal(jax.random.fold_in(jax.random.key(seed), 1), (1, 4096, 256), dtype=_x0.dtype)
    del _x0
    return _d

def reference(L0_attn_x, L0_attn_in_ln_w, L0_attn_in_ln_b, L0_attn_q_ln_w, L0_attn_q_ln_b, L0_attn_k_ln_w, L0_attn_k_ln_b, L0_attn_out_ln_w, L0_attn_out_ln_b, L0_attn_W_in, L0_attn_W_out, L0_attn_Wq, L0_attn_bq, L0_attn_Wk, L0_attn_bk, L0_attn_smear_factor, L0_attn_log_scale, L0_ffn_wqkv, L0_ffn_q_scale, L0_ffn_k_scale, L0_ffn_wo, L0_ffn_ln_g, L0_ffn_ln_b, L0_ffn_w1, L0_ffn_b1, L0_ffn_w2, L0_ffn_b2):

    def _L0_attn_ref(x, in_ln_w, in_ln_b, q_ln_w, q_ln_b, k_ln_w, k_ln_b, out_ln_w, out_ln_b, W_in, W_out, Wq, bq, Wk, bk, smear_factor, log_scale):
        import jax, jax.numpy as jnp
        import numpy as np
        LN_EPS = 1e-05
        ATTN_EPS = 1e-05

        def _ln(x, w, b):
            mu = x.mean(-1, keepdims=True)
            var = ((x - mu) ** 2).mean(-1, keepdims=True)
            return (x - mu) * jax.lax.rsqrt(var + LN_EPS) * w + b

        def _build_mask(heads, l):
            h2 = heads // 2
            slopes = 2.0 ** jnp.linspace(0.0, -8.0, h2)
            idx = jnp.arange(l)
            decay = -jnp.maximum(idx[:, None] - idx[None, :], 0).astype(jnp.float32)
            alibi = jnp.exp(slopes[:, None, None] * decay)
            return jnp.concatenate([alibi, jnp.ones((heads - h2, l, l), dtype=jnp.float32)], axis=0)
        b, l, d_model = x.shape
        heads = smear_factor.shape[0]
        d_exp = W_in.shape[1] // 2
        d_head = d_exp // heads
        vp = _ln(x, in_ln_w, in_ln_b) @ W_in
        v, p = jnp.split(vp, 2, axis=-1)
        q = _ln(x, q_ln_w, q_ln_b) @ Wq + bq
        k = _ln(x, k_ln_w, k_ln_b) @ Wk + bk

        def to_heads(t):
            return t.reshape(b, l, heads, d_head).transpose(0, 2, 1, 3)
        q, k, v = (to_heads(q), to_heads(k), to_heads(v))
        q = jax.nn.softmax(q, axis=-1)
        k = jax.nn.softmax(k, axis=-1)
        smear = jax.nn.sigmoid(smear_factor)[None, :, None, None]
        k_prev = jnp.pad(k, ((0, 0), (0, 0), (1, 0), (0, 0)))[:, :, :l, :]
        k = (1.0 - smear) * k + smear * k_prev
        s = jnp.exp(log_scale)[None, :, None, None]
        q = q / s
        k = k / s
        mask = _build_mask(heads, l)
        attn = jnp.tril(jnp.einsum('bhid,bhjd->bhij', q, k) * mask)
        norm = 1.0 / (attn.sum(axis=-1) + ATTN_EPS)
        o = jnp.einsum('bhij,bhjd->bhid', attn * norm[..., None], v)
        o = o.transpose(0, 2, 1, 3).reshape(b, l, d_exp)
        out = _ln(jax.nn.silu(p) * o @ W_out, out_ln_w, out_ln_b)
        return out

    def _L0_ffn_ref(x, wqkv, q_scale, k_scale, wo, ln_g, ln_b, w1, b1, w2, b2):
        import jax, jax.numpy as jnp
        import numpy as np
        DIM = 256
        DEPTH = 2
        HEADS = 8
        DIM_HEAD = 64
        WINDOW = 128
        INNER = HEADS * DIM_HEAD
        HID = int(DIM * 4 * 2 / 3)
        B, N = (2, 2048)
        QK_SCALE = 8.0

        def shift_token(t):
            t1, t2 = jnp.split(t, 2, axis=-1)
            t2 = jnp.pad(t2, ((0, 0), (1, 0), (0, 0)))[:, :-1]
            return jnp.concatenate([t1, t2], axis=-1)

        def l2norm(t):
            return t / jnp.clip(jnp.linalg.norm(t, axis=-1, keepdims=True), 1e-12)

        def rotate_half(x):
            x1, x2 = jnp.split(x, 2, axis=-1)
            return jnp.concatenate([-x2, x1], axis=-1)

        def rotary_xpos(q, k):
            n = q.shape[-2]
            half_idx = jnp.arange(0, DIM_HEAD, 2, dtype=jnp.float32)
            inv_freq = 1.0 / 10000.0 ** (half_idx / DIM_HEAD)
            t = jnp.arange(n, dtype=jnp.float32)
            freqs = t[:, None] * inv_freq[None, :]
            freqs = jnp.concatenate([freqs, freqs], axis=-1)
            base = (half_idx + 0.4 * DIM_HEAD) / (1.4 * DIM_HEAD)
            power = (t - n // 2) / float(WINDOW // 2)
            scale = base[None, :] ** power[:, None]
            scale = jnp.concatenate([scale, scale], axis=-1)
            cos, sin = (jnp.cos(freqs), jnp.sin(freqs))
            q = q * cos * scale + rotate_half(q) * sin * scale
            k = k * cos / scale + rotate_half(k) * sin / scale
            return (q, k)

        def local_attention(q, k, v):
            b, h, n, d = q.shape
            w = n // WINDOW
            bq = q.reshape(b, h, w, WINDOW, d) * QK_SCALE
            bk = k.reshape(b, h, w, WINDOW, d)
            bv = v.reshape(b, h, w, WINDOW, d)

            def look_around(t):
                p = jnp.pad(t, ((0, 0), (0, 0), (1, 0), (0, 0), (0, 0)))
                return jnp.concatenate([p[:, :, :w], p[:, :, 1:]], axis=3)
            bk, bv = (look_around(bk), look_around(bv))
            bt = jnp.arange(n).reshape(w, WINDOW)
            btp = jnp.pad(bt, ((1, 0), (0, 0)), constant_values=-1)
            btk = jnp.concatenate([btp[:w], btp[1:]], axis=1)
            sim = jnp.einsum('bhwid,bhwjd->bhwij', bq, bk)
            i = bt[:, :, None]
            j = btk[:, None, :]
            mask = (i < j) | (i > j + WINDOW) | (j == -1)
            sim = jnp.where(mask, -jnp.finfo(sim.dtype).max, sim)
            attn = jax.nn.softmax(sim, axis=-1)
            out = jnp.einsum('bhwij,bhwjd->bhwid', attn, bv)
            return out.reshape(b, h, n, d)

        def _layer(x, wqkv, qs, ksc, wo, lg, lb, w1, b1, w2, b2):
            b, n, _ = x.shape
            h = shift_token(x)
            qkv = h @ wqkv
            q, k, v = jnp.split(qkv, 3, axis=-1)
            to_heads = lambda t: t.reshape(b, n, HEADS, DIM_HEAD).transpose(0, 2, 1, 3)
            q, k, v = (to_heads(q), to_heads(k), to_heads(v))
            q = l2norm(q) * qs
            k = l2norm(k) * ksc
            q, k = rotary_xpos(q, k)
            o = local_attention(q, k, v)
            o = o.transpose(0, 2, 1, 3).reshape(b, n, INNER)
            x = x + o @ wo
            h = shift_token(x)
            mu = h.mean(-1, keepdims=True)
            var = h.var(-1, keepdims=True)
            h = (h - mu) / jnp.sqrt(var + 1e-05) * lg + lb
            h = h @ w1 + b1
            a, g = jnp.split(h, 2, axis=-1)
            h = a * jax.nn.gelu(g, approximate=False)
            x = x + h @ w2 + b2
            return x
        for l in range(DEPTH):
            x = _layer(x, wqkv[l], q_scale[l], k_scale[l], wo[l], ln_g[l], ln_b[l], w1[l], b1[l], w2[l], b2[l])
        return x
    x = L0_attn_x
    xn = _layernorm(x, axis=-1)
    s = _L0_attn_ref(xn, L0_attn_in_ln_w, L0_attn_in_ln_b, L0_attn_q_ln_w, L0_attn_q_ln_b, L0_attn_k_ln_w, L0_attn_k_ln_b, L0_attn_out_ln_w, L0_attn_out_ln_b, L0_attn_W_in, L0_attn_W_out, L0_attn_Wq, L0_attn_bq, L0_attn_Wk, L0_attn_bk, L0_attn_smear_factor, L0_attn_log_scale)
    g = _silu(_L0_ffn_ref(xn, L0_ffn_wqkv, L0_ffn_q_scale, L0_ffn_k_scale, L0_ffn_wo, L0_ffn_ln_g, L0_ffn_ln_b, L0_ffn_w1, L0_ffn_b1, L0_ffn_w2, L0_ffn_b2))
    x = x + s * g
    return x

_drawn_inputs = setup_inputs


def setup_inputs(seed=0):
    import zlib

    import numpy as np

    out = dict(_drawn_inputs(seed))
    spreads = {'L0_attn_in_ln_w': (1.0, 0.2),
     'L0_attn_in_ln_b': (0.0, 0.1),
     'L0_attn_q_ln_w': (1.0, 0.6),
     'L0_attn_q_ln_b': (0.0, 0.8),
     'L0_attn_k_ln_w': (1.0, 0.6),
     'L0_attn_k_ln_b': (0.0, 0.8),
     'L0_attn_out_ln_w': (1.0, 0.2),
     'L0_attn_out_ln_b': (0.0, 0.1),
     'L0_attn_log_scale': (0.8664339780807495, 0.6),
     'L0_ffn_q_scale': (1.0, 0.6),
     'L0_ffn_k_scale': (1.0, 0.6),
     'L0_ffn_ln_g': (1.0, 0.6),
     'L0_ffn_ln_b': (0.0, 0.8),
     'L0_ffn_b1': (0.0, 0.8),
     'L0_ffn_b2': (0.0, 0.387)}
    factors = {'L0_attn_Wq': 8.0,
     'L0_attn_bq': 8.0,
     'L0_attn_Wk': 8.0,
     'L0_attn_bk': 8.0,
     'L0_attn_smear_factor': 8.0,
     'L0_ffn_wqkv': 6.938,
     'L0_ffn_wo': 6.83,
     'L0_ffn_w1': 4.447,
     'L0_ffn_w2': 4.432}
    for name, (base, spread) in spreads.items():
        noise = np.random.default_rng([zlib.crc32(name.encode()), seed]).standard_normal(out[name].shape)
        drawn = base * np.exp(spread * noise) if base else spread * noise
        out[name] = jnp.asarray(drawn.astype(out[name].dtype))
    for name, factor in factors.items():
        out[name] = (out[name] * factor).astype(out[name].dtype)
    return out
```

```python
from contextlib import ExitStack

import numpy as np

import concourse.bass as bass
from concourse import mybir

F32 = mybir.dt.float32
ALU = mybir.AluOpType
ACT = mybir.ActivationFunctionType
AX_X = mybir.AxisListType.X

P = 128
D = 256
DC = D // P
TOKENS = 4096
NW = TOKENS // P
LAYERS = 2
NORM_ROWS = 10 * DC
UNITS = LAYERS * NW
EPS = 1e-5
MH, MD = 16, 32
ME = MH * MD
MG = ME // P
MR = P // MD
MV = MD + 1
H, HD = 8, 64
E = H * HD
HP = H // 2
QK_SCALE = 8.0
HID = int(D * 4 * 2 / 3)
HC = -(-HID // P)
HIDP = HC * P
TAIL = HID - (HC - 1) * P

ROWS = NORM_ROWS + LAYERS * 2 * HC

MASKED = -1e30

STEP_HEADS = {"a0": (0, 2), "a1": (1, 3), "b0": (4, 6), "b1": (5, 7)}


def constants():
    f = np.float32
    slopes = (f(2.0) ** np.linspace(0.0, -8.0, MH // 2, dtype=f)).astype(f)
    slopes = np.concatenate([slopes, np.zeros(MH - MH // 2, f)])
    t = np.arange(P, dtype=f)
    j, i = t[:, None], t[None, :]
    causal = (i >= j).astype(f)
    decay = np.zeros((P, MR, MG // 2, P), f)
    for r in range(MR):
        for g in range(MG // 2):
            decay[:, r, g, :] = np.exp(-slopes[g * MR + r] * np.maximum(i - j, 0)) * causal
    query = np.zeros((P, MG // 2, P), f)
    whole = np.zeros((P, MG), f)
    for r in range(MR):
        for g in range(MG):
            if g < MG // 2:
                query[r * MD:(r + 1) * MD, g, :] = np.exp(-slopes[g * MR + r] * (t + 1))[None, :]
            whole[r * MD:(r + 1) * MD, g] = np.exp(-slopes[g * MR + r] * f(P))
    key = np.repeat(np.exp(-slopes[None, :] * (P - 1 - t[:, None])), MD, axis=1).astype(f)
    own = np.where(i <= j, f(0), f(MASKED)).astype(f)
    before = np.where(i >= j, f(0), f(MASKED)).astype(f)
    none = np.full((P, P), MASKED, f)
    masks = np.stack([np.concatenate([own, before], 1), np.concatenate([before, own], 1),
                      np.concatenate([own, none], 1)], 1)
    shift = np.zeros((P, P), f)
    shift[np.arange(P - 1), np.arange(1, P)] = 1
    carry = np.zeros((P, P), f)
    carry[P - 1, 0] = 1
    parts = {
        "ident": np.eye(P, dtype=f), "shift": shift, "carry": carry, "causal": causal,
        "decay": decay.reshape(P, -1), "query": query.reshape(P, -1), "whole": whole,
        "key": key, "masks": masks.reshape(P, -1),
    }
    at, n = {}, 0
    for name, a in parts.items():
        at[name] = (n, n + a.shape[1])
        n += a.shape[1]
    table = np.ascontiguousarray(np.concatenate(list(parts.values()), 1).astype(f))
    half = np.arange(0, HD, 2, dtype=f)
    inv = (f(1.0) / f(10000.0) ** (half / f(HD))).astype(f)
    pos = np.arange(TOKENS, dtype=f)
    ang = (pos[:, None] * inv[None, :]).astype(f)
    base = ((half + f(0.4 * HD)) / f(1.4 * HD)).astype(f)
    power = ((pos - TOKENS // 2) / f(P // 2)).astype(f)
    scale = (base[None, :] ** power[:, None]).astype(f)
    cos, sin = np.cos(ang), np.sin(ang)
    rot = np.stack([cos * scale, cos / scale, sin * scale, sin / scale], 1).astype(f)
    return table, at, np.ascontiguousarray(rot.reshape(TOKENS, -1))


class Unit:

    def __init__(self, k, c, low):
        self.k, self.c, self.low = k, c, low
        self.parity = c % 2

    def number(self):
        return 2 * self.k + self.c

    def back(self, d):
        return Unit(self.k, self.c - d, self.low - d)

    def exists(self):
        return self.low >= 0

    def turn(self):
        return self.k + self.c // 2


class Steps:

    def __init__(self, sem, names):
        self.sem, self.names, self.next = sem, names.split(), 0

    def done(self, name):
        assert self.names[self.next] == name, (self.names[self.next], name)
        self.next = (self.next + 1) % len(self.names)
        return self.sem

    def at(self, name, unit):
        return len(self.names) * unit.number() + self.names.index(name) + 1


def build(nc, x_d, in_w, in_b, q_w, q_b, k_w, k_b, out_w, out_b, W_in, W_out, Wq, bq, Wk, bk,
          smear, log_scale, wqkv, q_scale, k_scale, wo, ln_g, ln_b, w1, b1, w2, b2,
          table_d, rot_d, table_at, out_d):
    TW = table_d.shape[1]
    x2_d = nc.dram_tensor("x2_between_layers", [TOKENS, D], F32, kind="Internal").ap()
    s_d = nc.dram_tensor("s_between_passes", [TOKENS, D], F32, kind="Internal").ap()
    x_f = x_d.rearrange("a t d -> (a t) d")
    out_f = out_d.rearrange("a t d -> (a t) d")

    with ExitStack() as ctx:
        def sb(name, shape):
            return ctx.enter_context(nc.sbuf_tensor(name, shape, F32))

        def sem(name):
            return ctx.enter_context(nc.semaphore(name))

        table = sb("table", [P, TW])

        def tab(name):
            a, b = table_at[name]
            return table[:, a:b]

        ident = tab("ident")
        decay = tab("decay").rearrange("p (r g i) -> p r g i", r=MR, g=MG // 2)
        causal = tab("causal")
        query_decay = tab("query").rearrange("p (g i) -> p g i", g=MG // 2)
        whole_decay = tab("whole")
        key_decay = tab("key")
        masks = tab("masks").rearrange("p (m j) -> p m j", m=3)
        win_s = sb("win_s", [P, DC, 2 * ME])
        wq_s = sb("wq_s", [P, DC, ME])
        wk_s = sb("wk_s", [P, DC, ME])
        wout_s = sb("wout_s", [P, ME // P, D])
        wqkv_s = [sb(f"wqkv_s{l}", [P, DC, 3 * E]) for l in range(LAYERS)]
        wo_s = [sb(f"wo_s{l}", [P, E // P, D]) for l in range(LAYERS)]
        w1_s = [sb(f"w1_s{l}", [P, DC, 2 * HIDP]) for l in range(LAYERS)]
        w2_s = [sb(f"w2_s{l}", [P, HC, D]) for l in range(LAYERS)]
        b1_s = [sb(f"b1_s{l}", [P, 2 * HC]) for l in range(LAYERS)]
        b2_s = [sb(f"b2_s{l}", [P, D]) for l in range(LAYERS)]
        rot_scale = [sb(f"rot_scale{l}", [P, 4, 2, HD // 2]) for l in range(LAYERS)]
        bias_mix = sb("bias_mix", [P, 4, ME])
        out_w_s = sb("out_w_s", [P, D])
        out_b_s = sb("out_b_s", [P, D])
        cols = sb("cols", [P, ROWS])
        head_scale = sb("head_scale", [P, MH])
        head_eps = sb("head_eps", [P, MH])
        smear_s = sb("smear_s", [P, MG])
        keep_s = sb("keep_s", [P, MG])
        half_neg = sb("half_neg", [P, 16])
        zero_col = sb("zero_col", [P, 1])
        paced = sb("paced", [P, 1])

        x_s = sb("x_s", [P, 2, D])
        xn = sb("xn", [P, 2, D])
        xh = sb("xh", [P, D])
        xhT = sb("xhT", [P, DC, P])
        stats_x = sb("stats_x", [P, 6])
        mv_x = sb("mv_x", [P, 2])
        small_x = sb("small_x", [P, 4])
        mix_work = sb("mix_work", [P, 4 * 4 * P])
        qk = mix_work[:, 0:2 * ME]
        p_lin = mix_work[:, 2 * ME:3 * ME]
        p_tanh = mix_work[:, 3 * ME:4 * ME]
        att = mix_work[:, :].rearrange("p (r g i) -> p r g i", r=MR, g=MG)
        gate = sb("gate", [P, ME])
        qk_max = sb("qk_max", [P, 2 * MH])
        qk_sum = sb("qk_sum", [P, 2 * MH])
        k_norm = sb("k_norm", [P, MH])
        q_eps = sb("q_eps", [P, MH])
        v_mix = sb("v_mix", [P, MH, MV])
        qT_mix = sb("qT_mix", [P, MG, P])
        qT_dec = sb("qT_dec", [P, MG // 2, P])
        kT_raw = sb("kT_raw", [P, MG, P + 1])
        kT_mix = sb("kT_mix", [P, MG, P])
        kT_prev = sb("kT_prev", [P, MG * P])
        go = kT_prev
        k_dec = sb("k_dec", [P, ME])
        goT = k_dec[:, :].rearrange("p (g i) -> p g i", g=MG)
        state = sb("state", [P, MG, MR * MV])
        o_den = sb("o_den", [P, 2, 2 * MR])
        o_rec = sb("o_rec", [P, 2, 2 * MR])
        stats_y = sb("stats_y", [P, 6])
        mv_y = sb("mv_y", [P, 2])
        small_y = sb("small_y", [P, 2])
        y_n = sb("y_n", [P, D])
        s_out = sb("s_out", [P, D])

        rot_s = sb("rot_s", [P, 2, 4, HD // 2])
        rot_t = sb("rot_t", [P, 4, 2, HD // 2])
        xT = sb("xT", [P, DC, P + 1])
        raw = sb("raw", [P, 2 * E])
        rot = sb("rot", [P, 2 * E])
        rot_other = sb("rot_other", [P, 2 * E])
        sq_sum = sb("sq_sum", [P, 2 * H])
        sq_clip = sb("sq_clip", [P, 2 * H])
        inv_norm = sb("inv_norm", [P, 2, 2 * H])
        v_loc = sb("v_loc", [P, 2, E])
        qT = sb("qT", [P, 2, HP, P])
        kT = sb("kT", [P, HP, 2, P])

        x_res = sb("x_res", [P, 2, D])
        prob = sb("prob", [P, H, 2 * P])
        row_max = sb("row_max", [P, H])
        neg_max = sb("neg_max", [P, H])
        row_sum = sb("row_sum", [P, H])
        row_inv = sb("row_inv", [P, H])
        pT = sb("pT", [P, 2, 4, P])
        oT = sb("oT", [P, HP, P])
        x1 = sb("x1", [P, 2, D])
        x1b = sb("x1b", [P, 2, D])

        stats_h = sb("stats_h", [P, 12])
        mv_h = sb("mv_h", [P, 2])
        small_h = sb("small_h", [P, 2])
        h_n = sb("h_n", [P, D])
        rows_in = h_n[0:ROWS, 0:P]
        hT_n = sb("hT_n", [P, DC, P])
        gel = sb("gel", [P, HC, P])
        hid = sb("hid", [P, HC, P])
        x2 = sb("x2", [P, D])
        s_in = s_out
        x_in = y_n
        y_tanh = gel[:, 0:2, :].rearrange("p a b -> p (a b)")
        y_out = sb("y_out", [P, D])

        bank = [ctx.enter_context(nc.psum_tensor(f"bank{i}", [P, 512], F32)) for i in range(8)]
        mix_bank = bank[0:2]
        proj_bank = bank[2]
        att_bank = bank[3:6]
        mlp_bank = bank[6:8]

        mix_pe = Steps(sem("mix_pe"), "xt p q k v qt kt kb s0 s1 s2 s3 o0 o1 st0 st1 gt wout")
        mix_act = Steps(sem("mix_act"), "xt tanh exp qt halo kt gt")
        mix_dve = Steps(sem("mix_dve"), "p q gate k max v sum kscale kinv qeps kprev ksmear kdec "
                        "s0 s1 s2 s3 den0 rec0 o0 go0 den1 rec1 o1 go1 st0 st1 "
                        "ystat yaggr yvar yn")
        mix_pool = Steps(sem("mix_pool"), "sub kn qdec kkeep sdec yrstd yw s")
        norm_dve = Steps(sem("norm_dve"), "stat aggr var xn sq var2 xh")
        norm_pool = Steps(sem("norm_pool"), "rstd rstd2")
        proj_pe = Steps(sem("proj_pe"), "xt q k qt kt v")
        proj_act = Steps(sem("proj_act"), "halo xt q k square qt kt v")
        proj_dve = Steps(sem("proj_dve"), "sqsum clip cos rot knorm")
        proj_pool = Steps(sem("proj_pool"), "table other inv")
        att_pe = Steps(sem("att_pe"), "sa0 sa1 sb0 ta0 ta1 sb1 pva tb0 tb1 pvb wo")
        att_act = Steps(sem("att_act"), "ea0 ea1 eb0 ta0 ta1 eb1 pva tb0 tb1 pvb")
        att_dve = Steps(sem("att_dve"), "sa0 ma0 sa1 ma1 sb0 mb0 ra0 na0 ra1 na1 rb0 nb0 sb1 mb1 "
                        "rb1 nb1 x1")
        att_pool = Steps(sem("att_pool"), "x1b")
        mlp_pe = Steps(sem("mlp_pe"), "sh ht g0 a0 ga w2")
        mlp_act = Steps(sem("mlp_act"), "ht g0 ga")
        mlp_dve = Steps(sem("mlp_dve"), "stat aggr var hn a0 ga x2")
        mlp_pool = Steps(sem("mlp_pool"), "rstd")
        fin_act = Steps(sem("fin_act"), "tanh")
        fin_dve = Steps(sem("fin_dve"), "u us out")
        x_loaded = [sem(f"x_loaded{i}") for i in range(2)]
        rot_loaded = [sem(f"rot_loaded{i}") for i in range(2)]
        res_loaded = [sem(f"res_loaded{i}") for i in range(2)]
        s_loaded = sem("s_loaded")
        xin_loaded = sem("xin_loaded")
        s_stored = sem("s_stored")
        x2_stored = sem("x2_stored")
        out_stored = sem("out_stored")
        table_loaded = sem("table_loaded")
        small_loaded = sem("small_loaded")
        mix_w_loaded = sem("mix_w_loaded")
        layer_w_loaded = [sem(f"layer_w_loaded{l}") for l in range(LAYERS)]
        pads_zeroed = sem("pads_zeroed")
        setup_pe = Steps(sem("setup_pe"), "cols vp q k b1_0 b1_1")
        setup_act = Steps(sem("setup_act"), "scale smear")
        setup_dve = Steps(sem("setup_dve"), "cols spread bias wscale rneg rcopy smear1 smear2 keep eps half "
                          "b1_0 w1_0 b1_1 w1_1")
        setup_pool = sem("setup_pool")

        SMALL_DMAS = 18 + 13
        MIX_W_DMAS = 4
        LAYER_W_DMAS = 7
        POOL_SETUP = 6
        ONCE = Unit(0, 0, 0)

        block = ctx.enter_context(nc.Block())
        row = lambda u: bass.ds(u.number() * P, P)
        window = lambda u: u if u.low < NW else u.back(NW)
        layer = lambda u: 0 if u.low < NW else 1

        def iterations(eng, body):
            edge = 4
            for first, last in ((0, NW), (NW, UNITS)):
                for i in range(first, first + edge):
                    body(Unit(i // 2, i % 2, i))
                low = first + edge
                with eng.Fori(low // 2, last // 2 - 1) as k:
                    body(Unit(k, 0, low))
                    body(Unit(k, 1, low))
                for i in range(last - 2, last):
                    body(Unit(i // 2, i % 2, i))
            for i in range(UNITS, UNITS + 2):
                body(Unit(i // 2, i % 2, i))

        def norm_cols(n):
            return cols[:, n * DC:(n + 1) * DC]

        def streams(i):
            return (i if i.low < NW else None,
                    i if i.low < UNITS else None,
                    i.back(1) if 1 <= i.low < UNITS + 1 else None,
                    i.back(2) if i.low >= 2 else None)

        @block.sync
        def _(sp):
            sp.dma_start(x_s[:, 0, :], x_f[0:P, :]).then_inc(x_loaded[0], 16)
            sp.dma_start(rot_s[:, 0, :, :].rearrange("p a f -> p (a f)"), rot_d[0:P, :]).then_inc(rot_loaded[0], 16)
            sp.dma_start(table[:, :], table_d).then_inc(table_loaded, 16)
            sp.wait_ge(pads_zeroed, 5)
            vectors = [in_w, in_b, q_w, q_b, k_w, k_b, ln_g[0], ln_b[0], ln_g[1], ln_b[1]]
            for n, v in enumerate(vectors):
                sp.dma_start(rows_in[n * DC:(n + 1) * DC, :], v.rearrange("(c p) -> c p", p=P)).then_inc(small_loaded, 16)
            for l in range(LAYERS):
                for a in range(2):
                    at = NORM_ROWS + (2 * l + a) * HC
                    v = b1[l][a * HID:(a + 1) * HID]
                    full = (HC - 1) * P
                    sp.dma_start(rows_in[at:at + HC - 1, :], v[0:full].rearrange("(m p) -> m p", p=P)).then_inc(small_loaded, 16)
                    sp.dma_start(rows_in[at + HC - 1:at + HC, 0:TAIL], v[full:HID].unsqueeze(0)).then_inc(small_loaded, 16)
            sp.dma_start(win_s[:, :, :], W_in.rearrange("(c p) n -> p c n", p=P)).then_inc(mix_w_loaded, 16)
            sp.dma_start(wq_s[:, :, :], Wq.rearrange("(c p) n -> p c n", p=P)).then_inc(mix_w_loaded, 16)
            sp.dma_start(wk_s[:, :, :], Wk.rearrange("(c p) n -> p c n", p=P)).then_inc(mix_w_loaded, 16)
            sp.dma_start(wout_s[:, :, :], W_out.rearrange("(c p) n -> p c n", p=P)).then_inc(mix_w_loaded, 16)
            def everywhere(v):
                return v.unsqueeze(0).to_broadcast([P, v.shape[0]])

            sp.dma_start(bias_mix[:, 2, :], everywhere(bq)).then_inc(small_loaded, 16)
            sp.dma_start(bias_mix[:, 3, :], everywhere(bk)).then_inc(small_loaded, 16)
            sp.dma_start(out_w_s[:, :], everywhere(out_w)).then_inc(small_loaded, 16)
            sp.dma_start(out_b_s[:, :], everywhere(out_b)).then_inc(small_loaded, 16)
            sp.dma_start(head_scale[:, :], everywhere(log_scale)).then_inc(small_loaded, 16)
            for r in range(MR):
                sp.dma_start(smear_s[r * MD:(r + 1) * MD, :],
                             smear.rearrange("(g r) -> r g", r=MR)[r:r + 1, :].to_broadcast([MD, MG]),
                             allow_slow_non_contiguous=True).then_inc(small_loaded, 16)
            for l in range(LAYERS):
                for n, v in enumerate((q_scale[l], k_scale[l])):
                    sp.dma_start(rot_scale[l][:, n, :, :].rearrange("p a f -> p (a f)"),
                                 everywhere(v)).then_inc(small_loaded, 16)
            for l in range(LAYERS):
                wl = layer_w_loaded[l]
                sp.dma_start(wqkv_s[l][:, :, :], wqkv[l].rearrange("(c p) n -> p c n", p=P)).then_inc(wl, 16)
                sp.dma_start(wo_s[l][:, :, :], wo[l].rearrange("(c p) n -> p c n", p=P)).then_inc(wl, 16)
                w1_v = w1[l].rearrange("(c p) (a n) -> p c a n", p=P, a=2)
                w1_t = w1_s[l][:, :, :].rearrange("p c (a n) -> p c a n", a=2)
                for a in range(2):
                    sp.dma_start(w1_t[:, :, a, 0:HID], w1_v[:, :, a, :]).then_inc(wl, 16)
                sp.dma_start(w2_s[l][:, 0:HC - 1, :],
                             w2[l][0:(HC - 1) * P, :].rearrange("(m p) n -> p m n", p=P)).then_inc(wl, 16)
                sp.dma_start(w2_s[l][0:TAIL, HC - 1, :], w2[l][(HC - 1) * P:HID, :]).then_inc(wl, 16)
                sp.dma_start(b2_s[l][:, :], everywhere(b2[l])).then_inc(wl, 16)

            def body(i):
                mix, proj, att_u, mlp_u = streams(i)
                if i.low + 1 < NW:
                    n = i.back(-1)
                    rows = row(n)
                    if n.back(2).exists():
                        sp.wait_ge(norm_dve.sem, norm_dve.at("xn", n.back(2)))
                    sp.dma_start(x_s[:, n.parity, :], x_f[rows, :]).then_inc(x_loaded[n.parity], 16)
                elif i.low + 1 < UNITS and i.low + 1 >= NW:
                    n = i.back(-1)
                    rows = row(window(n))
                    sp.wait_ge(x2_stored, 16 * (window(n).number() + 1))
                    if n.low >= NW + 2:
                        sp.wait_ge(proj_pe.sem, proj_pe.at("xt", n.back(2)))
                    else:
                        sp.wait_ge(norm_dve.sem, norm_dve.at("xn", n.back(2)))
                    sp.dma_start(x_s[:, n.parity, :], x2_d[rows, :]).then_inc(x_loaded[n.parity], 16)
                if i.low + 1 < UNITS:
                    n = i.back(-1)
                    rows = row(window(n))
                    if n.back(2).exists():
                        sp.wait_ge(proj_pool.sem, proj_pool.at("table", n.back(2)))
                    sp.dma_start(rot_s[:, n.parity, :, :].rearrange("p a f -> p (a f)"), rot_d[rows, :])\
                      .then_inc(rot_loaded[n.parity], 16)
                if proj is not None and layer(proj) == 1:
                    rows = row(window(proj))
                    sp.wait_ge(att_dve.sem, att_dve.at("x1", proj.back(2)))
                    sp.dma_start(x_res[:, proj.parity, :], x2_d[rows, :]).then_inc(res_loaded[proj.parity], 16)
                if mlp_u is not None and layer(mlp_u) == 1:
                    w = window(mlp_u)
                    rows = row(w)
                    if w.low == 0:
                        sp.wait_ge(s_stored, 16 * NW)
                    if w.back(1).exists():
                        sp.wait_ge(fin_dve.sem, fin_dve.at("out", w.back(1)))
                    sp.dma_start(s_in[:, :], s_d[rows, :]).then_inc(s_loaded, 16)
                    sp.dma_start(x_in[:, :], x_f[rows, :]).then_inc(xin_loaded, 16)
                if mlp_u is not None and layer(mlp_u) == 0:
                    rows = row(mlp_u)
                    sp.wait_ge(mlp_dve.sem, mlp_dve.at("x2", mlp_u))
                    sp.dma_start(x2_d[rows, :], x2[:, :]).then_inc(x2_stored, 16)
                if mix is not None:
                    rows = row(mix)
                    sp.wait_ge(mix_pool.sem, mix_pool.at("s", mix))
                    sp.dma_start(s_d[rows, :], s_out[:, :]).then_inc(s_stored, 16)
                if mlp_u is not None and layer(mlp_u) == 1:
                    w = window(mlp_u)
                    rows = row(w)
                    sp.wait_ge(fin_dve.sem, fin_dve.at("out", w))
                    sp.dma_start(out_f[rows, :], y_out[:, :]).then_inc(out_stored, 16)

            iterations(sp, body)
            sp.wait_ge(out_stored, 16 * NW)
            sp.wait_ge(s_stored, 16 * NW)
            sp.wait_ge(x2_stored, 16 * NW)

        @block.gpsimd
        def _(pool):
            pool.memset(rows_in, 0.0).then_inc(pads_zeroed, 1)
            for l in range(LAYERS):
                w1_t = w1_s[l][:, :, :].rearrange("p c (a n) -> p c a n", a=2)
                pool.memset(w1_t[:, :, :, HID:HIDP], 0.0).then_inc(pads_zeroed, 1)
                pool.memset(w2_s[l][:, HC - 1, :], 0.0).then_inc(pads_zeroed, 1)
            pool.memset(half_neg[:, :], -0.5).then_inc(setup_pool, 1)
            pool.memset(zero_col[:, :], 0.0).then_inc(setup_pool, 1)
            pool.memset(state[:, :, :], 0.0).then_inc(setup_pool, 1)
            pool.memset(v_mix[:, :, MD:MV], 1.0).then_inc(setup_pool, 1)
            pool.memset(kT[:, :, :, :], 0.0).then_inc(setup_pool, 1)
            pool.memset(v_loc[:, :, :], 0.0).then_inc(setup_pool, 1)
            pool.wait_ge(setup_pool, POOL_SETUP)

            def root(out, in_, w):
                return pool.tensor_tensor(out, in_, half_neg[:, 0:w], ALU.pow)

            def body(i):
                mix, proj, att_u, mlp_u = streams(i)
                if i.low == 0:
                    norm1(i)
                    norm2(i)
                if mlp_u is not None:
                    pool.wait_ge(mlp_dve.sem, mlp_dve.at("var", mlp_u))
                    root(small_h[:, 1:2], small_h[:, 0:1], 1).then_inc(mlp_pool.done("rstd"), 1)
                if proj is not None:
                    u, p = proj, proj.parity
                    if u.back(1).exists():
                        pool.wait_ge(proj_dve.sem, proj_dve.at("cos", u.back(1)))
                        pool.wait_ge(proj_pool.sem, proj_pool.at("inv", u.back(1)))
                    else:
                        pool.wait_ge(setup_dve.sem, setup_dve.at("half", ONCE))
                    pool.wait_ge(rot_loaded[p], 16 * (u.turn() + 1))
                    pool.tensor_tensor(rot_t[:, :, :, :],
                                       rot_s[:, p, :, :].unsqueeze(2).to_broadcast([P, 4, 2, HD // 2]),
                                       rot_scale[layer(u)][:, :, :, :], ALU.mult).then_inc(proj_pool.done("table"), 1)
                if proj is not None:
                    u = proj
                    pool.wait_ge(proj_act.sem, proj_act.at("k", u))
                    pool.wait_ge(proj_pool.sem, proj_pool.at("table", u))
                    r5 = raw[:, :].rearrange("p (a h s f) -> p a h s f", a=2, h=H, s=2)
                    o5 = rot_other[:, :].rearrange("p (a h s f) -> p a h s f", a=2, h=H, s=2)
                    for a in range(2):
                        for s in range(2):
                            ins = pool.tensor_tensor(o5[:, a, :, s, :], r5[:, a, :, 1 - s, :],
                                                     rot_t[:, 2 + a, s, :].unsqueeze(1).to_broadcast([P, H, HD // 2]),
                                                     ALU.mult)
                    ins.then_inc(proj_pool.done("other"), 1)
                if mix is not None:
                    n = mix
                    pool.wait_ge(mix_dve.sem, mix_dve.at("max", n))
                    qk_h = qk.rearrange("p (h d) -> p h d", d=MD)
                    pool.tensor_tensor(qk_h, qk_h, qk_max[:, :].unsqueeze(2).to_broadcast([P, 2 * MH, MD]),
                                       ALU.subtract).then_inc(mix_pool.done("sub"), 1)
                if proj is not None:
                    u, p = proj, proj.parity
                    pool.wait_ge(proj_dve.sem, proj_dve.at("clip", u))
                    root(inv_norm[:, p, :], sq_clip[:, :], 2 * H).then_inc(proj_pool.done("inv"), 1)
                if mix is not None:
                    n = mix
                    pool.wait_ge(mix_dve.sem, mix_dve.at("kinv", n))
                    k_h = qk[:, ME:2 * ME].rearrange("p (h d) -> p h d", d=MD)
                    pool.tensor_tensor(k_h, k_h, k_norm[:, :].unsqueeze(2).to_broadcast([P, MH, MD]),
                                       ALU.mult).then_inc(mix_pool.done("kn"), 1)
                    pool.wait_ge(mix_act.sem, mix_act.at("qt", n))
                    pool.tensor_tensor(qT_dec[:, :, :], qT_mix[:, 0:MG // 2, :], query_decay,
                                       ALU.mult).then_inc(mix_pool.done("qdec"), 1)
                    pool.wait_ge(mix_act.sem, mix_act.at("kt", n))
                    pool.tensor_tensor(kT_mix[:, :, :], kT_raw[:, :, 1:P + 1],
                                       keep_s[:, :].unsqueeze(2).to_broadcast([P, MG, P]),
                                       ALU.mult).then_inc(mix_pool.done("kkeep"), 1)
                if i.low + 1 < NW:
                    norm1(i.back(-1))
                if mix is not None:
                    pool.wait_ge(mix_pe.sem, mix_pe.at("o1", mix))
                    pool.tensor_tensor(state[:, :, :], state[:, :, :],
                                       whole_decay.unsqueeze(2).to_broadcast([P, MG, MR * MV]),
                                       ALU.mult).then_inc(mix_pool.done("sdec"), 1)
                if i.low + 1 < NW:
                    norm2(i.back(-1))
                if att_u is not None:
                    pool.wait_ge(att_dve.sem, att_dve.at("x1", att_u))
                    pool.tensor_tensor(x1b[:, att_u.parity, :], x1[:, att_u.parity, :], b2_s[layer(att_u)][:, :],
                                       ALU.add).then_inc(att_pool.done("x1b"), 1)
                if mix is not None:
                    n = mix
                    pool.wait_ge(mix_dve.sem, mix_dve.at("yvar", n))
                    root(small_y[:, 1:2], small_y[:, 0:1], 1).then_inc(mix_pool.done("yrstd"), 1)
                    pool.wait_ge(mix_dve.sem, mix_dve.at("yn", n))
                    pool.tensor_tensor(y_n[:, :], y_n[:, :], out_w_s[:, :], ALU.mult)\
                        .then_inc(mix_pool.done("yw"), 1)
                    if n.back(1).exists():
                        pool.wait_ge(s_stored, 16 * n.number())
                    pool.wait_ge(mix_pool.sem, mix_pool.at("yw", n))
                    pool.tensor_tensor(s_out[:, :], y_n[:, :], out_b_s[:, :], ALU.add)\
                        .then_inc(mix_pool.done("s"), 1)

            def norm1(n):
                pool.wait_ge(norm_dve.sem, norm_dve.at("var", n))
                root(small_x[:, 1:2], small_x[:, 0:1], 1).then_inc(norm_pool.done("rstd"), 1)

            def norm2(n):
                pool.wait_ge(norm_dve.sem, norm_dve.at("var2", n))
                root(small_x[:, 3:4], small_x[:, 2:3], 1).then_inc(norm_pool.done("rstd2"), 1)

            iterations(pool, body)

        @block.scalar
        def _(act):
            def copy(out, in_):
                return act.activation(out, in_, ACT.Copy)

            act.wait_ge(small_loaded, 16 * SMALL_DMAS)
            act.activation(head_scale[:, :], head_scale[:, :], ACT.Exp).then_inc(setup_act.done("scale"), 1)
            act.activation(smear_s[:, :], smear_s[:, :], ACT.Exp, scale=-1.0).then_inc(setup_act.done("smear"), 1)
            act.wait_ge(setup_pool, POOL_SETUP)

            def exps(step, a):
                s = list(STEP_HEADS).index(step)
                act.wait_ge(att_dve.sem, att_dve.at("m" + step, a))
                for j, h in enumerate(STEP_HEADS[step]):
                    c = 2 * s + j
                    ins = act.activation(prob[:, h, :], prob[:, h, :], ACT.Exp, bias=neg_max[:, c:c + 1],
                                         scale=QK_SCALE, accum_out=row_sum[:, c:c + 1])
                ins.then_inc(att_act.done("e" + step), 1)

            def turned(step, half, a, b):
                act.wait_ge(att_pe.sem, att_pe.at("t" + step, a))
                copy(pT[:, half, :, :], b[:, :].rearrange("p (b i) -> p b i", b=4))\
                    .then_inc(att_act.done("t" + step), 1)

            def body(i):
                mix, proj, a, m = streams(i)
                if proj is not None:
                    act.wait_ge(proj_pe.sem, proj_pe.at("xt", proj))
                    if window(proj).low > 0:
                        copy(xT[:, 1, 0:1], xT[:, 1, P:P + 1]).then_inc(proj_act.done("halo"), 1)
                    else:
                        copy(xT[:, 1, 0:1], zero_col[:, :]).then_inc(proj_act.done("halo"), 1)
                    act.wait_ge(proj_act.sem, proj_act.at("halo", proj))
                    copy(xT[:, :, 1:P + 1], proj_bank[:, 0:D].rearrange("p (c t) -> p c t", c=DC))\
                        .then_inc(proj_act.done("xt"), 1)
                if mix is not None:
                    act.wait_ge(mix_pe.sem, mix_pe.at("xt", mix))
                    copy(xhT[:, :, :], mix_bank[0][:, 0:D].rearrange("p (c t) -> p c t", c=DC))\
                        .then_inc(mix_act.done("xt"), 1)
                if a is not None:
                    exps("a0", a)
                if proj is not None:
                    act.wait_ge(proj_pe.sem, proj_pe.at("q", proj))
                    copy(raw[:, 0:E], proj_bank[:, :]).then_inc(proj_act.done("q"), 1)
                if a is not None:
                    exps("a1", a)
                    exps("b0", a)
                if mix is not None:
                    act.wait_ge(mix_dve.sem, mix_dve.at("p", mix))
                    act.activation(p_tanh, p_lin, ACT.Tanh, scale=0.5).then_inc(mix_act.done("tanh"), 1)
                if proj is not None:
                    act.wait_ge(proj_pe.sem, proj_pe.at("k", proj))
                    copy(raw[:, E:2 * E], proj_bank[:, :]).then_inc(proj_act.done("k"), 1)
                    act.wait_ge(proj_act.sem, proj_act.at("k", proj))
                    act.activation(rot[:, :], raw[:, :], ACT.Square).then_inc(proj_act.done("square"), 1)
                if m is not None:
                    act.wait_ge(mlp_pe.sem, mlp_pe.at("ht", m))
                    copy(hT_n[:, :, :], mlp_bank[1][:, 0:D].rearrange("p (c t) -> p c t", c=DC))\
                        .then_inc(mlp_act.done("ht"), 1)
                if a is not None:
                    for k in range(2):
                        turned(f"a{k}", k, a, att_bank[k])
                    exps("b1", a)
                if mix is not None:
                    act.wait_ge(mix_pool.sem, mix_pool.at("sub", mix))
                    act.activation(qk, qk, ACT.Exp).then_inc(mix_act.done("exp"), 1)
                if m is not None:
                    bias = b1_s[layer(m)]
                    act.wait_ge(mlp_pe.sem, mlp_pe.at("g0", m))
                    for j in range(4):
                        ins = act.activation(gel[:, j, :], mlp_bank[0][:, j * P:(j + 1) * P], ACT.Gelu,
                                             bias=bias[:, HC + j:HC + j + 1])
                    ins.then_inc(mlp_act.done("g0"), 1)
                if a is not None:
                    act.wait_ge(att_pe.sem, att_pe.at("pva", a))
                    copy(oT[:, 0:2, :], att_bank[0][:, 0:2 * P].rearrange("p (b i) -> p b i", b=2))\
                        .then_inc(att_act.done("pva"), 1)
                if mix is not None:
                    act.wait_ge(mix_pe.sem, mix_pe.at("qt", mix))
                    copy(qT_mix[:, :, :], mix_bank[1][:, :].rearrange("p (g i) -> p g i", g=MG))\
                        .then_inc(mix_act.done("qt"), 1)
                if a is not None:
                    turned("b0", 0, a, att_bank[1])
                if m is not None:
                    bias = b1_s[layer(m)]
                    act.wait_ge(mlp_pe.sem, mlp_pe.at("ga", m))
                    for j in range(4, HC):
                        ins = act.activation(gel[:, j, :], mlp_bank[0][:, (j - 4) * P:(j - 3) * P], ACT.Gelu,
                                             bias=bias[:, HC + j:HC + j + 1])
                    ins.then_inc(mlp_act.done("ga"), 1)
                if mix is not None:
                    act.wait_ge(mix_pe.sem, mix_pe.at("kt", mix))
                    if mix.low > 0:
                        copy(kT_raw[:, :, 0:1], kT_raw[:, :, P:P + 1]).then_inc(mix_act.done("halo"), 1)
                    else:
                        copy(kT_raw[:, :, 0:1], zero_col[:, :].unsqueeze(1).to_broadcast([P, MG, 1]))\
                            .then_inc(mix_act.done("halo"), 1)
                    act.wait_ge(mix_act.sem, mix_act.at("halo", mix))
                    copy(kT_raw[:, :, 1:P + 1], mix_bank[0][:, :].rearrange("p (g i) -> p g i", g=MG))\
                        .then_inc(mix_act.done("kt"), 1)
                if a is not None:
                    turned("b1", 1, a, att_bank[2])
                if proj is not None:
                    act.wait_ge(proj_pe.sem, proj_pe.at("qt", proj))
                    copy(qT[:, proj.parity, :, :], proj_bank[:, :].rearrange("p (g i) -> p g i", g=HP))\
                        .then_inc(proj_act.done("qt"), 1)
                if a is not None:
                    act.wait_ge(att_pe.sem, att_pe.at("pvb", a))
                    copy(oT[:, 2:4, :], att_bank[0][:, 0:2 * P].rearrange("p (b i) -> p b i", b=2))\
                        .then_inc(att_act.done("pvb"), 1)
                if proj is not None:
                    act.wait_ge(proj_pe.sem, proj_pe.at("kt", proj))
                    if proj.low == NW:
                        copy(kT[:, :, 1 - proj.parity, :], zero_col[:, :].unsqueeze(1).to_broadcast([P, HP, P]))
                    copy(kT[:, :, proj.parity, :], proj_bank[:, :].rearrange("p (g i) -> p g i", g=HP))\
                        .then_inc(proj_act.done("kt"), 1)
                    act.wait_ge(proj_pe.sem, proj_pe.at("v", proj))
                    copy(v_loc[:, proj.parity, :], proj_bank[:, :]).then_inc(proj_act.done("v"), 1)
                if mix is not None:
                    act.wait_ge(mix_pe.sem, mix_pe.at("gt", mix))
                    copy(goT, mix_bank[0][:, :].rearrange("p (g i) -> p g i", g=MG))\
                        .then_inc(mix_act.done("gt"), 1)
                if m is not None and layer(m) == 1:
                    act.wait_ge(mlp_dve.sem, mlp_dve.at("x2", m))
                    act.activation(y_tanh, x2[:, :], ACT.Tanh, scale=0.5).then_inc(fin_act.done("tanh"), 1)

            iterations(act, body)

        @block.vector
        def _(dve):
            spread = rot_other[:, 0:3 * DC * P].rearrange("p (n c t) -> p n c t", n=3, c=DC)

            dve.wait_ge(setup_pe.sem, setup_pe.at("cols", ONCE))
            dve.tensor_copy(cols[:, :], bank[4][:, 0:ROWS]).then_inc(setup_dve.done("cols"), 1)
            dve.wait_ge(setup_dve.sem, setup_dve.at("cols", ONCE))
            for n in range(3):
                ins = dve.tensor_copy(spread[:, n, :, :],
                                      norm_cols(2 * n + 1).unsqueeze(2).to_broadcast([P, DC, P]))
            ins.then_inc(setup_dve.done("spread"), 1)

            def pace():
                dve.memset(paced[:, :], 0.0)

            def norm1(n):
                p = n.parity
                dve.wait_ge(x_loaded[p], 16 * (n.turn() + 1))
                dve.bn_stats(stats_x[:, :], x_s[:, p, :]).then_inc(norm_dve.done("stat"), 1)
                dve.wait_ge(norm_dve.sem, norm_dve.at("stat", n))
                pace()
                dve.bn_aggr(mv_x[:, :], stats_x[:, :]).then_inc(norm_dve.done("aggr"), 1)
                dve.wait_ge(norm_dve.sem, norm_dve.at("aggr", n))
                dve.tensor_scalar(small_x[:, 0:1], mv_x[:, 1:2], EPS, None, ALU.add)\
                   .then_inc(norm_dve.done("var"), 1)

            def norm2(n):
                p = n.parity
                dve.wait_ge(norm_pool.sem, norm_pool.at("rstd", n))
                if n.back(2).exists():
                    dve.wait_ge(att_dve.sem, att_dve.at("x1", n.back(2)))
                dve.tensor_scalar(xn[:, p, :], x_s[:, p, :], mv_x[:, 0:1], small_x[:, 1:2],
                                  ALU.subtract, ALU.mult).then_inc(norm_dve.done("xn"), 1)
                dve.tensor_scalar(small_x[:, 2:3], mv_x[:, 1:2], small_x[:, 1:2], small_x[:, 1:2],
                                  ALU.mult, ALU.mult).then_inc(norm_dve.done("sq"), 1)
                dve.wait_ge(norm_dve.sem, norm_dve.at("sq", n))
                dve.tensor_scalar(small_x[:, 2:3], small_x[:, 2:3], EPS, None, ALU.add)\
                   .then_inc(norm_dve.done("var2"), 1)

            def norm3(n):
                p = n.parity
                dve.wait_ge(norm_pool.sem, norm_pool.at("rstd2", n))
                if n.back(1).exists():
                    dve.wait_ge(mix_pe.sem, mix_pe.at("xt", n.back(1)))
                dve.tensor_scalar(xh[:, :], xn[:, p, :], small_x[:, 3:4], None, ALU.mult)\
                   .then_inc(norm_dve.done("xh"), 1)

            def scores(step, a, b):
                s = list(STEP_HEADS).index(step)
                mask = masks[:, 2 if window(a).low == 0 else a.parity, :]
                dve.wait_ge(att_pe.sem, att_pe.at("s" + step, a))
                pace()
                for j, h in enumerate(STEP_HEADS[step]):
                    c = 2 * s + j
                    ins = dve.tensor_tensor_reduce(prob[:, h, :], b[:, j * 2 * P:(j + 1) * 2 * P], mask,
                                                   inv_norm[:, a.parity, h:h + 1], -3e38, ALU.add, ALU.max,
                                                   row_max[:, c:c + 1])
                ins.then_inc(att_dve.done("s" + step), 1)
                dve.wait_ge(att_dve.sem, att_dve.at("s" + step, a))
                dve.tensor_scalar(neg_max[:, 2 * s:2 * s + 2], row_max[:, 2 * s:2 * s + 2], -QK_SCALE, None,
                                  ALU.mult).then_inc(att_dve.done("m" + step), 1)

            def weigh(step, a):
                s = list(STEP_HEADS).index(step)
                dve.wait_ge(att_act.sem, att_act.at("e" + step, a))
                dve.reciprocal(row_inv[:, 2 * s:2 * s + 2], row_sum[:, 2 * s:2 * s + 2])\
                   .then_inc(att_dve.done("r" + step), 1)
                dve.wait_ge(att_dve.sem, att_dve.at("r" + step, a))
                for j, h in enumerate(STEP_HEADS[step]):
                    c = 2 * s + j
                    ins = dve.tensor_scalar(prob[:, h, :], prob[:, h, :], row_inv[:, c:c + 1], None, ALU.mult)
                ins.then_inc(att_dve.done("n" + step), 1)

            def heads(ap):
                return ap.rearrange("p (h d) -> p h d", d=MD)

            def mix_read(mix, g):
                b = mix_bank[g // 2][:, 0:2 * MR * MV].rearrange("p (h d) -> p h d", d=MV)
                k = str(g // 2)
                den, rec = o_den[:, g // 2, :], o_rec[:, g // 2, :]
                cols = slice(g * P, (g + 2) * P)
                dve.wait_ge(mix_pe.sem, mix_pe.at("o" + k, mix))
                dve.scalar_tensor_tensor(den, b[:, :, MD], 2.0, q_eps[:, g * MR:(g + 2) * MR],
                                         ALU.mult, ALU.add).then_inc(mix_dve.done("den" + k), 1)
                dve.wait_ge(mix_dve.sem, mix_dve.at("den" + k, mix))
                dve.reciprocal(rec, den).then_inc(mix_dve.done("rec" + k), 1)
                dve.wait_ge(mix_dve.sem, mix_dve.at("rec" + k, mix))
                dve.tensor_tensor(heads(go[:, cols]), b[:, :, 0:MD],
                                  rec.unsqueeze(2).to_broadcast([P, 2 * MR, MD]), ALU.mult)\
                   .then_inc(mix_dve.done("o" + k), 1)
                dve.wait_ge(mix_dve.sem, mix_dve.at("o" + k, mix))
                dve.tensor_tensor(go[:, cols], go[:, cols], gate[:, cols], ALU.mult)\
                   .then_inc(mix_dve.done("go" + k), 1)

            def state_add(mix, g):
                k = str(g // 2)
                b = mix_bank[g // 2][:, 0:2 * MR * MV].rearrange("p (g c) -> p g c", g=2)
                dve.wait_ge(mix_pe.sem, mix_pe.at("st" + k, mix))
                dve.wait_ge(mix_pool.sem, mix_pool.at("sdec", mix))
                for r in range(MR):
                    rows, cols = slice(r * MD, (r + 1) * MD), slice(r * MV, (r + 1) * MV)
                    ins = dve.tensor_tensor(state[rows, g:g + 2, cols], b[rows, :, cols],
                                            state[rows, g:g + 2, cols], ALU.add)
                ins.then_inc(mix_dve.done("st" + k), 1)

            def first_norm():
                norm1(Unit(0, 0, 0))
                norm2(Unit(0, 0, 0))
                norm3(Unit(0, 0, 0))

            first_norm()
            dve.wait_ge(setup_pe.sem, setup_pe.at("vp", ONCE))
            dve.tensor_copy(bias_mix[:, 0, :], bank[0][:, :])
            dve.tensor_copy(bias_mix[:, 1, :], bank[1][:, :])
            dve.wait_ge(setup_pe.sem, setup_pe.at("k", ONCE))
            dve.tensor_tensor(bias_mix[:, 2, :], bank[2][:, :], bias_mix[:, 2, :], ALU.add)
            dve.tensor_tensor(bias_mix[:, 3, :], bank[3][:, :], bias_mix[:, 3, :], ALU.add)\
               .then_inc(setup_dve.done("bias"), 1)
            for c in range(DC):
                dve.tensor_scalar(win_s[:, c, :], win_s[:, c, :], norm_cols(0)[:, c:c + 1], None, ALU.mult)
                dve.tensor_scalar(wq_s[:, c, :], wq_s[:, c, :], norm_cols(2)[:, c:c + 1], None, ALU.mult)
                ins = dve.tensor_scalar(wk_s[:, c, :], wk_s[:, c, :], norm_cols(4)[:, c:c + 1], None, ALU.mult)
            ins.then_inc(setup_dve.done("wscale"), 1)
            for l in range(LAYERS):
                ins = dve.tensor_scalar(rot_scale[l][:, 2:4, 0, :], rot_scale[l][:, 0:2, 1, :], -1.0, None, ALU.mult)
            ins.then_inc(setup_dve.done("rneg"), 1)
            for l in range(LAYERS):
                ins = dve.tensor_copy(rot_scale[l][:, 2:4, 1, :], rot_scale[l][:, 0:2, 0, :])
            ins.then_inc(setup_dve.done("rcopy"), 1)
            dve.wait_ge(setup_act.sem, setup_act.at("smear", ONCE))
            dve.tensor_scalar(smear_s[:, :], smear_s[:, :], 1.0, None, ALU.add).then_inc(setup_dve.done("smear1"), 1)
            dve.wait_ge(setup_dve.sem, setup_dve.at("smear1", ONCE))
            dve.reciprocal(smear_s[:, :], smear_s[:, :]).then_inc(setup_dve.done("smear2"), 1)
            dve.wait_ge(setup_dve.sem, setup_dve.at("smear2", ONCE))
            dve.tensor_scalar(keep_s[:, :], smear_s[:, :], -1.0, 1.0, ALU.mult, ALU.add)\
               .then_inc(setup_dve.done("keep"), 1)
            dve.tensor_scalar(head_eps[:, :], head_scale[:, :], 2 * EPS, None, ALU.mult)\
               .then_inc(setup_dve.done("eps"), 1)
            dve.tensor_scalar(out_w_s[:, :], out_w_s[:, :], 0.5, None, ALU.mult)
            dve.tensor_scalar(out_b_s[:, :], out_b_s[:, :], 0.5, None, ALU.mult)\
               .then_inc(setup_dve.done("half"), 1)
            dve.wait_ge(setup_dve.sem, setup_dve.at("half", ONCE))
            dve.wait_ge(table_loaded, 16)

            def fold(l):
                at = NORM_ROWS + l * 2 * HC
                dve.wait_ge(setup_pe.sem, setup_pe.at(f"b1_{l}", ONCE))
                dve.tensor_tensor(b1_s[l][:, :], proj_bank[:, 0:2 * HC], cols[:, at:at + 2 * HC], ALU.add)\
                   .then_inc(setup_dve.done(f"b1_{l}"), 1)
                for c in range(DC):
                    ins = dve.tensor_scalar(w1_s[l][:, c, :], w1_s[l][:, c, :],
                                            norm_cols(6 + 2 * l)[:, c:c + 1], None, ALU.mult)
                ins.then_inc(setup_dve.done(f"w1_{l}"), 1)

            def body(i):
                mix, u, a, m = streams(i)
                nxt = i.back(-1) if i.low + 1 < NW else None
                if i.low in (1, 3):
                    fold(i.low // 2)
                if a is not None:
                    scores("a0", a, att_bank[0])
                if m is not None:
                    dve.wait_ge(mlp_pe.sem, mlp_pe.at("sh", m))
                    dve.bn_stats(stats_h[:, 0:6], x1[:, m.parity, 0:P])
                    dve.bn_stats(stats_h[:, 6:12], mlp_bank[0][:, 0:P]).then_inc(mlp_dve.done("stat"), 1)
                    dve.wait_ge(mlp_dve.sem, mlp_dve.at("stat", m))
                    pace()
                    dve.bn_aggr(mv_h[:, :], stats_h[:, :]).then_inc(mlp_dve.done("aggr"), 1)
                    dve.wait_ge(mlp_dve.sem, mlp_dve.at("aggr", m))
                    dve.tensor_scalar(small_h[:, 0:1], mv_h[:, 1:2], EPS, None, ALU.add)\
                       .then_inc(mlp_dve.done("var"), 1)
                if a is not None:
                    scores("a1", a, att_bank[1])
                if m is not None:
                    dve.wait_ge(mlp_pool.sem, mlp_pool.at("rstd", m))
                    dve.tensor_scalar(h_n[:, 0:P], x1[:, m.parity, 0:P], mv_h[:, 0:1], small_h[:, 1:2],
                                      ALU.subtract, ALU.mult)
                    dve.tensor_scalar(h_n[:, P:D], mlp_bank[0][:, 0:P], mv_h[:, 0:1], small_h[:, 1:2],
                                      ALU.subtract, ALU.mult).then_inc(mlp_dve.done("hn"), 1)
                if a is not None:
                    scores("b0", a, att_bank[2])
                    weigh("a0", a)
                if mix is not None:
                    dve.wait_ge(mix_pe.sem, mix_pe.at("p", mix))
                    dve.tensor_tensor(p_lin, mix_bank[1][:, :], bias_mix[:, 1, :], ALU.add)\
                       .then_inc(mix_dve.done("p"), 1)
                if a is not None:
                    weigh("a1", a)
                if u is not None:
                    dve.wait_ge(proj_act.sem, proj_act.at("square", u))
                    dve.tensor_reduce(sq_sum[:, :], rot[:, :].rearrange("p (h d) -> p h d", d=HD), AX_X, ALU.add)\
                       .then_inc(proj_dve.done("sqsum"), 1)
                    dve.wait_ge(proj_dve.sem, proj_dve.at("sqsum", u))
                    dve.tensor_scalar(sq_clip[:, :], sq_sum[:, :], 1e-24, None, ALU.max)\
                       .then_inc(proj_dve.done("clip"), 1)
                if mix is not None:
                    dve.wait_ge(mix_pe.sem, mix_pe.at("q", mix))
                    dve.tensor_tensor(qk[:, 0:ME], mix_bank[0][:, :], bias_mix[:, 2, :], ALU.add)\
                       .then_inc(mix_dve.done("q"), 1)
                    dve.wait_ge(mix_act.sem, mix_act.at("tanh", mix))
                    dve.scalar_tensor_tensor(gate[:, :], p_tanh, 1.0, p_lin, ALU.add, ALU.mult)\
                       .then_inc(mix_dve.done("gate"), 1)
                if a is not None:
                    weigh("b0", a)
                if mix is not None:
                    dve.wait_ge(mix_pe.sem, mix_pe.at("k", mix))
                    dve.tensor_tensor(qk[:, ME:2 * ME], mix_bank[1][:, :], bias_mix[:, 3, :], ALU.add)\
                       .then_inc(mix_dve.done("k"), 1)
                    dve.wait_ge(mix_dve.sem, mix_dve.at("k", mix))
                    dve.tensor_reduce(qk_max[:, :], heads(qk), AX_X, ALU.max).then_inc(mix_dve.done("max"), 1)
                if a is not None:
                    scores("b1", a, att_bank[2])
                if u is not None:
                    four = lambda ap: ap.rearrange("p (a h d) -> p a h d", a=2, h=H)
                    dve.wait_ge(proj_pool.sem, proj_pool.at("table", u))
                    dve.tensor_tensor(four(rot[:, :]), four(raw[:, :]),
                                      rot_t[:, 0:2, :, :].rearrange("p a s f -> p a (s f)").unsqueeze(2)
                                      .to_broadcast([P, 2, H, HD]), ALU.mult).then_inc(proj_dve.done("cos"), 1)
                    dve.wait_ge(proj_pool.sem, proj_pool.at("other", u))
                    dve.wait_ge(proj_dve.sem, proj_dve.at("cos", u))
                    dve.tensor_tensor(rot[:, :], rot[:, :], rot_other[:, :], ALU.add)\
                       .then_inc(proj_dve.done("rot"), 1)
                if mix is not None:
                    dve.wait_ge(mix_pe.sem, mix_pe.at("v", mix))
                    dve.tensor_tensor(v_mix[:, :, 0:MD], heads(mix_bank[0][:, :]), heads(bias_mix[:, 0, :]),
                                      ALU.add).then_inc(mix_dve.done("v"), 1)
                    dve.wait_ge(mix_act.sem, mix_act.at("exp", mix))
                    dve.tensor_reduce(qk_sum[:, :], heads(qk), AX_X, ALU.add).then_inc(mix_dve.done("sum"), 1)
                    dve.wait_ge(mix_dve.sem, mix_dve.at("sum", mix))
                    dve.tensor_tensor(k_norm[:, :], qk_sum[:, MH:2 * MH], head_scale[:, :], ALU.mult)\
                       .then_inc(mix_dve.done("kscale"), 1)
                    dve.wait_ge(mix_dve.sem, mix_dve.at("kscale", mix))
                    dve.reciprocal(k_norm[:, :], k_norm[:, :]).then_inc(mix_dve.done("kinv"), 1)
                    dve.tensor_tensor(q_eps[:, :], qk_sum[:, 0:MH], head_eps[:, :], ALU.mult)\
                       .then_inc(mix_dve.done("qeps"), 1)
                if a is not None:
                    weigh("b1", a)
                if m is not None:
                    bias = b1_s[layer(m)]
                    dve.wait_ge(mlp_pe.sem, mlp_pe.at("a0", m))
                    dve.wait_ge(mlp_act.sem, mlp_act.at("g0", m))
                    for j in range(4):
                        ins = dve.scalar_tensor_tensor(hid[:, j, :], mlp_bank[1][:, j * P:(j + 1) * P],
                                                       bias[:, j:j + 1], gel[:, j, :], ALU.add, ALU.mult)
                    ins.then_inc(mlp_dve.done("a0"), 1)
                if u is not None:
                    k_h = rot[:, E:2 * E].rearrange("p (h d) -> p h d", d=HD)
                    dve.wait_ge(proj_pool.sem, proj_pool.at("inv", u))
                    dve.wait_ge(proj_dve.sem, proj_dve.at("rot", u))
                    dve.tensor_tensor(k_h, k_h, inv_norm[:, u.parity, H:2 * H].unsqueeze(2).to_broadcast([P, H, HD]),
                                      ALU.mult).then_inc(proj_dve.done("knorm"), 1)
                if m is not None:
                    bias = b1_s[layer(m)]
                    dve.wait_ge(mlp_act.sem, mlp_act.at("ga", m))
                    for j in range(4, HC):
                        ins = dve.scalar_tensor_tensor(hid[:, j, :], mlp_bank[0][:, (j - 2) * P:(j - 1) * P],
                                                       bias[:, j:j + 1], gel[:, j, :], ALU.add, ALU.mult)
                    ins.then_inc(mlp_dve.done("ga"), 1)
                if mix is not None:
                    dve.wait_ge(mix_act.sem, mix_act.at("kt", mix))
                    dve.tensor_tensor(kT_prev[:, :].rearrange("p (g i) -> p g i", g=MG), kT_raw[:, :, 0:P],
                                      smear_s[:, :].unsqueeze(2).to_broadcast([P, MG, P]), ALU.mult)\
                       .then_inc(mix_dve.done("kprev"), 1)
                    dve.wait_ge(mix_dve.sem, mix_dve.at("kprev", mix))
                    dve.wait_ge(mix_pool.sem, mix_pool.at("kkeep", mix))
                    kT_flat = kT_mix[:, :, :].rearrange("p g i -> p (g i)")
                    dve.tensor_tensor(kT_flat, kT_flat, kT_prev[:, :], ALU.add).then_inc(mix_dve.done("ksmear"), 1)
                    dve.wait_ge(mix_pe.sem, mix_pe.at("kb", mix))
                    dve.tensor_tensor(k_dec[:, :], mix_bank[1][:, :], key_decay, ALU.mult)\
                       .then_inc(mix_dve.done("kdec"), 1)
                    for r in range(MR):
                        b = mix_bank[r % 2][:, :].rearrange("p (g i) -> p g i", g=MG)
                        dve.wait_ge(mix_pe.sem, mix_pe.at(f"s{r}", mix))
                        dve.tensor_tensor(att[:, r, 0:MG // 2, :], b[:, 0:MG // 2, :], decay[:, r, :, :], ALU.mult)
                        dve.tensor_tensor(att[:, r, MG // 2:MG, :], b[:, MG // 2:MG, :],
                                          causal.unsqueeze(1).to_broadcast([P, MG // 2, P]), ALU.mult)\
                           .then_inc(mix_dve.done(f"s{r}"), 1)
                if mix is not None:
                    mix_read(mix, 0)
                    mix_read(mix, 2)
                if nxt is not None:
                    norm1(nxt)
                if a is not None:
                    dve.wait_ge(att_pe.sem, att_pe.at("wo", a))
                    if layer(a) == 0:
                        res = xn
                    else:
                        res = x_res
                        dve.wait_ge(res_loaded[a.parity], 16 * (window(a).turn() + 1))
                    dve.tensor_tensor(x1[:, a.parity, :], att_bank[1][:, 0:D], res[:, a.parity, :], ALU.add)\
                       .then_inc(att_dve.done("x1"), 1)
                if nxt is not None:
                    norm2(nxt)
                if mix is not None:
                    state_add(mix, 0)
                    state_add(mix, 2)
                if nxt is not None:
                    norm3(nxt)
                if m is not None:
                    dve.wait_ge(mlp_pe.sem, mlp_pe.at("w2", m))
                    dve.wait_ge(att_pool.sem, att_pool.at("x1b", m))
                    if layer(m) == 1:
                        dve.wait_ge(x2_stored, 16 * NW)
                    elif m.back(1).exists():
                        dve.wait_ge(x2_stored, 16 * m.number())
                    dve.tensor_tensor(x2[:, :], mlp_bank[1][:, 0:D], x1b[:, m.parity, :], ALU.add)\
                       .then_inc(mlp_dve.done("x2"), 1)
                if m is not None and layer(m) == 1:
                    w = window(m)
                    dve.wait_ge(fin_act.sem, fin_act.at("tanh", w))
                    if w.back(1).exists():
                        dve.wait_ge(out_stored, 16 * w.number())
                    dve.scalar_tensor_tensor(y_out[:, :], y_tanh, 1.0, x2[:, :], ALU.add, ALU.mult)\
                       .then_inc(fin_dve.done("u"), 1)
                    dve.wait_ge(s_loaded, 16 * (w.number() + 1))
                    dve.wait_ge(fin_dve.sem, fin_dve.at("u", w))
                    dve.tensor_tensor(y_out[:, :], y_out[:, :], s_in[:, :], ALU.mult)\
                       .then_inc(fin_dve.done("us"), 1)
                    dve.wait_ge(xin_loaded, 16 * (w.number() + 1))
                    dve.wait_ge(fin_dve.sem, fin_dve.at("us", w))
                    dve.tensor_tensor(y_out[:, :], y_out[:, :], x_in[:, :], ALU.add)\
                       .then_inc(fin_dve.done("out"), 1)
                if mix is not None:
                    b = mix_bank[1][:, 0:D]
                    dve.wait_ge(mix_pe.sem, mix_pe.at("wout", mix))
                    dve.bn_stats(stats_y[:, :], b).then_inc(mix_dve.done("ystat"), 1)
                    dve.wait_ge(mix_dve.sem, mix_dve.at("ystat", mix))
                    pace()
                    dve.bn_aggr(mv_y[:, :], stats_y[:, :]).then_inc(mix_dve.done("yaggr"), 1)
                    dve.wait_ge(mix_dve.sem, mix_dve.at("yaggr", mix))
                    dve.tensor_scalar(small_y[:, 0:1], mv_y[:, 1:2], EPS, None, ALU.add)\
                       .then_inc(mix_dve.done("yvar"), 1)
                    dve.wait_ge(mix_pool.sem, mix_pool.at("yrstd", mix))
                    dve.tensor_scalar(y_n[:, :], b, mv_y[:, 0:1], small_y[:, 1:2], ALU.subtract, ALU.mult)\
                       .then_inc(mix_dve.done("yn"), 1)

            iterations(dve, body)

        @block.tensor
        def _(pe):
            def mm(out, lhsT, rhs, first, last):
                return pe.matmul(out, lhsT, rhs, start=first, stop=last)

            def transposes(out, parts):
                for j, part in enumerate(parts):
                    ins = pe.transpose(out[:, j * P:(j + 1) * P], part, ident)
                return ins

            spread = rot_other[:, 0:3 * DC * P].rearrange("p (n c t) -> p n c t", n=3, c=DC)
            pe.wait_ge(small_loaded, 16 * SMALL_DMAS)
            pe.wait_ge(table_loaded, 16)
            pe.transpose(bank[4][:, 0:ROWS], rows_in, ident[0:ROWS, 0:ROWS]).then_inc(setup_pe.done("cols"), 1)
            pe.wait_ge(setup_dve.sem, setup_dve.at("spread", ONCE))
            pe.wait_ge(mix_w_loaded, 16 * MIX_W_DMAS)
            for t in range(2):
                for c in range(DC):
                    ins = mm(bank[t][:, :], spread[:, 0, c, :], win_s[:, c, t * ME:(t + 1) * ME], c == 0, c == DC - 1)
            ins.then_inc(setup_pe.done("vp"), 1)
            for n, (w, name) in enumerate(((wq_s, "q"), (wk_s, "k"))):
                for c in range(DC):
                    ins = mm(bank[2 + n][:, :], spread[:, 1 + n, c, :], w[:, c, :], c == 0, c == DC - 1)
                ins.then_inc(setup_pe.done(name), 1)
            pe.wait_ge(setup_dve.sem, setup_dve.at("half", ONCE))
            pe.wait_ge(setup_pool, POOL_SETUP)

            def fold(l):
                pe.wait_ge(layer_w_loaded[l], 16 * LAYER_W_DMAS)
                pe.wait_ge(proj_act.sem, proj_act.at("v", Unit(0, 2 * l, 2 * l)))
                for j in range(2 * HC):
                    for c in range(DC):
                        ins = mm(proj_bank[:, j:j + 1], w1_s[l][:, c, j * P:(j + 1) * P],
                                 norm_cols(7 + 2 * l)[:, c:c + 1], c == 0, c == DC - 1)
                ins.then_inc(setup_pe.done(f"b1_{l}"), 1)
                pe.wait_ge(setup_dve.sem, setup_dve.at(f"w1_{l}", ONCE))

            def att_scores(step, a, b):
                for j, h in enumerate(STEP_HEADS[step]):
                    rows = slice(HD * (h % 2), HD * (h % 2) + HD)
                    ins = mm(b[:, j * 2 * P:(j + 1) * 2 * P], qT[rows, a.parity, h // 2, :],
                             kT[rows, h // 2, :, :].rearrange("p s j -> p (s j)"), True, True)
                ins.then_inc(att_pe.done("s" + step), 1)

            def att_turn(step, a, b):
                pe.wait_ge(att_dve.sem, att_dve.at("n" + step, a))
                parts = [prob[:, h, s * P:(s + 1) * P] for h in STEP_HEADS[step] for s in range(2)]
                transposes(b, parts).then_inc(att_pe.done("t" + step), 1)

            def att_values(half, a, b):
                for s in range(2):
                    for j, h in enumerate(STEP_HEADS[f"{half}{s}"]):
                        out = b[HD * (h % 2):HD * (h % 2) + HD, j * P:(j + 1) * P]
                        for slot in range(2):
                            ins = mm(out, v_loc[:, slot, h * HD:(h + 1) * HD], pT[:, s, 2 * j + slot, :],
                                     slot == 0, slot == 1)
                ins.then_inc(att_pe.done("pv" + half), 1)

            def mix_linear(mix, step, b, w, col):
                for c in range(DC):
                    ins = mm(b[:, :], xhT[:, c, :], w[:, c, col:col + ME], c == 0, c == DC - 1)
                ins.then_inc(mix_pe.done(step), 1)

            def proj_linear(u, step, col):
                w = wqkv_s[layer(u)]
                for c in range(DC):
                    ins = mm(proj_bank[:, :], xT[:, c, 1 - c:1 - c + P], w[:, c, col:col + E], c == 0, c == DC - 1)
                ins.then_inc(proj_pe.done(step), 1)

            def hidden(m, b, at, first, count):
                w = w1_s[layer(m)]
                for j in range(count):
                    for c in range(DC):
                        ins = mm(b[:, (at + j) * P:(at + j + 1) * P], w[:, c, (first + j) * P:(first + j + 1) * P],
                                 hT_n[:, c, :], c == 0, c == DC - 1)
                return ins

            def body(i):
                mix, u, a, m = streams(i)
                if i.low in (1, 3):
                    fold(i.low // 2)
                if u is not None:
                    if layer(u) == 0:
                        pe.wait_ge(norm_dve.sem, norm_dve.at("xn", u))
                        src = xn
                    else:
                        pe.wait_ge(x_loaded[u.parity], 16 * (u.turn() + 1))
                        src = x_s
                    if u.back(1).exists():
                        pe.wait_ge(proj_act.sem, proj_act.at("v", u.back(1)))
                    transposes(proj_bank, [src[:, u.parity, c * P:(c + 1) * P] for c in range(DC)])\
                        .then_inc(proj_pe.done("xt"), 1)
                if mix is not None:
                    pe.wait_ge(norm_dve.sem, norm_dve.at("xh", mix))
                    if mix.back(1).exists():
                        pe.wait_ge(mix_act.sem, mix_act.at("gt", mix.back(1)))
                    transposes(mix_bank[0], [xh[:, c * P:(c + 1) * P] for c in range(DC)])\
                        .then_inc(mix_pe.done("xt"), 1)
                if a is not None:
                    pe.wait_ge(proj_act.sem, proj_act.at("kt", a))
                    if a.back(1).exists():
                        pe.wait_ge(att_act.sem, att_act.at("pvb", a.back(1)))
                    att_scores("a0", a, att_bank[0])
                if m is not None:
                    pe.wait_ge(att_dve.sem, att_dve.at("x1", m))
                    if m.back(1).exists():
                        pe.wait_ge(mlp_dve.sem, mlp_dve.at("ga", m.back(1)))
                    start = window(m).low == 0
                    ins = mm(mlp_bank[0][:, 0:P], tab("shift"), x1[:, m.parity, P:D], True, start)
                    if not start:
                        ins = mm(mlp_bank[0][:, 0:P], tab("carry"), x1[:, 1 - m.parity, P:D], False, True)
                    ins.then_inc(mlp_pe.done("sh"), 1)
                if a is not None:
                    if a.back(1).exists():
                        pe.wait_ge(att_dve.sem, att_dve.at("x1", a.back(1)))
                    att_scores("a1", a, att_bank[1])
                if u is not None:
                    if u.low == 0:
                        pe.wait_ge(layer_w_loaded[0], 16 * LAYER_W_DMAS)
                    pe.wait_ge(proj_act.sem, proj_act.at("xt", u))
                    proj_linear(u, "q", 0)
                if a is not None:
                    if a.back(1).exists():
                        pe.wait_ge(att_act.sem, att_act.at("tb1", a.back(1)))
                    att_scores("b0", a, att_bank[2])
                if mix is not None:
                    pe.wait_ge(mix_act.sem, mix_act.at("xt", mix))
                    if mix.back(1).exists():
                        pe.wait_ge(mix_dve.sem, mix_dve.at("yn", mix.back(1)))
                    mix_linear(mix, "p", mix_bank[1], win_s, ME)
                if u is not None:
                    pe.wait_ge(proj_act.sem, proj_act.at("q", u))
                    proj_linear(u, "k", E)
                if mix is not None:
                    mix_linear(mix, "q", mix_bank[0], wq_s, 0)
                if m is not None:
                    pe.wait_ge(mlp_dve.sem, mlp_dve.at("hn", m))
                    if m.back(1).exists():
                        pe.wait_ge(mlp_dve.sem, mlp_dve.at("x2", m.back(1)))
                    transposes(mlp_bank[1], [h_n[:, c * P:(c + 1) * P] for c in range(DC)])\
                        .then_inc(mlp_pe.done("ht"), 1)
                if a is not None:
                    att_turn("a0", a, att_bank[0])
                if mix is not None:
                    pe.wait_ge(mix_dve.sem, mix_dve.at("p", mix))
                    mix_linear(mix, "k", mix_bank[1], wk_s, 0)
                if a is not None:
                    att_turn("a1", a, att_bank[1])
                    pe.wait_ge(att_dve.sem, att_dve.at("sb0", a))
                    att_scores("b1", a, att_bank[2])
                if m is not None:
                    pe.wait_ge(mlp_act.sem, mlp_act.at("ht", m))
                    hidden(m, mlp_bank[0], 0, HC, 4).then_inc(mlp_pe.done("g0"), 1)
                if mix is not None:
                    pe.wait_ge(mix_dve.sem, mix_dve.at("q", mix))
                    mix_linear(mix, "v", mix_bank[0], win_s, 0)
                if a is not None:
                    pe.wait_ge(att_act.sem, att_act.at("ta1", a))
                    pe.wait_ge(proj_act.sem, proj_act.at("v", a))
                    att_values("a", a, att_bank[0])
                if m is not None:
                    hidden(m, mlp_bank[1], 0, 0, 4).then_inc(mlp_pe.done("a0"), 1)
                if mix is not None:
                    pe.wait_ge(mix_act.sem, mix_act.at("exp", mix))
                    pe.wait_ge(mix_dve.sem, mix_dve.at("k", mix))
                    transposes(mix_bank[1], [qk[:, g * P:(g + 1) * P] for g in range(MG)])\
                        .then_inc(mix_pe.done("qt"), 1)
                if a is not None:
                    att_turn("b0", a, att_bank[1])
                if m is not None:
                    pe.wait_ge(mlp_act.sem, mlp_act.at("g0", m))
                    hidden(m, mlp_bank[0], 0, HC + 4, 2)
                    hidden(m, mlp_bank[0], 2, 4, 2).then_inc(mlp_pe.done("ga"), 1)
                if mix is not None:
                    pe.wait_ge(mix_pool.sem, mix_pool.at("kn", mix))
                    pe.wait_ge(mix_dve.sem, mix_dve.at("v", mix))
                    transposes(mix_bank[0], [qk[:, ME + g * P:ME + (g + 1) * P] for g in range(MG)])\
                        .then_inc(mix_pe.done("kt"), 1)
                if a is not None:
                    att_turn("b1", a, att_bank[2])
                if u is not None:
                    pe.wait_ge(proj_act.sem, proj_act.at("k", u))
                    pe.wait_ge(proj_dve.sem, proj_dve.at("rot", u))
                    transposes(proj_bank, [rot[:, g * P:(g + 1) * P] for g in range(HP)])\
                        .then_inc(proj_pe.done("qt"), 1)
                if a is not None:
                    pe.wait_ge(att_act.sem, att_act.at("tb1", a))
                    att_values("b", a, att_bank[0])
                if mix is not None:
                    pe.wait_ge(mix_dve.sem, mix_dve.at("ksmear", mix))
                    pe.wait_ge(mix_act.sem, mix_act.at("qt", mix))
                    transposes(mix_bank[1], [kT_mix[:, g, :] for g in range(MG)]).then_inc(mix_pe.done("kb"), 1)
                if u is not None:
                    pe.wait_ge(proj_act.sem, proj_act.at("qt", u))
                    pe.wait_ge(proj_dve.sem, proj_dve.at("knorm", u))
                    transposes(proj_bank, [rot[:, E + g * P:E + (g + 1) * P] for g in range(HP)])\
                        .then_inc(proj_pe.done("kt"), 1)
                if mix is not None:
                    free = {0: (mix_act, "kt"), 1: (mix_dve, "kdec"), 2: (mix_dve, "s0"), 3: (mix_dve, "s1")}
                    for r in range(MR):
                        steps, name = free[r]
                        pe.wait_ge(steps.sem, steps.at(name, mix))
                        rows = slice(r * MD, (r + 1) * MD)
                        for g in range(MG):
                            ins = mm(mix_bank[r % 2][:, g * P:(g + 1) * P], kT_mix[rows, g, :], qT_mix[rows, g, :],
                                     True, True)
                        ins.then_inc(mix_pe.done(f"s{r}"), 1)
                if u is not None:
                    pe.wait_ge(proj_act.sem, proj_act.at("kt", u))
                    proj_linear(u, "v", 2 * E)
                if mix is not None:
                    pe.wait_ge(mix_pool.sem, mix_pool.at("qdec", mix))
                    if mix.back(1).exists():
                        pe.wait_ge(mix_dve.sem, mix_dve.at("st1", mix.back(1)))
                    pe.wait_ge(mix_dve.sem, mix_dve.at("s3", mix))
                    for k in range(2):
                        for g in (2 * k, 2 * k + 1):
                            q_g = qT_dec[:, g, :] if g < MG // 2 else qT_mix[:, g, :]
                            at = (g % 2) * MR * MV
                            mm(mix_bank[k][:, at:at + MR * MV], q_g, state[:, g, :], True, False)
                            for r in range(MR):
                                ins = mm(mix_bank[k][:, at + r * MV:at + (r + 1) * MV], att[:, r, g, :],
                                         v_mix[:, g * MR + r, :], False, r == MR - 1)
                        ins.then_inc(mix_pe.done(f"o{k}"), 1)
                if a is not None:
                    pe.wait_ge(att_act.sem, att_act.at("pvb", a))
                    for g in range(HP):
                        ins = mm(att_bank[1][:, 0:D], oT[:, g, :], wo_s[layer(a)][:, g, :], g == 0, g == HP - 1)
                    ins.then_inc(att_pe.done("wo"), 1)
                if mix is not None:
                    for k in range(2):
                        pe.wait_ge(mix_dve.sem, mix_dve.at(f"o{k}", mix))
                        for g in (2 * k, 2 * k + 1):
                            at = (g % 2) * MR * MV
                            ins = mm(mix_bank[k][:, at:at + MR * MV], k_dec[:, g * P:(g + 1) * P],
                                     v_mix[:, g * MR:(g + 1) * MR, :].rearrange("p h d -> p (h d)"), True, True)
                        ins.then_inc(mix_pe.done(f"st{k}"), 1)
                if m is not None:
                    pe.wait_ge(mlp_dve.sem, mlp_dve.at("ga", m))
                    for j in range(HC - 2):
                        mm(mlp_bank[1][:, 0:D], hid[:, j, :], w2_s[layer(m)][:, j, :], j == 0, False)
                if mix is not None:
                    pe.wait_ge(mix_dve.sem, mix_dve.at("st0", mix))
                    pe.wait_ge(mix_dve.sem, mix_dve.at("go1", mix))
                    transposes(mix_bank[0], [go[:, g * P:(g + 1) * P] for g in range(MG)])\
                        .then_inc(mix_pe.done("gt"), 1)
                if m is not None:
                    for j in range(HC - 2, HC):
                        ins = mm(mlp_bank[1][:, 0:D], hid[:, j, :], w2_s[layer(m)][:, j, :], False, j == HC - 1)
                    ins.then_inc(mlp_pe.done("w2"), 1)
                if mix is not None:
                    pe.wait_ge(mix_act.sem, mix_act.at("gt", mix))
                    pe.wait_ge(mix_dve.sem, mix_dve.at("st1", mix))
                    for g in range(MG):
                        ins = mm(mix_bank[1][:, 0:D], goT[:, g, :], wout_s[:, g, :], g == 0, g == MG - 1)
                    ins.then_inc(mix_pe.done("wout"), 1)

            iterations(pe, body)


_INS = ["x", "in_ln_w", "in_ln_b", "q_ln_w", "q_ln_b", "k_ln_w", "k_ln_b", "out_ln_w", "out_ln_b",
        "W_in", "W_out", "Wq", "bq", "Wk", "bk", "smear_factor", "log_scale"]
_FFN = ["wqkv", "q_scale", "k_scale", "wo", "ln_g", "ln_b", "w1", "b1", "w2", "b2"]


def kernel(**inputs):
    import concourse.bacc as _bacc
    from concourse.bass_utils import run_bass_kernel_spmd as _run

    nc = _bacc.Bacc("TRN2", target_bir_lowering=False, num_devices=1)
    table, table_at, rotary = constants()
    arrays, args = {}, []
    named = [(f"L0_attn_{n}", None) for n in _INS] + [(f"L0_ffn_{n}", None) for n in _FFN]
    named += [("table", table), ("rotary", rotary)]
    for name, a in named:
        a = np.ascontiguousarray(inputs[name] if a is None else a)
        arrays[f"in_{name}"] = a
        args.append(nc.dram_tensor(f"in_{name}", a.shape, mybir.dt.from_np(a.dtype), kind="ExternalInput").ap())
    out = nc.dram_tensor("out_0", [1, TOKENS, D], F32, kind="ExternalOutput").ap()
    build(nc, *args, table_at, out)
    r = _run(nc, [arrays], core_ids=[0])
    return r.results[0]["out_0"]
```

```python
from contextlib import ExitStack

import numpy as np

import concourse.bass as bass
from concourse import mybir

F32 = mybir.dt.float32
F32R = mybir.dt.float32r
ALU = mybir.AluOpType
ACT = mybir.ActivationFunctionType
AX_X = mybir.AxisListType.X

P = 128
D = 256
DC = D // P
TOKENS = 4096
NW = TOKENS // P
LAYERS = 2
NORM_ROWS = 10 * DC
UNITS = LAYERS * NW
EPS = 1e-5
MH, MD = 16, 32
ME = MH * MD
MG = ME // P
MR = P // MD
MV = MD + 1
H, HD = 8, 64
E = H * HD
HP = H // 2
QK_SCALE = 8.0
HID = int(D * 4 * 2 / 3)
HC = -(-HID // P)
HIDP = HC * P
TAIL = HID - (HC - 1) * P

ROWS = NORM_ROWS + LAYERS * 2 * HC

MASKED = -1e30

STEP_HEADS = {"a0": (0, 2), "a1": (1, 3), "b0": (4, 6), "b1": (5, 7)}


def constants():
    f = np.float32
    slopes = (f(2.0) ** np.linspace(0.0, -8.0, MH // 2, dtype=f)).astype(f)
    slopes = np.concatenate([slopes, np.zeros(MH - MH // 2, f)])
    t = np.arange(P, dtype=f)
    j, i = t[:, None], t[None, :]
    causal = (i >= j).astype(f)
    decay = np.zeros((P, MR, MG // 2, P), f)
    for r in range(MR):
        for g in range(MG // 2):
            decay[:, r, g, :] = np.exp(-slopes[g * MR + r] * np.maximum(i - j, 0)) * causal
    query = np.zeros((P, MG // 2, P), f)
    whole = np.zeros((P, MG), f)
    for r in range(MR):
        for g in range(MG):
            if g < MG // 2:
                query[r * MD:(r + 1) * MD, g, :] = np.exp(-slopes[g * MR + r] * (t + 1))[None, :]
            whole[r * MD:(r + 1) * MD, g] = np.exp(-slopes[g * MR + r] * f(P))
    key = np.exp(-slopes[None, :] * (P - 1 - t[:, None])).astype(f)
    own = np.where(i <= j, f(0), f(MASKED)).astype(f)
    before = np.where(i >= j, f(0), f(MASKED)).astype(f)
    none = np.full((P, P), MASKED, f)
    masks = np.stack([own, before, own, none], 1)
    ones = np.zeros((P, 2 * P), f)
    ones[np.arange(P), np.arange(1, P + 1)] = 1
    parts = {
        "ones": ones, "causal": causal,
        "decay": decay.reshape(P, -1), "query": query.reshape(P, -1), "whole": whole,
        "key": key, "masks": masks.reshape(P, -1),
    }
    at, n = {}, 0
    for name, a in parts.items():
        at[name] = (n, n + a.shape[1])
        n += a.shape[1]
    table = np.ascontiguousarray(np.concatenate(list(parts.values()), 1).astype(f))
    half = np.arange(0, HD, 2, dtype=f)
    inv = (f(1.0) / f(10000.0) ** (half / f(HD))).astype(f)
    pos = np.arange(TOKENS, dtype=f)
    ang = (pos[:, None] * inv[None, :]).astype(f)
    base = ((half + f(0.4 * HD)) / f(1.4 * HD)).astype(f)
    power = ((pos - TOKENS // 2) / f(P // 2)).astype(f)
    scale = (base[None, :] ** power[:, None]).astype(f)
    cos, sin = np.cos(ang), np.sin(ang)
    rot = np.stack([cos * scale, cos / scale, sin * scale, sin / scale], 1).astype(f)
    return table, at, np.ascontiguousarray(rot.reshape(TOKENS, -1))


class Unit:

    def __init__(self, k, c, low):
        self.k, self.c, self.low = k, c, low
        self.parity = c % 2

    def number(self):
        return 2 * self.k + self.c

    def back(self, d):
        return Unit(self.k, self.c - d, self.low - d)

    def exists(self):
        return self.low >= 0

    def turn(self):
        return self.k + self.c // 2


class Steps:

    def __init__(self, sem, names):
        self.sem, self.names, self.next = sem, names.split(), 0

    def done(self, name):
        assert self.names[self.next] == name, (self.names[self.next], name)
        self.next = (self.next + 1) % len(self.names)
        return self.sem

    def at(self, name, unit):
        return len(self.names) * unit.number() + self.names.index(name) + 1


def build(nc, x_d, in_w, in_b, q_w, q_b, k_w, k_b, out_w, out_b, W_in, W_out, Wq, bq, Wk, bk,
          smear, log_scale, wqkv, q_scale, k_scale, wo, ln_g, ln_b, w1, b1, w2, b2,
          table_d, rot_d, table_at, out_d):
    TW = table_d.shape[1]
    x2_d = nc.dram_tensor("x2_between_layers", [TOKENS, D], F32, kind="Internal").ap()
    s_d = nc.dram_tensor("s_between_passes", [TOKENS, D], F32, kind="Internal").ap()
    x_f = x_d.rearrange("a t d -> (a t) d")
    out_f = out_d.rearrange("a t d -> (a t) d")

    with ExitStack() as ctx:
        def sb(name, shape):
            return ctx.enter_context(nc.sbuf_tensor(name, shape, F32))

        def sb_halves(name, shape):
            with nc.sbuf_tensor(name + "_in", shape, F32) as loaded:
                pass
            return sb(name, shape), loaded

        def sem(name):
            return ctx.enter_context(nc.semaphore(name))

        table = sb("table", [P, TW])

        def tab(name):
            a, b = table_at[name]
            return table[:, a:b]

        shift, ident, carry = (tab("ones")[:, o:o + P] for o in (0, 1, P))
        decay = tab("decay").rearrange("p (r g i) -> p r g i", r=MR, g=MG // 2)
        causal = tab("causal")
        query_decay = tab("query").rearrange("p (g i) -> p g i", g=MG // 2)
        whole_decay = tab("whole")
        key_decay = tab("key")
        masks = tab("masks")
        win_s, win_in = sb_halves("win_s", [P, 2, DC, 2 * ME])
        wq_s, wq_in = sb_halves("wq_s", [P, 2, DC, ME])
        wk_s, wk_in = sb_halves("wk_s", [P, 2, DC, ME])
        wout_s = sb("wout_s", [P, ME // P, D])
        wqkv_s, wqkv_in = sb_halves("wqkv_s", [P, 2, DC, 3 * E])
        wo_s = sb("wo_s", [P, E // P, D])
        w1_s = sb("w1_s", [P, DC, 2 * HIDP])
        w2_s = sb("w2_s", [P, HC, D])
        b1_s = [sb(f"b1_s{l}", [P, 2 * HC]) for l in range(LAYERS)]
        b2_s = sb("b2_s", [P, D])
        rot_scale = [sb(f"rot_scale{l}", [P, 4, 2, HD // 2]) for l in range(LAYERS)]
        bias_mix = sb("bias_mix", [P, 4, ME])
        out_w_s = sb("out_w_s", [P, D])
        out_b_s = sb("out_b_s", [P, D])
        cols = sb("cols", [P, ROWS])
        head_scale = sb("head_scale", [P, MH])
        head_eps = sb("head_eps", [P, MH])
        smear_s = sb("smear_s", [P, MG])
        keep_s = sb("keep_s", [P, MG])
        half_neg = sb("half_neg", [P, 16])
        zero_col = sb("zero_col", [P, 1])
        paced = sb("paced", [P, 1])

        x_s = sb("x_s", [P, 2, D])
        xn = sb("xn", [P, 2, D])
        xh = sb("xh", [P, D])
        xhT = sb("xhT", [P, 2, DC, P])
        stats_x = sb("stats_x", [P, 6])
        mv_x = sb("mv_x", [P, 2])
        small_x = sb("small_x", [P, 4])
        mix_work = sb("mix_work", [P, 4 * 4 * P])
        qk = mix_work[:, 0:2 * ME]
        p_lin = mix_work[:, 2 * ME:3 * ME]
        p_tanh = mix_work[:, 3 * ME:4 * ME]
        att = mix_work[:, :].rearrange("p (r g i) -> p r g i", r=MR, g=MG)
        gate = sb("gate", [P, ME])
        qk_max = sb("qk_max", [P, 2 * MH])
        qk_sum = sb("qk_sum", [P, 2 * MH])
        k_norm = sb("k_norm", [P, MH])
        q_eps = sb("q_eps", [P, MH])
        v_mix = sb("v_mix", [P, MH, MV])
        qT_mix = sb("qT_mix", [P, MG, P])
        qT_dec = sb("qT_dec", [P, MG // 2, P])
        kT_raw = sb("kT_raw", [P, MG, P + 1])
        kT_mix = sb("kT_mix", [P, MG, P])
        go = sb("go", [P, MG * P])
        k_dec = sb("k_dec", [P, ME])
        goT = k_dec[:, :].rearrange("p (g i) -> p g i", g=MG)
        state = sb("state", [P, MG, MR * MV])
        o_den = sb("o_den", [P, 2, 2 * MR])
        o_rec = sb("o_rec", [P, 2, 2 * MR])
        stats_y = sb("stats_y", [P, 6])
        mv_y = sb("mv_y", [P, 2])
        small_y = sb("small_y", [P, 2])
        y_n = sb("y_n", [P, D])
        s_out = sb("s_out", [P, D])

        rot_s = sb("rot_s", [P, 2, 4, HD // 2])
        rot_t = sb("rot_t", [P, 4, 2, HD // 2])
        xT = sb("xT", [P, 2, DC, P + 1])
        raw = sb("raw", [P, 2 * E])
        rot = sb("rot", [P, 2 * E])
        rot_other = sb("rot_other", [P, 2 * E])
        sq_sum = sb("sq_sum", [P, 2 * H])
        sq_clip = sb("sq_clip", [P, 2 * H])
        inv_norm = sb("inv_norm", [P, 2, 2 * H])
        v_loc = sb("v_loc", [P, 2, E])
        qT = sb("qT", [P, 2, HP, P])
        kT = sb("kT", [P, HP, 2, P])

        x_res = xn
        prob = sb("prob", [P, H, 2 * P])
        row_max = sb("row_max", [P, H])
        neg_max = sb("neg_max", [P, H])
        row_sum = sb("row_sum", [P, H])
        row_inv = sb("row_inv", [P, H])
        pT = sb("pT", [P, 2, 4, P])
        oT = sb("oT", [P, HP, P])
        x1 = sb("x1", [P, 2, D])
        x1b = sb("x1b", [P, 2, D])

        stats_h = sb("stats_h", [P, 12])
        mv_h = sb("mv_h", [P, 2])
        small_h = sb("small_h", [P, 2])
        h_n = sb("h_n", [P, D])
        rows_in = h_n[0:ROWS, 0:P]
        hT_n = sb("hT_n", [P, DC, P])
        gel = sb("gel", [P, HC, P])
        hid = sb("hid", [P, HC, P])
        x2 = sb("x2", [P, D])
        s_in = s_out
        x_in = y_n
        y_tanh = gel[:, 0:2, :].rearrange("p a b -> p (a b)")
        y_out = gate[:, 0:D]

        bank = [ctx.enter_context(nc.psum_tensor(f"bank{i}", [P, 512], F32)) for i in range(8)]
        mix_bank = bank[0:2]
        proj_bank = bank[2]
        att_bank = bank[3:6]
        mlp_bank = bank[6:8]

        mix_pe = Steps(sem("mix_pe"), "xt q k v p qt kt kb s0 s1 s2 s3 o0 o1 st0 st1 gt wout")
        mix_act = Steps(sem("mix_act"), "xt exp tanh halo kt qt gt")
        mix_dve = Steps(sem("mix_dve"), "xl q k max v p sum kscale kinv qeps ksmear kdec gate "
                        "s0 s1 s2 s3 den0 rec0 o0 go0 den1 rec1 o1 go1 st0 st1 "
                        "ystat yaggr yvar yn")
        mix_pool = Steps(sem("mix_pool"), "sub kn kkeep qdec sdec yrstd yw s")
        norm_dve = Steps(sem("norm_dve"), "stat aggr var xn sq var2 xh")
        norm_pool = Steps(sem("norm_pool"), "rstd rstd2")
        proj_pe = Steps(sem("proj_pe"), "xt q k v qt kt")
        proj_act = Steps(sem("proj_act"), "halo xt q k square v qt kt")
        proj_dve = Steps(sem("proj_dve"), "xl sqsum clip cos rot knorm")
        proj_pool = Steps(sem("proj_pool"), "table other inv")
        att_pe = Steps(sem("att_pe"), "sa0 sa1 sb0 sb1 ta0 ta1 pva tb0 tb1 pvb wo")
        att_act = Steps(sem("att_act"), "ea0 ea1 eb0 ta0 ta1 eb1 pva tb0 tb1 pvb")
        att_dve = Steps(sem("att_dve"), "sa0 ma0 sa1 ma1 sb0 mb0 ra0 na0 ra1 na1 rb0 nb0 sb1 mb1 "
                        "rb1 nb1 x1")
        att_pool = Steps(sem("att_pool"), "x1b")
        mlp_pe = Steps(sem("mlp_pe"), "sh ht g0 a0 ga w2")
        mlp_act = Steps(sem("mlp_act"), "ht g0 ga")
        mlp_dve = Steps(sem("mlp_dve"), "stat aggr var hn a0 ga x2")
        mlp_pool = Steps(sem("mlp_pool"), "rstd")
        fin_act = Steps(sem("fin_act"), "tanh")
        fin_dve = Steps(sem("fin_dve"), "u us out")
        x_loaded = [sem(f"x_loaded{i}") for i in range(2)]
        rot_loaded = [sem(f"rot_loaded{i}") for i in range(2)]
        res_loaded = [sem(f"res_loaded{i}") for i in range(2)]
        s_loaded = sem("s_loaded")
        xin_loaded = sem("xin_loaded")
        s_stored = sem("s_stored")
        x2_stored = sem("x2_stored")
        out_stored = sem("out_stored")
        table_loaded = sem("table_loaded")
        small_loaded = sem("small_loaded")
        mix_w_loaded = sem("mix_w_loaded")
        wqkv_loaded = sem("wqkv_loaded")
        w1_loaded = sem("w1_loaded")
        wo_loaded = sem("wo_loaded")
        w2_loaded = sem("w2_loaded")
        b2_loaded = sem("b2_loaded")
        pads_zeroed = sem("pads_zeroed")
        setup_pe = Steps(sem("setup_pe"), "cols vp q k b1_0 b1_1")
        setup_act = Steps(sem("setup_act"), "scale smear mix_h qkv_0 qkv_1")
        setup_dve = Steps(sem("setup_dve"), "cols spread bias rneg rcopy smear1 smear2 keep eps half mix_l "
                          "qkv_0 b1_0 w1_0 qkv_1 b1_1 w1_1")
        setup_pool = sem("setup_pool")

        SMALL_DMAS = 18 + 13
        MIX_W_DMAS = 4
        PADS = 3
        W1_DMAS = 2
        W2_DMAS = 2
        QKV_CUT = {0: 0, NW: 1}
        W1_FOLD = {1: 0, NW + 2: 1}
        POOL_SETUP = 6
        ONCE = Unit(0, 0, 0)

        block = ctx.enter_context(nc.Block())
        row = lambda u: bass.ds(u.number() * P, P)
        window = lambda u: u if u.low < NW else u.back(NW)
        layer = lambda u: 0 if u.low < NW else 1

        def halved(ap):
            return ap.bitcast(F32R)

        def iterations(eng, body):
            edge = 4
            for first, last in ((0, NW), (NW, UNITS)):
                for i in range(first, first + edge):
                    body(Unit(i // 2, i % 2, i))
                low = first + edge
                with eng.Fori(low // 2, last // 2 - 1) as k:
                    body(Unit(k, 0, low))
                    body(Unit(k, 1, low))
                for i in range(last - 2, last):
                    body(Unit(i // 2, i % 2, i))
            for i in range(UNITS, UNITS + 3):
                body(Unit(i // 2, i % 2, i))

        def norm_cols(n):
            return cols[:, n * DC:(n + 1) * DC]

        def streams(i):
            return (i if i.low < NW else None,
                    i if i.low < UNITS else None,
                    i.back(1) if 1 <= i.low < UNITS + 1 else None,
                    i.back(2) if 2 <= i.low < UNITS + 2 else None,
                    i.back(3) if i.low >= NW + 3 else None)

        @block.sync
        def _(sp):
            sp.dma_start(x_s[:, 0, :], x_f[0:P, :]).then_inc(x_loaded[0], 16)
            sp.dma_start(rot_s[:, 0, :, :].rearrange("p a f -> p (a f)"), rot_d[0:P, :]).then_inc(rot_loaded[0], 16)
            sp.dma_start(table[:, :], table_d).then_inc(table_loaded, 16)
            sp.wait_ge(pads_zeroed, PADS)
            vectors = [in_w, in_b, q_w, q_b, k_w, k_b, ln_g[0], ln_b[0], ln_g[1], ln_b[1]]
            for n, v in enumerate(vectors):
                sp.dma_start(rows_in[n * DC:(n + 1) * DC, :], v.rearrange("(c p) -> c p", p=P)).then_inc(small_loaded, 16)
            for l in range(LAYERS):
                for a in range(2):
                    at = NORM_ROWS + (2 * l + a) * HC
                    v = b1[l][a * HID:(a + 1) * HID]
                    full = (HC - 1) * P
                    sp.dma_start(rows_in[at:at + HC - 1, :], v[0:full].rearrange("(m p) -> m p", p=P)).then_inc(small_loaded, 16)
                    sp.dma_start(rows_in[at + HC - 1:at + HC, 0:TAIL], v[full:HID].unsqueeze(0)).then_inc(small_loaded, 16)
            sp.dma_start(win_in[:, 1, :, :], W_in.rearrange("(c p) n -> p c n", p=P)).then_inc(mix_w_loaded, 16)
            sp.dma_start(wq_in[:, 1, :, :], Wq.rearrange("(c p) n -> p c n", p=P)).then_inc(mix_w_loaded, 16)
            sp.dma_start(wk_in[:, 1, :, :], Wk.rearrange("(c p) n -> p c n", p=P)).then_inc(mix_w_loaded, 16)
            sp.dma_start(wout_s[:, :, :], W_out.rearrange("(c p) n -> p c n", p=P)).then_inc(mix_w_loaded, 16)
            def everywhere(v):
                return v.unsqueeze(0).to_broadcast([P, v.shape[0]])

            sp.dma_start(bias_mix[:, 2, :], everywhere(bq)).then_inc(small_loaded, 16)
            sp.dma_start(bias_mix[:, 3, :], everywhere(bk)).then_inc(small_loaded, 16)
            sp.dma_start(out_w_s[:, :], everywhere(out_w)).then_inc(small_loaded, 16)
            sp.dma_start(out_b_s[:, :], everywhere(out_b)).then_inc(small_loaded, 16)
            sp.dma_start(head_scale[:, :], everywhere(log_scale)).then_inc(small_loaded, 16)
            for r in range(MR):
                sp.dma_start(smear_s[r * MD:(r + 1) * MD, :],
                             smear.rearrange("(g r) -> r g", r=MR)[r:r + 1, :].to_broadcast([MD, MG]),
                             allow_slow_non_contiguous=True).then_inc(small_loaded, 16)
            for l in range(LAYERS):
                for n, v in enumerate((q_scale[l], k_scale[l])):
                    sp.dma_start(rot_scale[l][:, n, :, :].rearrange("p a f -> p (a f)"),
                                 everywhere(v)).then_inc(small_loaded, 16)

            def load_wqkv(l):
                sp.dma_start(wqkv_in[:, 1, :, :], wqkv[l].rearrange("(c p) n -> p c n", p=P)).then_inc(wqkv_loaded, 16)

            def load_wo(l):
                sp.dma_start(wo_s[:, :, :], wo[l].rearrange("(c p) n -> p c n", p=P)).then_inc(wo_loaded, 16)

            def load_w1(l):
                w1_v = w1[l].rearrange("(c p) (a n) -> p c a n", p=P, a=2)
                w1_t = w1_s[:, :, :].rearrange("p c (a n) -> p c a n", a=2)
                for a in range(2):
                    sp.dma_start(w1_t[:, :, a, 0:HID], w1_v[:, :, a, :]).then_inc(w1_loaded, 16)

            def load_w2(l):
                sp.dma_start(w2_s[:, 0:HC - 1, :],
                             w2[l][0:(HC - 1) * P, :].rearrange("(m p) n -> p m n", p=P)).then_inc(w2_loaded, 16)
                sp.dma_start(w2_s[0:TAIL, HC - 1, :], w2[l][(HC - 1) * P:HID, :]).then_inc(w2_loaded, 16)

            def load_b2(l):
                sp.dma_start(b2_s[:, :], everywhere(b2[l])).then_inc(b2_loaded, 16)

            load_wqkv(0)
            load_wo(0)
            load_w1(0)
            load_w2(0)
            load_b2(0)

            def body(i):
                mix, proj, att_u, mlp_u, fin = streams(i)
                if i.low + 1 < NW:
                    n = i.back(-1)
                    rows = row(n)
                    if n.back(2).exists():
                        sp.wait_ge(norm_dve.sem, norm_dve.at("xn", n.back(2)))
                    sp.dma_start(x_s[:, n.parity, :], x_f[rows, :]).then_inc(x_loaded[n.parity], 16)
                elif i.low + 1 < UNITS and i.low + 1 >= NW:
                    n = i.back(-1)
                    rows = row(window(n))
                    sp.wait_ge(x2_stored, 16 * (window(n).number() + 1))
                    if n.low >= NW + 2:
                        sp.wait_ge(proj_pe.sem, proj_pe.at("xt", n.back(2)))
                    else:
                        sp.wait_ge(norm_dve.sem, norm_dve.at("xn", n.back(2)))
                    sp.dma_start(x_s[:, n.parity, :], x2_d[rows, :]).then_inc(x_loaded[n.parity], 16)
                if i.low + 1 < UNITS:
                    n = i.back(-1)
                    rows = row(window(n))
                    if n.back(2).exists():
                        sp.wait_ge(proj_pool.sem, proj_pool.at("table", n.back(2)))
                    sp.dma_start(rot_s[:, n.parity, :, :].rearrange("p a f -> p (a f)"), rot_d[rows, :])\
                      .then_inc(rot_loaded[n.parity], 16)
                if proj is not None and layer(proj) == 1:
                    rows = row(window(proj))
                    sp.wait_ge(att_dve.sem, att_dve.at("x1", proj.back(2)))
                    sp.dma_start(x_res[:, proj.parity, :], x2_d[rows, :]).then_inc(res_loaded[proj.parity], 16)
                if fin is not None:
                    w = window(fin)
                    rows = row(w)
                    sp.wait_ge(fin_dve.sem, fin_dve.at("out", w))
                    sp.dma_start(out_f[rows, :], y_out[:, :]).then_inc(out_stored, 16)
                if mlp_u is not None and layer(mlp_u) == 1:
                    w = window(mlp_u)
                    rows = row(w)
                    if w.low == 0:
                        sp.wait_ge(s_stored, 16 * NW)
                    sp.dma_start(s_in[:, :], s_d[rows, :]).then_inc(s_loaded, 16)
                    sp.dma_start(x_in[:, :], x_f[rows, :]).then_inc(xin_loaded, 16)
                if mlp_u is not None and mlp_u.low == NW - 1:
                    sp.wait_ge(mlp_pe.sem, mlp_pe.at("ga", mlp_u))
                    load_w1(1)
                if mlp_u is not None and layer(mlp_u) == 0:
                    rows = row(mlp_u)
                    sp.wait_ge(mlp_dve.sem, mlp_dve.at("x2", mlp_u))
                    sp.dma_start(x2_d[rows, :], x2[:, :]).then_inc(x2_stored, 16)
                if mix is not None:
                    rows = row(mix)
                    sp.wait_ge(mix_pool.sem, mix_pool.at("s", mix))
                    sp.dma_start(s_d[rows, :], s_out[:, :]).then_inc(s_stored, 16)
                if proj is not None and proj.low == NW - 1:
                    sp.wait_ge(proj_pe.sem, proj_pe.at("v", proj))
                    load_wqkv(1)
                if att_u is not None and att_u.low == NW - 1:
                    sp.wait_ge(att_pe.sem, att_pe.at("wo", att_u))
                    load_wo(1)
                    sp.wait_ge(att_pool.sem, att_pool.at("x1b", att_u))
                    load_b2(1)
                if mlp_u is not None and mlp_u.low == NW - 1:
                    sp.wait_ge(mlp_pe.sem, mlp_pe.at("w2", mlp_u))
                    load_w2(1)

            iterations(sp, body)
            sp.wait_ge(out_stored, 16 * NW)
            sp.wait_ge(s_stored, 16 * NW)
            sp.wait_ge(x2_stored, 16 * NW)

        @block.gpsimd
        def _(pool):
            pool.memset(rows_in, 0.0).then_inc(pads_zeroed, 1)
            w1_t = w1_s[:, :, :].rearrange("p c (a n) -> p c a n", a=2)
            pool.memset(w1_t[:, :, :, HID:HIDP], 0.0).then_inc(pads_zeroed, 1)
            pool.memset(w2_s[:, HC - 1, :], 0.0).then_inc(pads_zeroed, 1)
            pool.memset(half_neg[:, :], -0.5).then_inc(setup_pool, 1)
            pool.memset(zero_col[:, :], 0.0).then_inc(setup_pool, 1)
            pool.memset(state[:, :, :], 0.0).then_inc(setup_pool, 1)
            pool.memset(v_mix[:, :, MD:MV], 1.0).then_inc(setup_pool, 1)
            pool.memset(kT[:, :, :, :], 0.0).then_inc(setup_pool, 1)
            pool.memset(v_loc[:, :, :], 0.0).then_inc(setup_pool, 1)
            pool.wait_ge(setup_pool, POOL_SETUP)

            def root(out, in_, w):
                return pool.tensor_tensor(out, in_, half_neg[:, 0:w], ALU.pow)

            def body(i):
                mix, proj, att_u, mlp_u, fin = streams(i)
                if i.low == 0:
                    norm1(i)
                    norm2(i)
                if mlp_u is not None:
                    pool.wait_ge(mlp_dve.sem, mlp_dve.at("var", mlp_u))
                    root(small_h[:, 1:2], small_h[:, 0:1], 1).then_inc(mlp_pool.done("rstd"), 1)
                if proj is not None:
                    u, p = proj, proj.parity
                    if u.back(1).exists():
                        pool.wait_ge(proj_dve.sem, proj_dve.at("cos", u.back(1)))
                        pool.wait_ge(proj_pool.sem, proj_pool.at("inv", u.back(1)))
                    else:
                        pool.wait_ge(setup_dve.sem, setup_dve.at("half", ONCE))
                    pool.wait_ge(rot_loaded[p], 16 * (u.turn() + 1))
                    pool.tensor_tensor(rot_t[:, :, :, :],
                                       rot_s[:, p, :, :].unsqueeze(2).to_broadcast([P, 4, 2, HD // 2]),
                                       rot_scale[layer(u)][:, :, :, :], ALU.mult).then_inc(proj_pool.done("table"), 1)
                if proj is not None:
                    u = proj
                    pool.wait_ge(proj_act.sem, proj_act.at("k", u))
                    pool.wait_ge(proj_pool.sem, proj_pool.at("table", u))
                    r5 = raw[:, :].rearrange("p (a h s f) -> p a h s f", a=2, h=H, s=2)
                    o5 = rot_other[:, :].rearrange("p (a h s f) -> p a h s f", a=2, h=H, s=2)
                    for a in range(2):
                        for s in range(2):
                            ins = pool.tensor_tensor(o5[:, a, :, s, :], r5[:, a, :, 1 - s, :],
                                                     rot_t[:, 2 + a, s, :].unsqueeze(1).to_broadcast([P, H, HD // 2]),
                                                     ALU.mult)
                    ins.then_inc(proj_pool.done("other"), 1)
                if mix is not None:
                    n = mix
                    pool.wait_ge(mix_dve.sem, mix_dve.at("max", n))
                    qk_h = qk.rearrange("p (h d) -> p h d", d=MD)
                    pool.tensor_tensor(qk_h, qk_h, qk_max[:, :].unsqueeze(2).to_broadcast([P, 2 * MH, MD]),
                                       ALU.subtract).then_inc(mix_pool.done("sub"), 1)
                if proj is not None:
                    u, p = proj, proj.parity
                    pool.wait_ge(proj_dve.sem, proj_dve.at("clip", u))
                    root(inv_norm[:, p, :], sq_clip[:, :], 2 * H).then_inc(proj_pool.done("inv"), 1)
                if mix is not None:
                    n = mix
                    pool.wait_ge(mix_dve.sem, mix_dve.at("kinv", n))
                    k_h = qk[:, ME:2 * ME].rearrange("p (h d) -> p h d", d=MD)
                    pool.tensor_tensor(k_h, k_h, k_norm[:, :].unsqueeze(2).to_broadcast([P, MH, MD]),
                                       ALU.mult).then_inc(mix_pool.done("kn"), 1)
                    pool.wait_ge(mix_act.sem, mix_act.at("kt", n))
                    pool.tensor_tensor(kT_mix[:, :, :], kT_raw[:, :, 1:P + 1],
                                       keep_s[:, :].unsqueeze(2).to_broadcast([P, MG, P]),
                                       ALU.mult).then_inc(mix_pool.done("kkeep"), 1)
                    pool.wait_ge(mix_act.sem, mix_act.at("qt", n))
                    pool.tensor_tensor(qT_dec[:, :, :], qT_mix[:, 0:MG // 2, :], query_decay,
                                       ALU.mult).then_inc(mix_pool.done("qdec"), 1)
                if i.low + 1 < NW:
                    norm1(i.back(-1))
                if att_u is not None:
                    if window(att_u).low == 0:
                        pool.wait_ge(b2_loaded, 16 * (layer(att_u) + 1))
                    pool.wait_ge(att_dve.sem, att_dve.at("x1", att_u))
                    pool.tensor_tensor(x1b[:, att_u.parity, :], x1[:, att_u.parity, :], b2_s[:, :],
                                       ALU.add).then_inc(att_pool.done("x1b"), 1)
                if i.low + 1 < NW:
                    norm2(i.back(-1))
                if mix is not None:
                    pool.wait_ge(mix_pe.sem, mix_pe.at("o1", mix))
                    pool.tensor_tensor(state[:, :, :], state[:, :, :],
                                       whole_decay.unsqueeze(2).to_broadcast([P, MG, MR * MV]),
                                       ALU.mult).then_inc(mix_pool.done("sdec"), 1)
                if mix is not None:
                    n = mix
                    pool.wait_ge(mix_dve.sem, mix_dve.at("yvar", n))
                    root(small_y[:, 1:2], small_y[:, 0:1], 1).then_inc(mix_pool.done("yrstd"), 1)
                    pool.wait_ge(mix_dve.sem, mix_dve.at("yn", n))
                    pool.tensor_tensor(y_n[:, :], y_n[:, :], out_w_s[:, :], ALU.mult)\
                        .then_inc(mix_pool.done("yw"), 1)
                    if n.back(1).exists():
                        pool.wait_ge(s_stored, 16 * n.number())
                    pool.wait_ge(mix_pool.sem, mix_pool.at("yw", n))
                    pool.tensor_tensor(s_out[:, :], y_n[:, :], out_b_s[:, :], ALU.add)\
                        .then_inc(mix_pool.done("s"), 1)

            def norm1(n):
                pool.wait_ge(norm_dve.sem, norm_dve.at("var", n))
                root(small_x[:, 1:2], small_x[:, 0:1], 1).then_inc(norm_pool.done("rstd"), 1)

            def norm2(n):
                pool.wait_ge(norm_dve.sem, norm_dve.at("var2", n))
                root(small_x[:, 3:4], small_x[:, 2:3], 1).then_inc(norm_pool.done("rstd2"), 1)

            iterations(pool, body)

        @block.scalar
        def _(act):
            def copy(out, in_):
                return act.activation(out, in_, ACT.Copy)

            act.wait_ge(small_loaded, 16 * SMALL_DMAS)
            act.activation(head_scale[:, :], head_scale[:, :], ACT.Exp).then_inc(setup_act.done("scale"), 1)
            act.activation(smear_s[:, :], smear_s[:, :], ACT.Exp, scale=-1.0).then_inc(setup_act.done("smear"), 1)
            act.wait_ge(setup_pool, POOL_SETUP)
            act.wait_ge(mix_w_loaded, 16 * MIX_W_DMAS)
            act.wait_ge(setup_dve.sem, setup_dve.at("cols", ONCE))
            for n, (w, w_in) in enumerate(((win_s, win_in), (wq_s, wq_in), (wk_s, wk_in))):
                for c in range(DC):
                    ins = act.activation(halved(w[:, 0, c, :]), w_in[:, 1, c, :], ACT.Copy,
                                         scale=norm_cols(2 * n)[:, c:c + 1])
            ins.then_inc(setup_act.done("mix_h"), 1)

            def cut_qkv(l):
                act.wait_ge(wqkv_loaded, 16 * (l + 1))
                copy(halved(wqkv_s[:, 0, :, :]), wqkv_in[:, 1, :, :]).then_inc(setup_act.done(f"qkv_{l}"), 1)

            def exps(step, a):
                s = list(STEP_HEADS).index(step)
                act.wait_ge(att_dve.sem, att_dve.at("m" + step, a))
                for j, h in enumerate(STEP_HEADS[step]):
                    c = 2 * s + j
                    ins = act.activation(prob[:, h, :], prob[:, h, :], ACT.Exp, bias=neg_max[:, c:c + 1],
                                         scale=QK_SCALE, accum_out=row_sum[:, c:c + 1])
                ins.then_inc(att_act.done("e" + step), 1)

            def turned(step, half, a, b):
                act.wait_ge(att_pe.sem, att_pe.at("t" + step, a))
                copy(pT[:, half, :, :], b[:, :].rearrange("p (b i) -> p b i", b=4))\
                    .then_inc(att_act.done("t" + step), 1)

            def body(i):
                mix, proj, a, m, f = streams(i)
                if i.low in QKV_CUT:
                    cut_qkv(QKV_CUT[i.low])
                if proj is not None:
                    act.wait_ge(proj_pe.sem, proj_pe.at("xt", proj))
                    if proj.back(1).exists():
                        act.wait_ge(proj_dve.sem, proj_dve.at("xl", proj.back(1)))
                    if window(proj).low > 0:
                        copy(halved(xT[:, :, 1, 0:1]), halved(xT[:, :, 1, P:P + 1])).then_inc(proj_act.done("halo"), 1)
                    else:
                        copy(halved(xT[:, :, 1, 0:1]), zero_col[:, :].unsqueeze(1).to_broadcast([P, 2, 1]))\
                            .then_inc(proj_act.done("halo"), 1)
                    act.wait_ge(proj_act.sem, proj_act.at("halo", proj))
                    copy(halved(xT[:, 0, :, 1:P + 1]), proj_bank[:, 0:D].rearrange("p (c t) -> p c t", c=DC))\
                        .then_inc(proj_act.done("xt"), 1)
                if mix is not None:
                    act.wait_ge(mix_pe.sem, mix_pe.at("xt", mix))
                    copy(halved(xhT[:, 0, :, :]), mix_bank[0][:, 0:D].rearrange("p (c t) -> p c t", c=DC))\
                        .then_inc(mix_act.done("xt"), 1)
                if f is not None:
                    act.wait_ge(mlp_dve.sem, mlp_dve.at("x2", f))
                    act.activation(y_tanh, x2[:, :], ACT.Tanh, scale=0.5).then_inc(fin_act.done("tanh"), 1)
                if a is not None:
                    exps("a0", a)
                if proj is not None:
                    act.wait_ge(proj_pe.sem, proj_pe.at("q", proj))
                    copy(raw[:, 0:E], proj_bank[:, :]).then_inc(proj_act.done("q"), 1)
                if a is not None:
                    exps("a1", a)
                    exps("b0", a)
                if proj is not None:
                    act.wait_ge(proj_pe.sem, proj_pe.at("k", proj))
                    copy(raw[:, E:2 * E], proj_bank[:, :]).then_inc(proj_act.done("k"), 1)
                if m is not None:
                    act.wait_ge(mlp_pe.sem, mlp_pe.at("ht", m))
                    copy(hT_n[:, :, :], mlp_bank[1][:, 0:D].rearrange("p (c t) -> p c t", c=DC))\
                        .then_inc(mlp_act.done("ht"), 1)
                if proj is not None:
                    act.wait_ge(proj_act.sem, proj_act.at("k", proj))
                    act.activation(rot[:, :], raw[:, :], ACT.Square).then_inc(proj_act.done("square"), 1)
                if a is not None:
                    for k in range(2):
                        turned(f"a{k}", k, a, att_bank[k])
                if mix is not None:
                    act.wait_ge(mix_pool.sem, mix_pool.at("sub", mix))
                    act.activation(qk, qk, ACT.Exp).then_inc(mix_act.done("exp"), 1)
                if a is not None:
                    exps("b1", a)
                if mix is not None:
                    act.wait_ge(mix_dve.sem, mix_dve.at("p", mix))
                    act.activation(p_tanh, p_lin, ACT.Tanh, scale=0.5).then_inc(mix_act.done("tanh"), 1)
                if m is not None:
                    bias = b1_s[layer(m)]
                    if f is not None:
                        act.wait_ge(fin_dve.sem, fin_dve.at("u", window(f)))
                    act.wait_ge(mlp_pe.sem, mlp_pe.at("g0", m))
                    for j in range(4):
                        ins = act.activation(gel[:, j, :], mlp_bank[0][:, j * P:(j + 1) * P], ACT.Gelu,
                                             bias=bias[:, HC + j:HC + j + 1])
                    ins.then_inc(mlp_act.done("g0"), 1)
                if a is not None:
                    act.wait_ge(att_pe.sem, att_pe.at("pva", a))
                    copy(oT[:, 0:2, :], att_bank[0][:, 0:2 * P].rearrange("p (b i) -> p b i", b=2))\
                        .then_inc(att_act.done("pva"), 1)
                if mix is not None:
                    act.wait_ge(mix_pe.sem, mix_pe.at("kt", mix))
                    if mix.low > 0:
                        copy(kT_raw[:, :, 0:1], kT_raw[:, :, P:P + 1]).then_inc(mix_act.done("halo"), 1)
                    else:
                        copy(kT_raw[:, :, 0:1], zero_col[:, :].unsqueeze(1).to_broadcast([P, MG, 1]))\
                            .then_inc(mix_act.done("halo"), 1)
                    act.wait_ge(mix_act.sem, mix_act.at("halo", mix))
                    copy(kT_raw[:, :, 1:P + 1], mix_bank[0][:, :].rearrange("p (g i) -> p g i", g=MG))\
                        .then_inc(mix_act.done("kt"), 1)
                if mix is not None:
                    act.wait_ge(mix_pe.sem, mix_pe.at("qt", mix))
                    copy(qT_mix[:, :, :], mix_bank[1][:, :].rearrange("p (g i) -> p g i", g=MG))\
                        .then_inc(mix_act.done("qt"), 1)
                if a is not None:
                    for k in range(2):
                        turned(f"b{k}", k, a, att_bank[1 + k])
                if m is not None:
                    bias = b1_s[layer(m)]
                    act.wait_ge(mlp_pe.sem, mlp_pe.at("ga", m))
                    for j in range(4, HC):
                        ins = act.activation(gel[:, j, :], mlp_bank[0][:, (j - 4) * P:(j - 3) * P], ACT.Gelu,
                                             bias=bias[:, HC + j:HC + j + 1])
                    ins.then_inc(mlp_act.done("ga"), 1)
                if a is not None:
                    act.wait_ge(att_pe.sem, att_pe.at("pvb", a))
                    copy(oT[:, 2:4, :], att_bank[0][:, 0:2 * P].rearrange("p (b i) -> p b i", b=2))\
                        .then_inc(att_act.done("pvb"), 1)
                if proj is not None:
                    act.wait_ge(proj_pe.sem, proj_pe.at("v", proj))
                    if a is not None:
                        act.wait_ge(att_pe.sem, att_pe.at("pvb", a))
                    copy(v_loc[:, proj.parity, :], proj_bank[:, :]).then_inc(proj_act.done("v"), 1)
                if proj is not None:
                    act.wait_ge(proj_pe.sem, proj_pe.at("qt", proj))
                    copy(qT[:, proj.parity, :, :], proj_bank[:, :].rearrange("p (g i) -> p g i", g=HP))\
                        .then_inc(proj_act.done("qt"), 1)
                if proj is not None:
                    act.wait_ge(proj_pe.sem, proj_pe.at("kt", proj))
                    if proj.low == NW:
                        copy(kT[:, :, 1 - proj.parity, :], zero_col[:, :].unsqueeze(1).to_broadcast([P, HP, P]))
                    copy(kT[:, :, proj.parity, :], proj_bank[:, :].rearrange("p (g i) -> p g i", g=HP))\
                        .then_inc(proj_act.done("kt"), 1)
                if mix is not None:
                    act.wait_ge(mix_pe.sem, mix_pe.at("gt", mix))
                    copy(goT, mix_bank[0][:, :].rearrange("p (g i) -> p g i", g=MG))\
                        .then_inc(mix_act.done("gt"), 1)

            iterations(act, body)

        @block.vector
        def _(dve):
            spread = rot_other[:, 0:3 * DC * P].rearrange("p (n c t) -> p n c t", n=3, c=DC)

            dve.wait_ge(setup_pe.sem, setup_pe.at("cols", ONCE))
            dve.tensor_copy(cols[:, :], bank[4][:, 0:ROWS]).then_inc(setup_dve.done("cols"), 1)
            dve.wait_ge(setup_dve.sem, setup_dve.at("cols", ONCE))
            for n in range(3):
                ins = dve.tensor_copy(spread[:, n, :, :],
                                      norm_cols(2 * n + 1).unsqueeze(2).to_broadcast([P, DC, P]))
            ins.then_inc(setup_dve.done("spread"), 1)

            def pace():
                dve.memset(paced[:, :], 0.0)

            def norm1(n):
                p = n.parity
                dve.wait_ge(x_loaded[p], 16 * (n.turn() + 1))
                dve.bn_stats(stats_x[:, :], x_s[:, p, :]).then_inc(norm_dve.done("stat"), 1)
                dve.wait_ge(norm_dve.sem, norm_dve.at("stat", n))
                pace()
                dve.bn_aggr(mv_x[:, :], stats_x[:, :]).then_inc(norm_dve.done("aggr"), 1)
                dve.wait_ge(norm_dve.sem, norm_dve.at("aggr", n))
                dve.tensor_scalar(small_x[:, 0:1], mv_x[:, 1:2], EPS, None, ALU.add)\
                   .then_inc(norm_dve.done("var"), 1)

            def norm2(n):
                p = n.parity
                dve.wait_ge(norm_pool.sem, norm_pool.at("rstd", n))
                if n.back(2).exists():
                    dve.wait_ge(att_dve.sem, att_dve.at("x1", n.back(2)))
                dve.tensor_scalar(xn[:, p, :], x_s[:, p, :], mv_x[:, 0:1], small_x[:, 1:2],
                                  ALU.subtract, ALU.mult).then_inc(norm_dve.done("xn"), 1)
                dve.tensor_scalar(small_x[:, 2:3], mv_x[:, 1:2], small_x[:, 1:2], small_x[:, 1:2],
                                  ALU.mult, ALU.mult).then_inc(norm_dve.done("sq"), 1)
                dve.wait_ge(norm_dve.sem, norm_dve.at("sq", n))
                dve.tensor_scalar(small_x[:, 2:3], small_x[:, 2:3], EPS, None, ALU.add)\
                   .then_inc(norm_dve.done("var2"), 1)

            def norm3(n):
                p = n.parity
                dve.wait_ge(norm_pool.sem, norm_pool.at("rstd2", n))
                if n.back(1).exists():
                    dve.wait_ge(mix_pe.sem, mix_pe.at("xt", n.back(1)))
                dve.tensor_scalar(xh[:, :], xn[:, p, :], small_x[:, 3:4], None, ALU.mult)\
                   .then_inc(norm_dve.done("xh"), 1)

            def scores(step, a, b):
                s = list(STEP_HEADS).index(step)
                at = (2 if window(a).low == 0 else a.parity) * P
                mask = masks[:, at:at + 2 * P]
                dve.wait_ge(att_pe.sem, att_pe.at("s" + step, a))
                pace()
                for j, h in enumerate(STEP_HEADS[step]):
                    c = 2 * s + j
                    ins = dve.tensor_tensor_reduce(prob[:, h, :], b[:, j * 2 * P:(j + 1) * 2 * P], mask,
                                                   inv_norm[:, a.parity, h:h + 1], -3e38, ALU.add, ALU.max,
                                                   row_max[:, c:c + 1])
                ins.then_inc(att_dve.done("s" + step), 1)
                dve.wait_ge(att_dve.sem, att_dve.at("s" + step, a))
                dve.tensor_scalar(neg_max[:, 2 * s:2 * s + 2], row_max[:, 2 * s:2 * s + 2], -QK_SCALE, None,
                                  ALU.mult).then_inc(att_dve.done("m" + step), 1)

            def weigh(step, a):
                s = list(STEP_HEADS).index(step)
                dve.wait_ge(att_act.sem, att_act.at("e" + step, a))
                dve.reciprocal(row_inv[:, 2 * s:2 * s + 2], row_sum[:, 2 * s:2 * s + 2])\
                   .then_inc(att_dve.done("r" + step), 1)
                dve.wait_ge(att_dve.sem, att_dve.at("r" + step, a))
                for j, h in enumerate(STEP_HEADS[step]):
                    c = 2 * s + j
                    ins = dve.tensor_scalar(prob[:, h, :], prob[:, h, :], row_inv[:, c:c + 1], None, ALU.mult)
                ins.then_inc(att_dve.done("n" + step), 1)

            def heads(ap):
                return ap.rearrange("p (h d) -> p h d", d=MD)

            def mix_read(mix, g):
                b = mix_bank[g // 2][:, 0:2 * MR * MV].rearrange("p (h d) -> p h d", d=MV)
                k = str(g // 2)
                den, rec = o_den[:, g // 2, :], o_rec[:, g // 2, :]
                cols = slice(g * P, (g + 2) * P)
                dve.wait_ge(mix_pe.sem, mix_pe.at("o" + k, mix))
                dve.scalar_tensor_tensor(den, b[:, :, MD], 2.0, q_eps[:, g * MR:(g + 2) * MR],
                                         ALU.mult, ALU.add).then_inc(mix_dve.done("den" + k), 1)
                dve.wait_ge(mix_dve.sem, mix_dve.at("den" + k, mix))
                dve.reciprocal(rec, den).then_inc(mix_dve.done("rec" + k), 1)
                dve.wait_ge(mix_dve.sem, mix_dve.at("rec" + k, mix))
                dve.tensor_tensor(heads(go[:, cols]), b[:, :, 0:MD],
                                  rec.unsqueeze(2).to_broadcast([P, 2 * MR, MD]), ALU.mult)\
                   .then_inc(mix_dve.done("o" + k), 1)
                dve.wait_ge(mix_dve.sem, mix_dve.at("o" + k, mix))
                dve.tensor_tensor(go[:, cols], go[:, cols], gate[:, cols], ALU.mult)\
                   .then_inc(mix_dve.done("go" + k), 1)

            def state_add(mix, g):
                k = str(g // 2)
                b = mix_bank[g // 2][:, 0:2 * MR * MV].rearrange("p (g c) -> p g c", g=2)
                dve.wait_ge(mix_pe.sem, mix_pe.at("st" + k, mix))
                dve.wait_ge(mix_pool.sem, mix_pool.at("sdec", mix))
                for r in range(MR):
                    rows, cols = slice(r * MD, (r + 1) * MD), slice(r * MV, (r + 1) * MV)
                    ins = dve.tensor_tensor(state[rows, g:g + 2, cols], b[rows, :, cols],
                                            state[rows, g:g + 2, cols], ALU.add)
                ins.then_inc(mix_dve.done("st" + k), 1)

            def first_norm():
                norm1(Unit(0, 0, 0))
                norm2(Unit(0, 0, 0))
                norm3(Unit(0, 0, 0))

            first_norm()
            dve.wait_ge(setup_pe.sem, setup_pe.at("vp", ONCE))
            dve.tensor_copy(bias_mix[:, 0, :], bank[0][:, :])
            dve.tensor_copy(bias_mix[:, 1, :], bank[1][:, :])
            dve.wait_ge(setup_pe.sem, setup_pe.at("k", ONCE))
            dve.tensor_tensor(bias_mix[:, 2, :], bank[2][:, :], bias_mix[:, 2, :], ALU.add)
            dve.tensor_tensor(bias_mix[:, 3, :], bank[3][:, :], bias_mix[:, 3, :], ALU.add)\
               .then_inc(setup_dve.done("bias"), 1)
            for l in range(LAYERS):
                ins = dve.tensor_scalar(rot_scale[l][:, 2:4, 0, :], rot_scale[l][:, 0:2, 1, :], -1.0, None, ALU.mult)
            ins.then_inc(setup_dve.done("rneg"), 1)
            for l in range(LAYERS):
                ins = dve.tensor_copy(rot_scale[l][:, 2:4, 1, :], rot_scale[l][:, 0:2, 0, :])
            ins.then_inc(setup_dve.done("rcopy"), 1)
            dve.wait_ge(setup_act.sem, setup_act.at("smear", ONCE))
            dve.tensor_scalar(smear_s[:, :], smear_s[:, :], 1.0, None, ALU.add).then_inc(setup_dve.done("smear1"), 1)
            dve.wait_ge(setup_dve.sem, setup_dve.at("smear1", ONCE))
            dve.reciprocal(smear_s[:, :], smear_s[:, :]).then_inc(setup_dve.done("smear2"), 1)
            dve.wait_ge(setup_dve.sem, setup_dve.at("smear2", ONCE))
            dve.tensor_scalar(keep_s[:, :], smear_s[:, :], -1.0, 1.0, ALU.mult, ALU.add)\
               .then_inc(setup_dve.done("keep"), 1)
            dve.tensor_scalar(head_eps[:, :], head_scale[:, :], 2 * EPS, None, ALU.mult)\
               .then_inc(setup_dve.done("eps"), 1)
            dve.tensor_scalar(out_w_s[:, :], out_w_s[:, :], 0.5, None, ALU.mult)
            dve.tensor_scalar(out_b_s[:, :], out_b_s[:, :], 0.5, None, ALU.mult)\
               .then_inc(setup_dve.done("half"), 1)
            dve.wait_ge(setup_dve.sem, setup_dve.at("half", ONCE))
            dve.wait_ge(table_loaded, 16)

            def low(w, w_in, c, scale):
                return dve.scalar_tensor_tensor(halved(w[:, 1, c, :]), w_in[:, 1, c, :], norm_cols(scale)[:, c:c + 1],
                                                w[:, 0, c, :], ALU.mult, ALU.subtract)

            dve.wait_ge(setup_act.sem, setup_act.at("mix_h", ONCE))
            for n, (w, w_in) in enumerate(((win_s, win_in), (wq_s, wq_in), (wk_s, wk_in))):
                for c in range(DC):
                    ins = low(w, w_in, c, 2 * n)
            ins.then_inc(setup_dve.done("mix_l"), 1)

            def cut_qkv(l):
                dve.wait_ge(setup_act.sem, setup_act.at(f"qkv_{l}", ONCE))
                dve.tensor_tensor(halved(wqkv_s[:, 1, :, :]), wqkv_in[:, 1, :, :], wqkv_s[:, 0, :, :], ALU.subtract)\
                   .then_inc(setup_dve.done(f"qkv_{l}"), 1)

            def low_x(xt, b):
                return dve.tensor_tensor(halved(xt[:, 1, :, :]), b[:, 0:D].rearrange("p (c t) -> p c t", c=DC),
                                         xt[:, 0, :, :], ALU.subtract)

            def fold(l):
                at = NORM_ROWS + l * 2 * HC
                dve.wait_ge(setup_pe.sem, setup_pe.at(f"b1_{l}", ONCE))
                dve.tensor_tensor(b1_s[l][:, :], proj_bank[:, 0:2 * HC], cols[:, at:at + 2 * HC], ALU.add)\
                   .then_inc(setup_dve.done(f"b1_{l}"), 1)
                for c in range(DC):
                    ins = dve.tensor_scalar(w1_s[:, c, :], w1_s[:, c, :], norm_cols(6 + 2 * l)[:, c:c + 1],
                                            None, ALU.mult)
                ins.then_inc(setup_dve.done(f"w1_{l}"), 1)

            def body(i):
                mix, u, a, m, f = streams(i)
                nxt = i.back(-1) if i.low + 1 < NW else None
                if i.low in QKV_CUT:
                    cut_qkv(QKV_CUT[i.low])
                if i.low in W1_FOLD:
                    fold(W1_FOLD[i.low])
                if u is not None:
                    dve.wait_ge(proj_act.sem, proj_act.at("xt", u))
                    low_x(xT[:, :, :, 1:P + 1], proj_bank).then_inc(proj_dve.done("xl"), 1)
                if mix is not None:
                    dve.wait_ge(mix_act.sem, mix_act.at("xt", mix))
                    low_x(xhT, mix_bank[0]).then_inc(mix_dve.done("xl"), 1)
                if a is not None:
                    scores("a0", a, att_bank[0])
                if m is not None:
                    dve.wait_ge(mlp_pe.sem, mlp_pe.at("sh", m))
                    dve.bn_stats(stats_h[:, 0:6], x1[:, m.parity, 0:P])
                    dve.bn_stats(stats_h[:, 6:12], mlp_bank[0][:, 0:P]).then_inc(mlp_dve.done("stat"), 1)
                    dve.wait_ge(mlp_dve.sem, mlp_dve.at("stat", m))
                    pace()
                    dve.bn_aggr(mv_h[:, :], stats_h[:, :]).then_inc(mlp_dve.done("aggr"), 1)
                    dve.wait_ge(mlp_dve.sem, mlp_dve.at("aggr", m))
                    dve.tensor_scalar(small_h[:, 0:1], mv_h[:, 1:2], EPS, None, ALU.add)\
                       .then_inc(mlp_dve.done("var"), 1)
                if a is not None:
                    scores("a1", a, att_bank[1])
                if m is not None:
                    dve.wait_ge(mlp_pool.sem, mlp_pool.at("rstd", m))
                    dve.tensor_scalar(h_n[:, 0:P], x1[:, m.parity, 0:P], mv_h[:, 0:1], small_h[:, 1:2],
                                      ALU.subtract, ALU.mult)
                    dve.tensor_scalar(h_n[:, P:D], mlp_bank[0][:, 0:P], mv_h[:, 0:1], small_h[:, 1:2],
                                      ALU.subtract, ALU.mult).then_inc(mlp_dve.done("hn"), 1)
                if a is not None:
                    scores("b0", a, att_bank[2])
                    weigh("a0", a)
                if mix is not None:
                    dve.wait_ge(mix_pe.sem, mix_pe.at("q", mix))
                    dve.tensor_tensor(qk[:, 0:ME], mix_bank[0][:, :], bias_mix[:, 2, :], ALU.add)\
                       .then_inc(mix_dve.done("q"), 1)
                if a is not None:
                    weigh("a1", a)
                    weigh("b0", a)
                if f is not None:
                    w = window(f)
                    dve.wait_ge(fin_act.sem, fin_act.at("tanh", w))
                    if w.back(1).exists():
                        dve.wait_ge(out_stored, 16 * w.number())
                    dve.scalar_tensor_tensor(y_out[:, :], y_tanh, 1.0, x2[:, :], ALU.add, ALU.mult)\
                       .then_inc(fin_dve.done("u"), 1)
                    dve.wait_ge(s_loaded, 16 * (w.number() + 1))
                    dve.wait_ge(fin_dve.sem, fin_dve.at("u", w))
                    dve.tensor_tensor(y_out[:, :], y_out[:, :], s_in[:, :], ALU.mult)\
                       .then_inc(fin_dve.done("us"), 1)
                    dve.wait_ge(xin_loaded, 16 * (w.number() + 1))
                    dve.wait_ge(fin_dve.sem, fin_dve.at("us", w))
                    dve.tensor_tensor(y_out[:, :], y_out[:, :], x_in[:, :], ALU.add)\
                       .then_inc(fin_dve.done("out"), 1)
                if mix is not None:
                    dve.wait_ge(mix_pe.sem, mix_pe.at("k", mix))
                    dve.tensor_tensor(qk[:, ME:2 * ME], mix_bank[1][:, :], bias_mix[:, 3, :], ALU.add)\
                       .then_inc(mix_dve.done("k"), 1)
                    dve.wait_ge(mix_dve.sem, mix_dve.at("k", mix))
                    dve.tensor_reduce(qk_max[:, :], heads(qk), AX_X, ALU.max).then_inc(mix_dve.done("max"), 1)
                if u is not None:
                    dve.wait_ge(proj_act.sem, proj_act.at("square", u))
                    dve.tensor_reduce(sq_sum[:, :], rot[:, :].rearrange("p (h d) -> p h d", d=HD), AX_X, ALU.add)\
                       .then_inc(proj_dve.done("sqsum"), 1)
                    dve.wait_ge(proj_dve.sem, proj_dve.at("sqsum", u))
                    dve.tensor_scalar(sq_clip[:, :], sq_sum[:, :], 1e-24, None, ALU.max)\
                       .then_inc(proj_dve.done("clip"), 1)
                if a is not None:
                    scores("b1", a, att_bank[2])
                if mix is not None:
                    dve.wait_ge(mix_pe.sem, mix_pe.at("v", mix))
                    dve.tensor_tensor(v_mix[:, :, 0:MD], heads(mix_bank[0][:, :]), heads(bias_mix[:, 0, :]),
                                      ALU.add).then_inc(mix_dve.done("v"), 1)
                if mix is not None:
                    dve.wait_ge(mix_pe.sem, mix_pe.at("p", mix))
                    dve.tensor_tensor(p_lin, mix_bank[1][:, :], bias_mix[:, 1, :], ALU.add)\
                       .then_inc(mix_dve.done("p"), 1)
                if mix is not None:
                    dve.wait_ge(mix_act.sem, mix_act.at("exp", mix))
                    dve.tensor_reduce(qk_sum[:, :], heads(qk), AX_X, ALU.add).then_inc(mix_dve.done("sum"), 1)
                    dve.wait_ge(mix_dve.sem, mix_dve.at("sum", mix))
                    dve.tensor_tensor(k_norm[:, :], qk_sum[:, MH:2 * MH], head_scale[:, :], ALU.mult)\
                       .then_inc(mix_dve.done("kscale"), 1)
                    dve.wait_ge(mix_dve.sem, mix_dve.at("kscale", mix))
                    dve.reciprocal(k_norm[:, :], k_norm[:, :]).then_inc(mix_dve.done("kinv"), 1)
                    dve.tensor_tensor(q_eps[:, :], qk_sum[:, 0:MH], head_eps[:, :], ALU.mult)\
                       .then_inc(mix_dve.done("qeps"), 1)
                if a is not None:
                    weigh("b1", a)
                if u is not None:
                    four = lambda ap: ap.rearrange("p (a h d) -> p a h d", a=2, h=H)
                    dve.wait_ge(proj_pool.sem, proj_pool.at("table", u))
                    dve.tensor_tensor(four(rot[:, :]), four(raw[:, :]),
                                      rot_t[:, 0:2, :, :].rearrange("p a s f -> p a (s f)").unsqueeze(2)
                                      .to_broadcast([P, 2, H, HD]), ALU.mult).then_inc(proj_dve.done("cos"), 1)
                    dve.wait_ge(proj_pool.sem, proj_pool.at("other", u))
                    dve.wait_ge(proj_dve.sem, proj_dve.at("cos", u))
                    dve.tensor_tensor(rot[:, :], rot[:, :], rot_other[:, :], ALU.add)\
                       .then_inc(proj_dve.done("rot"), 1)
                if mix is not None:
                    dve.wait_ge(mix_pool.sem, mix_pool.at("kkeep", mix))
                    for g in range(MG):
                        ins = dve.scalar_tensor_tensor(kT_mix[:, g, :], kT_raw[:, g, 0:P], smear_s[:, g:g + 1],
                                                       kT_mix[:, g, :], ALU.mult, ALU.add)
                    ins.then_inc(mix_dve.done("ksmear"), 1)
                if u is not None:
                    k_h = rot[:, E:2 * E].rearrange("p (h d) -> p h d", d=HD)
                    dve.wait_ge(proj_pool.sem, proj_pool.at("inv", u))
                    dve.wait_ge(proj_dve.sem, proj_dve.at("rot", u))
                    dve.tensor_tensor(k_h, k_h, inv_norm[:, u.parity, H:2 * H].unsqueeze(2).to_broadcast([P, H, HD]),
                                      ALU.mult).then_inc(proj_dve.done("knorm"), 1)
                if m is not None:
                    bias = b1_s[layer(m)]
                    dve.wait_ge(mlp_pe.sem, mlp_pe.at("a0", m))
                    dve.wait_ge(mlp_act.sem, mlp_act.at("g0", m))
                    for j in range(4):
                        ins = dve.scalar_tensor_tensor(hid[:, j, :], mlp_bank[1][:, j * P:(j + 1) * P],
                                                       bias[:, j:j + 1], gel[:, j, :], ALU.add, ALU.mult)
                    ins.then_inc(mlp_dve.done("a0"), 1)
                if mix is not None:
                    dve.wait_ge(mix_pe.sem, mix_pe.at("kb", mix))
                    dve.tensor_tensor(heads(k_dec[:, :]), heads(mix_bank[1][:, :]),
                                      key_decay.unsqueeze(2).to_broadcast([P, MH, MD]), ALU.mult)\
                       .then_inc(mix_dve.done("kdec"), 1)
                if mix is not None:
                    dve.wait_ge(mix_act.sem, mix_act.at("tanh", mix))
                    dve.scalar_tensor_tensor(gate[:, :], p_tanh, 1.0, p_lin, ALU.add, ALU.mult)\
                       .then_inc(mix_dve.done("gate"), 1)
                if mix is not None:
                    for r in range(MR):
                        b = mix_bank[r % 2][:, :].rearrange("p (g i) -> p g i", g=MG)
                        dve.wait_ge(mix_pe.sem, mix_pe.at(f"s{r}", mix))
                        dve.tensor_tensor(att[:, r, 0:MG // 2, :], b[:, 0:MG // 2, :], decay[:, r, :, :], ALU.mult)
                        dve.tensor_tensor(att[:, r, MG // 2:MG, :], b[:, MG // 2:MG, :],
                                          causal.unsqueeze(1).to_broadcast([P, MG // 2, P]), ALU.mult)\
                           .then_inc(mix_dve.done(f"s{r}"), 1)
                if m is not None:
                    bias = b1_s[layer(m)]
                    dve.wait_ge(mlp_act.sem, mlp_act.at("ga", m))
                    for j in range(4, HC):
                        ins = dve.scalar_tensor_tensor(hid[:, j, :], mlp_bank[0][:, (j - 2) * P:(j - 1) * P],
                                                       bias[:, j:j + 1], gel[:, j, :], ALU.add, ALU.mult)
                    ins.then_inc(mlp_dve.done("ga"), 1)
                if nxt is not None:
                    norm1(nxt)
                if a is not None:
                    dve.wait_ge(att_pe.sem, att_pe.at("wo", a))
                    if layer(a) == 0:
                        res = xn
                    else:
                        res = x_res
                        dve.wait_ge(res_loaded[a.parity], 16 * (window(a).turn() + 1))
                    dve.tensor_tensor(x1[:, a.parity, :], att_bank[1][:, 0:D], res[:, a.parity, :], ALU.add)\
                       .then_inc(att_dve.done("x1"), 1)
                if mix is not None:
                    mix_read(mix, 0)
                if nxt is not None:
                    norm2(nxt)
                if mix is not None:
                    mix_read(mix, 2)
                if nxt is not None:
                    norm3(nxt)
                if mix is not None:
                    state_add(mix, 0)
                if mix is not None:
                    state_add(mix, 2)
                if m is not None:
                    dve.wait_ge(mlp_pe.sem, mlp_pe.at("w2", m))
                    dve.wait_ge(att_pool.sem, att_pool.at("x1b", m))
                    if layer(m) == 1:
                        dve.wait_ge(x2_stored, 16 * NW)
                    elif m.back(1).exists():
                        dve.wait_ge(x2_stored, 16 * m.number())
                    dve.tensor_tensor(x2[:, :], mlp_bank[1][:, 0:D], x1b[:, m.parity, :], ALU.add)\
                       .then_inc(mlp_dve.done("x2"), 1)
                if mix is not None:
                    b = mix_bank[1][:, 0:D]
                    dve.wait_ge(mix_pe.sem, mix_pe.at("wout", mix))
                    dve.bn_stats(stats_y[:, :], b).then_inc(mix_dve.done("ystat"), 1)
                    dve.wait_ge(mix_dve.sem, mix_dve.at("ystat", mix))
                    pace()
                    dve.bn_aggr(mv_y[:, :], stats_y[:, :]).then_inc(mix_dve.done("yaggr"), 1)
                    dve.wait_ge(mix_dve.sem, mix_dve.at("yaggr", mix))
                    dve.tensor_scalar(small_y[:, 0:1], mv_y[:, 1:2], EPS, None, ALU.add)\
                       .then_inc(mix_dve.done("yvar"), 1)
                    dve.wait_ge(mix_pool.sem, mix_pool.at("yrstd", mix))
                    dve.tensor_scalar(y_n[:, :], b, mv_y[:, 0:1], small_y[:, 1:2], ALU.subtract, ALU.mult)\
                       .then_inc(mix_dve.done("yn"), 1)

            iterations(dve, body)

        @block.tensor
        def _(pe):
            def mm(out, lhsT, rhs, first, last):
                return pe.matmul(out, lhsT, rhs, start=first, stop=last)

            def mm3(out, left, right, first, last):
                for n, (a, b) in enumerate(((1, 0), (0, 1), (0, 0))):
                    ins = pe.matmul(out, halved(left[:, a]), halved(right[:, b]), start=first and n == 0,
                                    stop=last and n == 2)
                return ins

            def transposes(out, parts):
                for j, part in enumerate(parts):
                    ins = pe.transpose(out[:, j * P:(j + 1) * P], part, ident)
                return ins

            spread = rot_other[:, 0:3 * DC * P].rearrange("p (n c t) -> p n c t", n=3, c=DC)
            pe.wait_ge(small_loaded, 16 * SMALL_DMAS)
            pe.wait_ge(table_loaded, 16)
            pe.transpose(bank[4][:, 0:ROWS], rows_in, ident[0:ROWS, 0:ROWS]).then_inc(setup_pe.done("cols"), 1)
            pe.wait_ge(setup_dve.sem, setup_dve.at("spread", ONCE))
            pe.wait_ge(mix_w_loaded, 16 * MIX_W_DMAS)
            for t in range(2):
                for c in range(DC):
                    ins = mm(bank[t][:, :], spread[:, 0, c, :], win_in[:, 1, c, t * ME:(t + 1) * ME], c == 0, c == DC - 1)
            ins.then_inc(setup_pe.done("vp"), 1)
            for n, (w, name) in enumerate(((wq_in, "q"), (wk_in, "k"))):
                for c in range(DC):
                    ins = mm(bank[2 + n][:, :], spread[:, 1 + n, c, :], w[:, 1, c, :], c == 0, c == DC - 1)
                ins.then_inc(setup_pe.done(name), 1)
            pe.wait_ge(setup_dve.sem, setup_dve.at("mix_l", ONCE))
            pe.wait_ge(setup_pool, POOL_SETUP)

            def fold(i, l):
                pe.wait_ge(w1_loaded, 16 * W1_DMAS * (l + 1))
                pe.wait_ge(proj_act.sem, proj_act.at("kt", i.back(1)))
                for j in range(2 * HC):
                    for c in range(DC):
                        ins = mm(proj_bank[:, j:j + 1], w1_s[:, c, j * P:(j + 1) * P],
                                 norm_cols(7 + 2 * l)[:, c:c + 1], c == 0, c == DC - 1)
                ins.then_inc(setup_pe.done(f"b1_{l}"), 1)
                pe.wait_ge(setup_dve.sem, setup_dve.at(f"b1_{l}", ONCE))

            def att_scores(step, a, b):
                for j, h in enumerate(STEP_HEADS[step]):
                    rows = slice(HD * (h % 2), HD * (h % 2) + HD)
                    ins = mm(b[:, j * 2 * P:(j + 1) * 2 * P], qT[rows, a.parity, h // 2, :],
                             kT[rows, h // 2, :, :].rearrange("p s j -> p (s j)"), True, True)
                ins.then_inc(att_pe.done("s" + step), 1)

            def att_turn(step, a, b):
                pe.wait_ge(att_dve.sem, att_dve.at("n" + step, a))
                parts = [prob[:, h, s * P:(s + 1) * P] for h in STEP_HEADS[step] for s in range(2)]
                transposes(b, parts).then_inc(att_pe.done("t" + step), 1)

            def att_values(half, a, b):
                for s in range(2):
                    for j, h in enumerate(STEP_HEADS[f"{half}{s}"]):
                        out = b[HD * (h % 2):HD * (h % 2) + HD, j * P:(j + 1) * P]
                        for slot in range(2):
                            ins = mm(out, v_loc[:, slot, h * HD:(h + 1) * HD], pT[:, s, 2 * j + slot, :],
                                     slot == 0, slot == 1)
                ins.then_inc(att_pe.done("pv" + half), 1)

            def mix_linear(mix, step, b, w, col):
                for c in range(DC):
                    ins = mm3(b[:, :], xhT[:, :, c, :], w[:, :, c, col:col + ME], c == 0, c == DC - 1)
                ins.then_inc(mix_pe.done(step), 1)

            def proj_linear(u, step, col):
                for c in range(DC):
                    ins = mm3(proj_bank[:, :], xT[:, :, c, 1 - c:1 - c + P], wqkv_s[:, :, c, col:col + E],
                              c == 0, c == DC - 1)
                ins.then_inc(proj_pe.done(step), 1)

            def hidden(m, b, at, first, count):
                for j in range(count):
                    for c in range(DC):
                        ins = mm(b[:, (at + j) * P:(at + j + 1) * P], w1_s[:, c, (first + j) * P:(first + j + 1) * P],
                                 hT_n[:, c, :], c == 0, c == DC - 1)
                return ins

            def out_projection(a):
                if window(a).low == 0:
                    pe.wait_ge(wo_loaded, 16 * (layer(a) + 1))
                pe.wait_ge(att_act.sem, att_act.at("pvb", a))
                for g in range(HP):
                    ins = mm(att_bank[1][:, 0:D], oT[:, g, :], wo_s[:, g, :], g == 0, g == HP - 1)
                ins.then_inc(att_pe.done("wo"), 1)

            def mlp_out(m, first, last):
                if first == 0:
                    if window(m).low == 0:
                        pe.wait_ge(w2_loaded, 16 * W2_DMAS * (layer(m) + 1))
                    pe.wait_ge(mlp_dve.sem, mlp_dve.at("a0", m))
                if last > 4:
                    pe.wait_ge(mlp_dve.sem, mlp_dve.at("ga", m))
                for j in range(first, last):
                    ins = mm(mlp_bank[1][:, 0:D], hid[:, j, :], w2_s[:, j, :], j == 0, j == HC - 1)
                if last == HC:
                    ins.then_inc(mlp_pe.done("w2"), 1)

            def mix_scores(mix, r):
                steps, name = [(mix_act, "kt"), (mix_dve, "kdec"), (mix_dve, "s0"), (mix_dve, "s1")][r]
                pe.wait_ge(steps.sem, steps.at(name, mix))
                rows = slice(r * MD, (r + 1) * MD)
                for g in range(MG):
                    ins = mm(mix_bank[r % 2][:, g * P:(g + 1) * P], kT_mix[rows, g, :], qT_mix[rows, g, :],
                             True, True)
                ins.then_inc(mix_pe.done(f"s{r}"), 1)

            def mix_out(mix, k):
                for g in (2 * k, 2 * k + 1):
                    q_g = qT_dec[:, g, :] if g < MG // 2 else qT_mix[:, g, :]
                    at = (g % 2) * MR * MV
                    mm(mix_bank[k][:, at:at + MR * MV], q_g, state[:, g, :], True, False)
                    for r in range(MR):
                        ins = mm(mix_bank[k][:, at + r * MV:at + (r + 1) * MV], att[:, r, g, :],
                                 v_mix[:, g * MR + r, :], False, r == MR - 1)
                ins.then_inc(mix_pe.done(f"o{k}"), 1)

            def body(i):
                mix, u, a, m, f = streams(i)
                if i.low in W1_FOLD:
                    fold(i, W1_FOLD[i.low])
                if u is not None:
                    if layer(u) == 0:
                        pe.wait_ge(norm_dve.sem, norm_dve.at("xn", u))
                        src = xn
                    else:
                        pe.wait_ge(x_loaded[u.parity], 16 * (u.turn() + 1))
                        src = x_s
                    if u.back(1).exists():
                        pe.wait_ge(proj_act.sem, proj_act.at("kt", u.back(1)))
                    transposes(proj_bank, [src[:, u.parity, c * P:(c + 1) * P] for c in range(DC)])\
                        .then_inc(proj_pe.done("xt"), 1)
                if mix is not None:
                    pe.wait_ge(norm_dve.sem, norm_dve.at("xh", mix))
                    if mix.back(1).exists():
                        pe.wait_ge(mix_act.sem, mix_act.at("gt", mix.back(1)))
                    transposes(mix_bank[0], [xh[:, c * P:(c + 1) * P] for c in range(DC)])\
                        .then_inc(mix_pe.done("xt"), 1)
                if a is not None:
                    pe.wait_ge(proj_act.sem, proj_act.at("kt", a))
                    if a.back(1).exists():
                        pe.wait_ge(att_act.sem, att_act.at("pvb", a.back(1)))
                    att_scores("a0", a, att_bank[0])
                if m is not None:
                    pe.wait_ge(att_dve.sem, att_dve.at("x1", m))
                    if m.back(1).exists():
                        pe.wait_ge(mlp_dve.sem, mlp_dve.at("ga", m.back(1)))
                    start = window(m).low == 0
                    ins = mm(mlp_bank[0][:, 0:P], shift, x1[:, m.parity, P:D], True, start)
                    if not start:
                        ins = mm(mlp_bank[0][:, 0:P], carry, x1[:, 1 - m.parity, P:D], False, True)
                    ins.then_inc(mlp_pe.done("sh"), 1)
                if a is not None:
                    if a.back(1).exists():
                        pe.wait_ge(att_dve.sem, att_dve.at("x1", a.back(1)))
                    att_scores("a1", a, att_bank[1])
                if u is not None:
                    if window(u).low == 0:
                        pe.wait_ge(setup_dve.sem, setup_dve.at(f"qkv_{layer(u)}", ONCE))
                    pe.wait_ge(proj_dve.sem, proj_dve.at("xl", u))
                    proj_linear(u, "q", 0)
                if a is not None:
                    if a.back(1).exists():
                        pe.wait_ge(att_act.sem, att_act.at("tb1", a.back(1)))
                    att_scores("b0", a, att_bank[2])
                if mix is not None:
                    pe.wait_ge(mix_dve.sem, mix_dve.at("xl", mix))
                    mix_linear(mix, "q", mix_bank[0], wq_s, 0)
                if u is not None:
                    pe.wait_ge(proj_act.sem, proj_act.at("q", u))
                    proj_linear(u, "k", E)
                if mix is not None:
                    if mix.back(1).exists():
                        pe.wait_ge(mix_dve.sem, mix_dve.at("yn", mix.back(1)))
                    mix_linear(mix, "k", mix_bank[1], wk_s, 0)
                if m is not None:
                    pe.wait_ge(mlp_dve.sem, mlp_dve.at("hn", m))
                    if m.back(1).exists():
                        pe.wait_ge(mlp_dve.sem, mlp_dve.at("x2", m.back(1)))
                    transposes(mlp_bank[1], [h_n[:, c * P:(c + 1) * P] for c in range(DC)])\
                        .then_inc(mlp_pe.done("ht"), 1)
                if a is not None:
                    pe.wait_ge(att_dve.sem, att_dve.at("sb0", a))
                    att_scores("b1", a, att_bank[2])
                if a is not None:
                    att_turn("a0", a, att_bank[0])
                if mix is not None:
                    pe.wait_ge(mix_dve.sem, mix_dve.at("q", mix))
                    mix_linear(mix, "v", mix_bank[0], win_s, 0)
                if a is not None:
                    att_turn("a1", a, att_bank[1])
                if mix is not None:
                    pe.wait_ge(mix_dve.sem, mix_dve.at("k", mix))
                    mix_linear(mix, "p", mix_bank[1], win_s, ME)
                if m is not None:
                    if window(m).low == 0:
                        pe.wait_ge(setup_dve.sem, setup_dve.at(f"w1_{layer(m)}", ONCE))
                    pe.wait_ge(mlp_act.sem, mlp_act.at("ht", m))
                    hidden(m, mlp_bank[0], 0, HC, 4).then_inc(mlp_pe.done("g0"), 1)
                if a is not None:
                    pe.wait_ge(att_act.sem, att_act.at("ta1", a))
                    pe.wait_ge(proj_act.sem, proj_act.at("v", a))
                    att_values("a", a, att_bank[0])
                if m is not None:
                    hidden(m, mlp_bank[1], 0, 0, 4).then_inc(mlp_pe.done("a0"), 1)
                if mix is not None:
                    pe.wait_ge(mix_act.sem, mix_act.at("exp", mix))
                    pe.wait_ge(mix_dve.sem, mix_dve.at("p", mix))
                    transposes(mix_bank[1], [qk[:, g * P:(g + 1) * P] for g in range(MG)])\
                        .then_inc(mix_pe.done("qt"), 1)
                if mix is not None:
                    pe.wait_ge(mix_pool.sem, mix_pool.at("kn", mix))
                    pe.wait_ge(mix_dve.sem, mix_dve.at("v", mix))
                    transposes(mix_bank[0], [qk[:, ME + g * P:ME + (g + 1) * P] for g in range(MG)])\
                        .then_inc(mix_pe.done("kt"), 1)
                if a is not None:
                    att_turn("b0", a, att_bank[1])
                if u is not None and mix is None:
                    pe.wait_ge(proj_act.sem, proj_act.at("k", u))
                    proj_linear(u, "v", 2 * E)
                if a is not None:
                    att_turn("b1", a, att_bank[2])
                if m is not None:
                    pe.wait_ge(mlp_act.sem, mlp_act.at("g0", m))
                    hidden(m, mlp_bank[0], 0, HC + 4, 2)
                    hidden(m, mlp_bank[0], 2, 4, 2).then_inc(mlp_pe.done("ga"), 1)
                if u is not None and mix is not None:
                    pe.wait_ge(proj_act.sem, proj_act.at("k", u))
                    proj_linear(u, "v", 2 * E)
                if a is not None:
                    pe.wait_ge(att_act.sem, att_act.at("tb1", a))
                    att_values("b", a, att_bank[0])
                if mix is not None:
                    pe.wait_ge(mix_dve.sem, mix_dve.at("ksmear", mix))
                    pe.wait_ge(mix_act.sem, mix_act.at("qt", mix))
                    transposes(mix_bank[1], [kT_mix[:, g, :] for g in range(MG)]).then_inc(mix_pe.done("kb"), 1)
                if m is not None and mix is None:
                    mlp_out(m, 0, 4)
                if mix is not None:
                    mix_scores(mix, 0)
                if u is not None:
                    pe.wait_ge(proj_act.sem, proj_act.at("v", u))
                    pe.wait_ge(proj_dve.sem, proj_dve.at("rot", u))
                    transposes(proj_bank, [rot[:, g * P:(g + 1) * P] for g in range(HP)])\
                        .then_inc(proj_pe.done("qt"), 1)
                if mix is not None:
                    mix_scores(mix, 1)
                if a is not None and mix is None:
                    out_projection(a)
                if u is not None:
                    pe.wait_ge(proj_act.sem, proj_act.at("qt", u))
                    pe.wait_ge(proj_dve.sem, proj_dve.at("knorm", u))
                    transposes(proj_bank, [rot[:, E + g * P:E + (g + 1) * P] for g in range(HP)])\
                        .then_inc(proj_pe.done("kt"), 1)
                if mix is not None:
                    for r in range(MR // 2, MR):
                        mix_scores(mix, r)
                if a is not None and mix is not None:
                    out_projection(a)
                if mix is not None:
                    pe.wait_ge(mix_pool.sem, mix_pool.at("qdec", mix))
                    if mix.back(1).exists():
                        pe.wait_ge(mix_dve.sem, mix_dve.at("st1", mix.back(1)))
                    pe.wait_ge(mix_dve.sem, mix_dve.at("s3", mix))
                    mix_out(mix, 0)
                if m is not None and mix is not None:
                    mlp_out(m, 0, 3)
                if mix is not None:
                    mix_out(mix, 1)
                if m is not None and mix is not None:
                    mlp_out(m, 3, 5)
                if m is not None and mix is None:
                    mlp_out(m, 4, 5)
                if mix is not None:
                    for k in range(2):
                        pe.wait_ge(mix_dve.sem, mix_dve.at(f"o{k}", mix))
                        for g in (2 * k, 2 * k + 1):
                            at = (g % 2) * MR * MV
                            ins = mm(mix_bank[k][:, at:at + MR * MV], k_dec[:, g * P:(g + 1) * P],
                                     v_mix[:, g * MR:(g + 1) * MR, :].rearrange("p h d -> p (h d)"), True, True)
                        ins.then_inc(mix_pe.done(f"st{k}"), 1)
                if mix is not None:
                    pe.wait_ge(mix_dve.sem, mix_dve.at("st0", mix))
                    pe.wait_ge(mix_dve.sem, mix_dve.at("go1", mix))
                    transposes(mix_bank[0], [go[:, g * P:(g + 1) * P] for g in range(MG)])\
                        .then_inc(mix_pe.done("gt"), 1)
                if m is not None:
                    mlp_out(m, 5, HC)
                if mix is not None:
                    pe.wait_ge(mix_act.sem, mix_act.at("gt", mix))
                    pe.wait_ge(mix_dve.sem, mix_dve.at("st1", mix))
                    for g in range(MG):
                        ins = mm(mix_bank[1][:, 0:D], goT[:, g, :], wout_s[:, g, :], g == 0, g == MG - 1)
                    ins.then_inc(mix_pe.done("wout"), 1)

            iterations(pe, body)


_INS = ["x", "in_ln_w", "in_ln_b", "q_ln_w", "q_ln_b", "k_ln_w", "k_ln_b", "out_ln_w", "out_ln_b",
        "W_in", "W_out", "Wq", "bq", "Wk", "bk", "smear_factor", "log_scale"]
_FFN = ["wqkv", "q_scale", "k_scale", "wo", "ln_g", "ln_b", "w1", "b1", "w2", "b2"]


def kernel(**inputs):
    import concourse.bacc as _bacc
    from concourse.bass_utils import run_bass_kernel_spmd as _run

    nc = _bacc.Bacc("TRN2", target_bir_lowering=False, num_devices=1)
    table, table_at, rotary = constants()
    arrays, args = {}, []
    named = [(f"L0_attn_{n}", None) for n in _INS] + [(f"L0_ffn_{n}", None) for n in _FFN]
    named += [("table", table), ("rotary", rotary)]
    for name, a in named:
        a = np.ascontiguousarray(inputs[name] if a is None else a)
        arrays[f"in_{name}"] = a
        args.append(nc.dram_tensor(f"in_{name}", a.shape, mybir.dt.from_np(a.dtype), kind="ExternalInput").ap())
    out = nc.dram_tensor("out_0", [1, TOKENS, D], F32, kind="ExternalOutput").ap()
    build(nc, *args, table_at, out)
    r = _run(nc, [arrays], core_ids=[0])
    return r.results[0]["out_0"]
```

```python
from contextlib import ExitStack

import numpy as np

import concourse.bass as bass
from concourse import mybir

F32 = mybir.dt.float32
F32R = mybir.dt.float32r
ALU = mybir.AluOpType
ACT = mybir.ActivationFunctionType
AX_X = mybir.AxisListType.X

P = 128
D = 256
DC = D // P
TOKENS = 4096
NW = TOKENS // P
LAYERS = 2
IN_ROWS = 6 * DC
NORM_ROWS = 10 * DC
UNITS = LAYERS * NW
EPS = 1e-5
MH, MD = 16, 32
ME = MH * MD
MG = ME // P
MR = P // MD
MV = MD + 1
H, HD = 8, 64
E = H * HD
HP = H // 2
QK_SCALE = 8.0
HID = int(D * 4 * 2 / 3)
HC = -(-HID // P)
HIDP = HC * P
TAIL = HID - (HC - 1) * P

ROWS = NORM_ROWS + LAYERS * 2 * HC

MASKED = -1e30

STEP_HEADS = {"a0": (0, 2), "a1": (1, 3), "b0": (4, 6), "b1": (5, 7)}


def constants():
    f = np.float32
    slopes = (f(2.0) ** np.linspace(0.0, -8.0, MH // 2, dtype=f)).astype(f)
    slopes = np.concatenate([slopes, np.zeros(MH - MH // 2, f)])
    t = np.arange(P, dtype=f)
    j, i = t[:, None], t[None, :]
    causal = (i >= j).astype(f)
    decay = np.zeros((P, MR, MG // 2, P), f)
    for r in range(MR):
        for g in range(MG // 2):
            decay[:, r, g, :] = np.exp(-slopes[g * MR + r] * np.maximum(i - j, 0)) * causal
    query = np.zeros((P, MG // 2, P), f)
    whole = np.zeros((P, MG), f)
    for r in range(MR):
        for g in range(MG):
            if g < MG // 2:
                query[r * MD:(r + 1) * MD, g, :] = np.exp(-slopes[g * MR + r] * (t + 1))[None, :]
            whole[r * MD:(r + 1) * MD, g] = np.exp(-slopes[g * MR + r] * f(P))
    key = np.exp(-slopes[None, :] * (P - 1 - t[:, None])).astype(f)
    own = np.where(i <= j, f(0), f(MASKED)).astype(f)
    before = np.where(i >= j, f(0), f(MASKED)).astype(f)
    none = np.full((P, P), MASKED, f)
    masks = np.stack([own, before, own, none], 1)
    parts = {
        "ident": np.eye(P, dtype=f), "causal": causal,
        "decay": decay.reshape(P, -1), "query": query.reshape(P, -1), "whole": whole,
        "key": key, "masks": masks.reshape(P, -1),
    }
    at, n = {}, 0
    for name, a in parts.items():
        at[name] = (n, n + a.shape[1])
        n += a.shape[1]
    table = np.ascontiguousarray(np.concatenate(list(parts.values()), 1).astype(f))
    half = np.arange(0, HD, 2, dtype=f)
    inv = (f(1.0) / f(10000.0) ** (half / f(HD))).astype(f)
    pos = np.arange(TOKENS, dtype=f)
    ang = (pos[:, None] * inv[None, :]).astype(f)
    base = ((half + f(0.4 * HD)) / f(1.4 * HD)).astype(f)
    power = ((pos - TOKENS // 2) / f(P // 2)).astype(f)
    scale = (base[None, :] ** power[:, None]).astype(f)
    cos, sin = np.cos(ang), np.sin(ang)
    rot = np.stack([cos * scale, cos / scale, sin * scale, sin / scale], 1).astype(f)
    return table, at, np.ascontiguousarray(rot.reshape(TOKENS, -1))


class Unit:

    def __init__(self, k, c, low):
        self.k, self.c, self.low = k, c, low
        self.parity = c % 2

    def number(self):
        return 2 * self.k + self.c

    def back(self, d):
        return Unit(self.k, self.c - d, self.low - d)

    def exists(self):
        return self.low >= 0

    def turn(self):
        return self.k + self.c // 2


class Steps:

    def __init__(self, sem, names):
        self.sem, self.names, self.next = sem, names.split(), 0

    def done(self, name):
        assert self.names[self.next] == name, (self.names[self.next], name)
        self.next = (self.next + 1) % len(self.names)
        return self.sem

    def at(self, name, unit):
        return len(self.names) * unit.number() + self.names.index(name) + 1


def build(nc, x_d, in_w, in_b, q_w, q_b, k_w, k_b, out_w, out_b, W_in, W_out, Wq, bq, Wk, bk,
          smear, log_scale, wqkv, q_scale, k_scale, wo, ln_g, ln_b, w1, b1, w2, b2,
          table_d, rot_d, table_at, out_d):
    TW = table_d.shape[1]
    x2_d = nc.dram_tensor("x2_between_layers", [TOKENS, D], F32, kind="Internal").ap()
    s_d = nc.dram_tensor("s_between_passes", [TOKENS, D], F32, kind="Internal").ap()
    x_f = x_d.rearrange("a t d -> (a t) d")
    out_f = out_d.rearrange("a t d -> (a t) d")

    with ExitStack() as ctx:
        def sb(name, shape):
            return ctx.enter_context(nc.sbuf_tensor(name, shape, F32))

        def sb_halves(name, shape):
            with nc.sbuf_tensor(name + "_in", shape, F32) as loaded:
                pass
            return sb(name, shape), loaded

        def sem(name):
            return ctx.enter_context(nc.semaphore(name))

        table = sb("table", [P, TW])

        def tab(name):
            a, b = table_at[name]
            return table[:, a:b]

        ident = tab("ident")
        zero_row = tab("masks")[P - 1:P, 0:P]
        decay = tab("decay").rearrange("p (r g i) -> p r g i", r=MR, g=MG // 2)
        causal = tab("causal")
        query_decay = tab("query").rearrange("p (g i) -> p g i", g=MG // 2)
        whole_decay = tab("whole")
        key_decay = tab("key")
        masks = tab("masks")
        win_s, win_in = sb_halves("win_s", [P, 2, DC, 2 * ME])
        wq_s, wq_in = sb_halves("wq_s", [P, 2, DC, ME])
        wk_s, wk_in = sb_halves("wk_s", [P, 2, DC, ME])
        wout_s = sb("wout_s", [P, ME // P, D])
        wqkv_s, wqkv_in = sb_halves("wqkv_s", [P, 2, DC, 3 * E])
        wo_s, wo_in = sb_halves("wo_s", [P, 2, E // P, D])
        w1_s = sb("w1_s", [P, DC, 2 * HIDP])
        w2_s = sb("w2_s", [P, HC, D])
        b1_s = [sb(f"b1_s{l}", [P, 2 * HC]) for l in range(LAYERS)]
        b2_s = sb("b2_s", [P, D])
        rot_scale = [sb(f"rot_scale{l}", [P, 4, 2, HD // 2]) for l in range(LAYERS)]
        bias_mix = sb("bias_mix", [P, 4, ME])
        out_w_s = sb("out_w_s", [P, D])
        out_b_s = sb("out_b_s", [P, D])
        cols = sb("cols", [P, ROWS])
        head_scale = sb("head_scale", [P, MH])
        head_eps = sb("head_eps", [P, MH])
        smear_s = sb("smear_s", [P, MG])
        keep_s = sb("keep_s", [P, MG])
        half_neg = sb("half_neg", [P, 16])
        zero_col = sb("zero_col", [P, 1])
        paced = sb("paced", [P, 1])

        x_s = sb("x_s", [P, 2, D])
        xn = sb("xn", [P, 2, D])
        xh = sb("xh", [P, D])
        xhT = sb("xhT", [P, 2, DC, P])
        stats_x = sb("stats_x", [P, 6])
        mv_x = sb("mv_x", [P, 2])
        small_x = sb("small_x", [P, 4])
        mix_work = sb("mix_work", [P, 4 * 4 * P])
        qk = mix_work[:, 0:2 * ME]
        p_lin = mix_work[:, 2 * ME:3 * ME]
        p_tanh = mix_work[:, 3 * ME:4 * ME]
        att = mix_work[:, :].rearrange("p (r g i) -> p r g i", r=MR, g=MG)
        gate = sb("gate", [P, ME])
        qk_max = sb("qk_max", [P, 2 * MH])
        qk_sum = sb("qk_sum", [P, 2 * MH])
        k_norm = sb("k_norm", [P, MH])
        q_eps = sb("q_eps", [P, MH])
        v_mix = sb("v_mix", [P, MH, MV])
        qT_mix = sb("qT_mix", [P, MG, P])
        qT_dec = sb("qT_dec", [P, MG // 2, P])
        kT_raw = sb("kT_raw", [P, MG, P + 1])
        kT_mix = sb("kT_mix", [P, MG, P])
        go = sb("go", [P, MG * P])
        k_dec = sb("k_dec", [P, ME])
        goT = k_dec[:, :].rearrange("p (g i) -> p g i", g=MG)
        state = sb("state", [P, MG, MR * MV])
        o_den = sb("o_den", [P, 2, 2 * MR])
        o_rec = sb("o_rec", [P, 2, 2 * MR])
        stats_y = sb("stats_y", [P, 6])
        mv_y = sb("mv_y", [P, 2])
        small_y = sb("small_y", [P, 2])
        y_n = sb("y_n", [P, D])
        s_out = sb("s_out", [P, D])

        rot_s = sb("rot_s", [P, 2, 4, HD // 2])
        rot_t = sb("rot_t", [P, 4, 2, HD // 2])
        xT = sb("xT", [P, 2, DC, P + 1])
        raw = sb("raw", [P, 2 * E])
        rot = sb("rot", [P, 2 * E])
        rot_other = sb("rot_other", [P, 2 * E])
        sq_sum = sb("sq_sum", [P, 2 * H])
        sq_clip = sb("sq_clip", [P, 2 * H])
        inv_norm = sb("inv_norm", [P, 2, 2 * H])
        v_loc = sb("v_loc", [P, 2, E])
        qT = sb("qT", [P, 2, HP, P])
        kT = sb("kT", [P, 2, HP, 2, P])

        x_res = xn
        prob = sb("prob", [P, H, 2 * P])
        row_max = sb("row_max", [P, H])
        neg_max = sb("neg_max", [P, H])
        row_sum = sb("row_sum", [P, H])
        row_inv = sb("row_inv", [P, H])
        pT = sb("pT", [P, 2, 4, P])
        oT = sb("oT", [P, 2, HP, P])
        x1 = sb("x1", [P, 2, D])
        x1_shift = sb("x1_shift", [P, 2, P])
        x1b = sb("x1b", [P, 2, D])

        stats_h = sb("stats_h", [P, 12])
        mv_h = sb("mv_h", [P, 2])
        small_h = sb("small_h", [P, 2])
        h_n = sb("h_n", [P, D])
        rows_in, rows_mlp = h_n[0:IN_ROWS, 0:P], h_n[32:32 + ROWS - IN_ROWS, 0:P]
        hT_n = sb("hT_n", [P, DC, P])
        gel = sb("gel", [P, HC, P])
        hid = sb("hid", [P, HC, P])
        x2 = sb("x2", [P, D])
        s_in = s_out
        x_in = y_n
        y_tanh = gel[:, 0:2, :].rearrange("p a b -> p (a b)")
        y_out = gate[:, 0:D]

        bank = [ctx.enter_context(nc.psum_tensor(f"bank{i}", [P, 512], F32)) for i in range(8)]
        mix_bank = bank[0:2]
        proj_bank = bank[2]
        att_bank = bank[3:6]
        mlp_bank = bank[6:8]

        mix_pe = Steps(sem("mix_pe"), "xt q k v p qt kt kb s0 s1 s2 s3 o0 o1 st0 st1 gt wout")
        mix_act = Steps(sem("mix_act"), "xt exp tanh halo kt qt gt")
        mix_dve = Steps(sem("mix_dve"), "xl q k max p sum kscale kinv qeps v ksmear kdec "
                        "s0 s1 s2 s3 den0 rec0 o0 go0 den1 rec1 o1 go1 st0 st1 "
                        "ystat yaggr yvar")
        y_dve = Steps(sem("y_dve"), "yn")
        mix_pool = Steps(sem("mix_pool"), "sub kn kkeep qdec gatep gate sdec yrstd yw s")
        norm_dve = Steps(sem("norm_dve"), "stat aggr var xn sq var2 xh")
        norm_pool = Steps(sem("norm_pool"), "rstd rstd2")
        proj_pe = Steps(sem("proj_pe"), "xt q k v qt kt")
        proj_act = Steps(sem("proj_act"), "halo xt q k square v qt kt")
        proj_dve = Steps(sem("proj_dve"), "xl sqsum clip cos rot knorm ql kl")
        proj_pool = Steps(sem("proj_pool"), "table other inv")
        att_pe = Steps(sem("att_pe"), "sa0 sa1 sb0 sb1 ta0 ta1 pva tb0 tb1 pvb wo")
        att_act = Steps(sem("att_act"), "ea0 ea1 eb0 ta0 ta1 eb1 pva tb0 tb1 pvb")
        att_dve = Steps(sem("att_dve"), "sa0 ma0 sa1 ma1 sb0 mb0 ra0 na0 ra1 na1 rb0 nb0 sb1 mb1 "
                        "rb1 nb1 la lb x1")
        att_pool = Steps(sem("att_pool"), "x1b")
        mlp_pe = Steps(sem("mlp_pe"), "ht g0 a0 ga w2")
        mlp_act = Steps(sem("mlp_act"), "ht g0 ga")
        mlp_dve = Steps(sem("mlp_dve"), "stat aggr var hn a0 ga x2")
        mlp_pool = Steps(sem("mlp_pool"), "rstd")
        fin_act = Steps(sem("fin_act"), "tanh")
        fin_dve = Steps(sem("fin_dve"), "u us out")
        x_loaded = [sem(f"x_loaded{i}") for i in range(2)]
        rot_loaded = [sem(f"rot_loaded{i}") for i in range(2)]
        res_loaded = [sem(f"res_loaded{i}") for i in range(2)]
        shifted = [sem(f"shifted{i}") for i in range(2)]
        s_loaded = sem("s_loaded")
        xin_loaded = sem("xin_loaded")
        s_stored = sem("s_stored")
        x2_stored = sem("x2_stored")
        out_stored = sem("out_stored")
        table_loaded = sem("table_loaded")
        rows_loaded = sem("rows_loaded")
        mlp_rows_loaded = sem("mlp_rows_loaded")
        small_loaded = sem("small_loaded")
        wout_loaded = sem("wout_loaded")
        mix_w_loaded = sem("mix_w_loaded")
        wqkv_loaded = sem("wqkv_loaded")
        w1_loaded = sem("w1_loaded")
        wo_loaded = sem("wo_loaded")
        w2_loaded = sem("w2_loaded")
        b2_loaded = sem("b2_loaded")
        pads_zeroed = sem("pads_zeroed")
        setup_pe = Steps(sem("setup_pe"), "cols vp q k mlp_cols b1_0 b1_1")
        setup_act = Steps(sem("setup_act"), "mix_h scale smear q_0 kv_0 wo_0 q_1 kv_1 wo_1")
        setup_dve = Steps(sem("setup_dve"), "cols spread mix_l bias rneg rcopy smear1 smear2 keep eps half mlp_cols "
                          "q_0 kv_0 b1_0 w1_0 wo_0 q_1 kv_1 wo_1 b1_1 w1_1")
        setup_pool = sem("setup_pool")

        ROWS_DMAS = 6
        MLP_ROWS_DMAS = 4 + 4 * LAYERS
        SMALL_DMAS = 3 + MR + 2 * LAYERS + 2
        MIX_W_DMAS = 3
        PADS = 3
        W1_DMAS = 2
        W2_DMAS = 2
        QKV_CUT = {0: 0, NW: 1}
        WO_CUT = {1: 0, NW + 1: 1}
        W1_FOLD = {1: 0, NW + 2: 1}
        POOL_SETUP = 5
        ONCE = Unit(0, 0, 0)

        block = ctx.enter_context(nc.Block())
        row = lambda u: bass.ds(u.number() * P, P)
        window = lambda u: u if u.low < NW else u.back(NW)
        layer = lambda u: 0 if u.low < NW else 1

        def halved(ap):
            return ap.bitcast(F32R)

        def iterations(eng, body):
            edge = 4
            for first, last in ((0, NW), (NW, UNITS)):
                for i in range(first, first + edge):
                    body(Unit(i // 2, i % 2, i))
                low = first + edge
                with eng.Fori(low // 2, last // 2 - 1) as k:
                    body(Unit(k, 0, low))
                    body(Unit(k, 1, low))
                for i in range(last - 2, last):
                    body(Unit(i // 2, i % 2, i))
            for i in range(UNITS, UNITS + 3):
                body(Unit(i // 2, i % 2, i))

        def turn_bank(u, a):
            return proj_bank if u.low < NW else mix_bank[a]

        def norm_cols(n):
            return cols[:, n * DC:(n + 1) * DC]

        def streams(i):
            return (i if i.low < NW else None,
                    i if i.low < UNITS else None,
                    i.back(1) if 1 <= i.low < UNITS + 1 else None,
                    i.back(2) if 2 <= i.low < UNITS + 2 else None,
                    i.back(3) if i.low >= NW + 3 else None)

        @block.sync
        def _(sp):
            sp.dma_start(x_s[:, 0, :], x_f[0:P, :]).then_inc(x_loaded[0], 16)
            sp.wait_ge(pads_zeroed, 1)
            for n, v in enumerate((in_w, in_b, q_w, q_b, k_w, k_b)):
                sp.dma_start(rows_in[n * DC:(n + 1) * DC, :], v.rearrange("(c p) -> c p", p=P)).then_inc(rows_loaded, 16)
            sp.dma_start(table[:, :], table_d).then_inc(table_loaded, 16)
            sp.dma_start(win_in[:, 1, :, :], W_in.rearrange("(c p) n -> p c n", p=P)).then_inc(mix_w_loaded, 16)
            sp.dma_start(wq_in[:, 1, :, :], Wq.rearrange("(c p) n -> p c n", p=P)).then_inc(mix_w_loaded, 16)
            sp.dma_start(wk_in[:, 1, :, :], Wk.rearrange("(c p) n -> p c n", p=P)).then_inc(mix_w_loaded, 16)

            def everywhere(v):
                return v.unsqueeze(0).to_broadcast([P, v.shape[0]])

            def load_wqkv(l):
                sp.dma_start(wqkv_in[:, 1, :, :], wqkv[l].rearrange("(c p) n -> p c n", p=P)).then_inc(wqkv_loaded, 16)

            def load_wo(l):
                sp.dma_start(wo_in[:, 1, :, :], wo[l].rearrange("(c p) n -> p c n", p=P)).then_inc(wo_loaded, 16)

            def load_w1(l):
                w1_v = w1[l].rearrange("(c p) (a n) -> p c a n", p=P, a=2)
                w1_t = w1_s[:, :, :].rearrange("p c (a n) -> p c a n", a=2)
                for a in range(2):
                    sp.dma_start(w1_t[:, :, a, 0:HID], w1_v[:, :, a, :]).then_inc(w1_loaded, 16)

            def load_w2(l):
                sp.dma_start(w2_s[:, 0:HC - 1, :],
                             w2[l][0:(HC - 1) * P, :].rearrange("(m p) n -> p m n", p=P)).then_inc(w2_loaded, 16)
                sp.dma_start(w2_s[0:TAIL, HC - 1, :], w2[l][(HC - 1) * P:HID, :]).then_inc(w2_loaded, 16)

            def load_b2(l):
                sp.dma_start(b2_s[:, :], everywhere(b2[l])).then_inc(b2_loaded, 16)

            load_wqkv(0)
            sp.dma_start(bias_mix[:, 2, :], everywhere(bq)).then_inc(small_loaded, 16)
            sp.dma_start(bias_mix[:, 3, :], everywhere(bk)).then_inc(small_loaded, 16)
            sp.dma_start(head_scale[:, :], everywhere(log_scale)).then_inc(small_loaded, 16)
            for r in range(MR):
                sp.dma_start(smear_s[r * MD:(r + 1) * MD, :],
                             smear.rearrange("(g r) -> r g", r=MR)[r:r + 1, :].to_broadcast([MD, MG]),
                             allow_slow_non_contiguous=True).then_inc(small_loaded, 16)
            for l in range(LAYERS):
                for n, v in enumerate((q_scale[l], k_scale[l])):
                    sp.dma_start(rot_scale[l][:, n, :, :].rearrange("p a f -> p (a f)"),
                                 everywhere(v)).then_inc(small_loaded, 16)
            sp.dma_start(out_w_s[:, :], everywhere(out_w)).then_inc(small_loaded, 16)
            sp.dma_start(out_b_s[:, :], everywhere(out_b)).then_inc(small_loaded, 16)
            sp.dma_start(rot_s[:, 0, :, :].rearrange("p a f -> p (a f)"), rot_d[0:P, :]).then_inc(rot_loaded[0], 16)
            for n, v in enumerate((ln_g[0], ln_b[0], ln_g[1], ln_b[1])):
                sp.dma_start(rows_mlp[n * DC:(n + 1) * DC, :], v.rearrange("(c p) -> c p", p=P))\
                  .then_inc(mlp_rows_loaded, 16)
            for l in range(LAYERS):
                for a in range(2):
                    at = NORM_ROWS - IN_ROWS + (2 * l + a) * HC
                    v = b1[l][a * HID:(a + 1) * HID]
                    full = (HC - 1) * P
                    sp.dma_start(rows_mlp[at:at + HC - 1, :], v[0:full].rearrange("(m p) -> m p", p=P))\
                      .then_inc(mlp_rows_loaded, 16)
                    sp.dma_start(rows_mlp[at + HC - 1:at + HC, 0:TAIL], v[full:HID].unsqueeze(0))\
                      .then_inc(mlp_rows_loaded, 16)
            sp.dma_start(wout_s[:, :, :], W_out.rearrange("(c p) n -> p c n", p=P)).then_inc(wout_loaded, 16)
            sp.wait_ge(table_loaded, 16)
            sp.dma_start(x1_shift[0:1, 0, :], zero_row).then_inc(shifted[0], 16)
            sp.wait_ge(pads_zeroed, PADS)
            load_wo(0)
            load_w1(0)
            load_w2(0)
            load_b2(0)

            def body(i):
                mix, proj, att_u, mlp_u, fin = streams(i)
                if i.low + 1 < NW:
                    n = i.back(-1)
                    rows = row(n)
                    if n.back(2).exists():
                        sp.wait_ge(norm_dve.sem, norm_dve.at("xn", n.back(2)))
                    sp.dma_start(x_s[:, n.parity, :], x_f[rows, :]).then_inc(x_loaded[n.parity], 16)
                elif i.low + 1 < UNITS and i.low + 1 >= NW:
                    n = i.back(-1)
                    rows = row(window(n))
                    sp.wait_ge(x2_stored, 16 * (window(n).number() + 1))
                    if n.low >= NW + 2:
                        sp.wait_ge(proj_pe.sem, proj_pe.at("xt", n.back(2)))
                    else:
                        sp.wait_ge(norm_dve.sem, norm_dve.at("xn", n.back(2)))
                    sp.dma_start(x_s[:, n.parity, :], x2_d[rows, :]).then_inc(x_loaded[n.parity], 16)
                if i.low + 1 < UNITS:
                    n = i.back(-1)
                    rows = row(window(n))
                    if n.back(2).exists():
                        sp.wait_ge(proj_pool.sem, proj_pool.at("table", n.back(2)))
                    sp.dma_start(rot_s[:, n.parity, :, :].rearrange("p a f -> p (a f)"), rot_d[rows, :])\
                      .then_inc(rot_loaded[n.parity], 16)
                if proj is not None and layer(proj) == 1:
                    rows = row(window(proj))
                    sp.wait_ge(att_dve.sem, att_dve.at("x1", proj.back(2)))
                    sp.dma_start(x_res[:, proj.parity, :], x2_d[rows, :]).then_inc(res_loaded[proj.parity], 16)
                if fin is not None:
                    w = window(fin)
                    rows = row(w)
                    sp.wait_ge(fin_dve.sem, fin_dve.at("out", w))
                    sp.dma_start(out_f[rows, :], y_out[:, :]).then_inc(out_stored, 16)
                if mlp_u is not None and layer(mlp_u) == 1:
                    w = window(mlp_u)
                    rows = row(w)
                    if w.low == 0:
                        sp.wait_ge(s_stored, 16 * NW)
                    sp.dma_start(s_in[:, :], s_d[rows, :]).then_inc(s_loaded, 16)
                    sp.dma_start(x_in[:, :], x_f[rows, :]).then_inc(xin_loaded, 16)
                if mlp_u is not None and mlp_u.low == NW - 1:
                    sp.wait_ge(mlp_pe.sem, mlp_pe.at("ga", mlp_u))
                    load_w1(1)
                if proj is not None and proj.low == NW - 1:
                    sp.wait_ge(proj_pe.sem, proj_pe.at("v", proj))
                    load_wqkv(1)
                if att_u is not None:
                    a, p = att_u, att_u.parity
                    sp.wait_ge(att_dve.sem, att_dve.at("x1", a))
                    sp.dma_start(x1_shift[1:P, p, :], x1[0:P - 1, p, P:D]).then_inc(shifted[p], 16)
                    if a.back(1).exists():
                        sp.wait_ge(mlp_dve.sem, mlp_dve.at("hn", a.back(1)))
                    if a.low + 1 < UNITS:
                        last = zero_row if a.low == NW - 1 else x1[P - 1:P, p, P:D]
                        sp.dma_start(x1_shift[0:1, 1 - p, :], last).then_inc(shifted[1 - p], 16)
                if mlp_u is not None and layer(mlp_u) == 0:
                    rows = row(mlp_u)
                    sp.wait_ge(mlp_dve.sem, mlp_dve.at("x2", mlp_u))
                    sp.dma_start(x2_d[rows, :], x2[:, :]).then_inc(x2_stored, 16)
                if mix is not None:
                    rows = row(mix)
                    sp.wait_ge(mix_pool.sem, mix_pool.at("s", mix))
                    sp.dma_start(s_d[rows, :], s_out[:, :]).then_inc(s_stored, 16)
                if att_u is not None and att_u.low == NW - 1:
                    sp.wait_ge(att_pe.sem, att_pe.at("wo", att_u))
                    load_wo(1)
                    sp.wait_ge(att_pool.sem, att_pool.at("x1b", att_u))
                    load_b2(1)
                if mlp_u is not None and mlp_u.low == NW - 1:
                    sp.wait_ge(mlp_pe.sem, mlp_pe.at("w2", mlp_u))
                    load_w2(1)

            iterations(sp, body)
            sp.wait_ge(out_stored, 16 * NW)
            sp.wait_ge(s_stored, 16 * NW)
            sp.wait_ge(x2_stored, 16 * NW)

        @block.gpsimd
        def _(pool):
            pool.memset(h_n[0:32 + ROWS - IN_ROWS, 0:P], 0.0).then_inc(pads_zeroed, 1)
            w1_t = w1_s[:, :, :].rearrange("p c (a n) -> p c a n", a=2)
            pool.memset(w1_t[:, :, :, HID:HIDP], 0.0).then_inc(pads_zeroed, 1)
            pool.memset(w2_s[:, HC - 1, :], 0.0).then_inc(pads_zeroed, 1)
            pool.memset(half_neg[:, :], -0.5).then_inc(setup_pool, 1)
            pool.memset(zero_col[:, :], 0.0).then_inc(setup_pool, 1)
            pool.memset(state[:, :, :], 0.0).then_inc(setup_pool, 1)
            pool.memset(v_mix[:, :, MD:MV], 1.0).then_inc(setup_pool, 1)
            pool.memset(v_loc[:, :, :], 0.0).then_inc(setup_pool, 1)
            pool.wait_ge(setup_pool, POOL_SETUP)

            def root(out, in_, w):
                return pool.tensor_tensor(out, in_, half_neg[:, 0:w], ALU.pow)

            def body(i):
                mix, proj, att_u, mlp_u, fin = streams(i)
                if i.low == 0:
                    norm1(i)
                    norm2(i)
                if mlp_u is not None:
                    pool.wait_ge(mlp_dve.sem, mlp_dve.at("var", mlp_u))
                    root(small_h[:, 1:2], small_h[:, 0:1], 1).then_inc(mlp_pool.done("rstd"), 1)
                if proj is not None:
                    u, p = proj, proj.parity
                    if u.back(1).exists():
                        pool.wait_ge(proj_dve.sem, proj_dve.at("cos", u.back(1)))
                        pool.wait_ge(proj_pool.sem, proj_pool.at("inv", u.back(1)))
                    else:
                        pool.wait_ge(setup_dve.sem, setup_dve.at("half", ONCE))
                    pool.wait_ge(rot_loaded[p], 16 * (u.turn() + 1))
                    pool.tensor_tensor(rot_t[:, :, :, :],
                                       rot_s[:, p, :, :].unsqueeze(2).to_broadcast([P, 4, 2, HD // 2]),
                                       rot_scale[layer(u)][:, :, :, :], ALU.mult).then_inc(proj_pool.done("table"), 1)
                if proj is not None:
                    u = proj
                    pool.wait_ge(proj_act.sem, proj_act.at("k", u))
                    pool.wait_ge(proj_pool.sem, proj_pool.at("table", u))
                    r5 = raw[:, :].rearrange("p (a h s f) -> p a h s f", a=2, h=H, s=2)
                    o5 = rot_other[:, :].rearrange("p (a h s f) -> p a h s f", a=2, h=H, s=2)
                    for a in range(2):
                        for s in range(2):
                            ins = pool.tensor_tensor(o5[:, a, :, s, :], r5[:, a, :, 1 - s, :],
                                                     rot_t[:, 2 + a, s, :].unsqueeze(1).to_broadcast([P, H, HD // 2]),
                                                     ALU.mult)
                    ins.then_inc(proj_pool.done("other"), 1)
                if mix is not None:
                    n = mix
                    pool.wait_ge(mix_dve.sem, mix_dve.at("max", n))
                    qk_h = qk.rearrange("p (h d) -> p h d", d=MD)
                    pool.tensor_tensor(qk_h, qk_h, qk_max[:, :].unsqueeze(2).to_broadcast([P, 2 * MH, MD]),
                                       ALU.subtract).then_inc(mix_pool.done("sub"), 1)
                if proj is not None:
                    u, p = proj, proj.parity
                    pool.wait_ge(proj_dve.sem, proj_dve.at("clip", u))
                    root(inv_norm[:, p, :], sq_clip[:, :], 2 * H).then_inc(proj_pool.done("inv"), 1)
                if mix is not None:
                    n = mix
                    pool.wait_ge(mix_dve.sem, mix_dve.at("kinv", n))
                    k_h = qk[:, ME:2 * ME].rearrange("p (h d) -> p h d", d=MD)
                    pool.tensor_tensor(k_h, k_h, k_norm[:, :].unsqueeze(2).to_broadcast([P, MH, MD]),
                                       ALU.mult).then_inc(mix_pool.done("kn"), 1)
                    pool.wait_ge(mix_act.sem, mix_act.at("kt", n))
                    pool.tensor_tensor(kT_mix[:, :, :], kT_raw[:, :, 1:P + 1],
                                       keep_s[:, :].unsqueeze(2).to_broadcast([P, MG, P]),
                                       ALU.mult).then_inc(mix_pool.done("kkeep"), 1)
                    pool.wait_ge(mix_act.sem, mix_act.at("qt", n))
                    pool.tensor_tensor(qT_dec[:, :, :], qT_mix[:, 0:MG // 2, :], query_decay,
                                       ALU.mult).then_inc(mix_pool.done("qdec"), 1)
                    pool.wait_ge(mix_act.sem, mix_act.at("tanh", n))
                    pool.tensor_tensor(gate[:, :], p_tanh, p_lin, ALU.mult).then_inc(mix_pool.done("gatep"), 1)
                    pool.wait_ge(mix_pool.sem, mix_pool.at("gatep", n))
                    pool.tensor_tensor(gate[:, :], gate[:, :], p_lin, ALU.add).then_inc(mix_pool.done("gate"), 1)
                if i.low + 1 < NW:
                    norm1(i.back(-1))
                if att_u is not None:
                    if window(att_u).low == 0:
                        pool.wait_ge(b2_loaded, 16 * (layer(att_u) + 1))
                    pool.wait_ge(att_dve.sem, att_dve.at("x1", att_u))
                    pool.tensor_tensor(x1b[:, att_u.parity, :], x1[:, att_u.parity, :], b2_s[:, :],
                                       ALU.add).then_inc(att_pool.done("x1b"), 1)
                if i.low + 1 < NW:
                    norm2(i.back(-1))
                if mix is not None:
                    pool.wait_ge(mix_pe.sem, mix_pe.at("o1", mix))
                    pool.tensor_tensor(state[:, :, :], state[:, :, :],
                                       whole_decay.unsqueeze(2).to_broadcast([P, MG, MR * MV]),
                                       ALU.mult).then_inc(mix_pool.done("sdec"), 1)
                if mix is not None:
                    n = mix
                    pool.wait_ge(mix_dve.sem, mix_dve.at("yvar", n))
                    root(small_y[:, 1:2], small_y[:, 0:1], 1).then_inc(mix_pool.done("yrstd"), 1)
                    pool.wait_ge(y_dve.sem, y_dve.at("yn", n))
                    pool.tensor_tensor(y_n[:, :], y_n[:, :], out_w_s[:, :], ALU.mult)\
                        .then_inc(mix_pool.done("yw"), 1)
                    if n.back(1).exists():
                        pool.wait_ge(s_stored, 16 * n.number())
                    pool.wait_ge(mix_pool.sem, mix_pool.at("yw", n))
                    pool.tensor_tensor(s_out[:, :], y_n[:, :], out_b_s[:, :], ALU.add)\
                        .then_inc(mix_pool.done("s"), 1)

            def norm1(n):
                pool.wait_ge(norm_dve.sem, norm_dve.at("var", n))
                root(small_x[:, 1:2], small_x[:, 0:1], 1).then_inc(norm_pool.done("rstd"), 1)

            def norm2(n):
                pool.wait_ge(norm_dve.sem, norm_dve.at("var2", n))
                root(small_x[:, 3:4], small_x[:, 2:3], 1).then_inc(norm_pool.done("rstd2"), 1)

            iterations(pool, body)

        @block.scalar
        def _(act):
            def copy(out, in_):
                return act.activation(out, in_, ACT.Copy)

            act.wait_ge(mix_w_loaded, 16 * MIX_W_DMAS)
            act.wait_ge(setup_dve.sem, setup_dve.at("cols", ONCE))
            for n, (w, w_in) in enumerate(((win_s, win_in), (wq_s, wq_in), (wk_s, wk_in))):
                for c in range(DC):
                    ins = act.activation(halved(w[:, 0, c, :]), w_in[:, 1, c, :], ACT.Copy,
                                         scale=norm_cols(2 * n)[:, c:c + 1])
            ins.then_inc(setup_act.done("mix_h"), 1)
            act.wait_ge(small_loaded, 16 * SMALL_DMAS)
            act.activation(head_scale[:, :], head_scale[:, :], ACT.Exp).then_inc(setup_act.done("scale"), 1)
            act.activation(smear_s[:, :], smear_s[:, :], ACT.Exp, scale=-1.0).then_inc(setup_act.done("smear"), 1)
            act.wait_ge(setup_pool, POOL_SETUP)

            def cut_qkv(l, name, cols):
                act.wait_ge(wqkv_loaded, 16 * (l + 1))
                copy(halved(wqkv_s[:, 0, :, cols]), wqkv_in[:, 1, :, cols]).then_inc(setup_act.done(f"{name}_{l}"), 1)

            def cut_wo(l):
                act.wait_ge(wo_loaded, 16 * (l + 1))
                copy(halved(wo_s[:, 0, :, :]), wo_in[:, 1, :, :]).then_inc(setup_act.done(f"wo_{l}"), 1)

            def exps(step, a):
                s = list(STEP_HEADS).index(step)
                act.wait_ge(att_dve.sem, att_dve.at("m" + step, a))
                for j, h in enumerate(STEP_HEADS[step]):
                    c = 2 * s + j
                    ins = act.activation(prob[:, h, :], prob[:, h, :], ACT.Exp, bias=neg_max[:, c:c + 1],
                                         scale=QK_SCALE, accum_out=row_sum[:, c:c + 1])
                ins.then_inc(att_act.done("e" + step), 1)

            def turned(step, half, a, b):
                act.wait_ge(att_pe.sem, att_pe.at("t" + step, a))
                copy(pT[:, half, :, :], b[:, :].rearrange("p (b i) -> p b i", b=4))\
                    .then_inc(att_act.done("t" + step), 1)

            def last_gates(m):
                bias = b1_s[layer(m)]
                act.wait_ge(mlp_pe.sem, mlp_pe.at("ga", m))
                for j in range(4, HC):
                    ins = act.activation(gel[:, j, :], mlp_bank[0][:, (j - 4) * P:(j - 3) * P], ACT.Gelu,
                                         bias=bias[:, HC + j:HC + j + 1])
                ins.then_inc(mlp_act.done("ga"), 1)

            def body(i):
                mix, proj, a, m, f = streams(i)
                if i.low in QKV_CUT:
                    cut_qkv(QKV_CUT[i.low], "q", slice(0, E))
                if proj is not None:
                    act.wait_ge(proj_pe.sem, proj_pe.at("xt", proj))
                    if proj.back(1).exists():
                        act.wait_ge(proj_dve.sem, proj_dve.at("xl", proj.back(1)))
                    if window(proj).low > 0:
                        copy(halved(xT[:, :, 1, 0:1]), halved(xT[:, :, 1, P:P + 1])).then_inc(proj_act.done("halo"), 1)
                    else:
                        copy(halved(xT[:, :, 1, 0:1]), zero_col[:, :].unsqueeze(1).to_broadcast([P, 2, 1]))\
                            .then_inc(proj_act.done("halo"), 1)
                    act.wait_ge(proj_act.sem, proj_act.at("halo", proj))
                    copy(halved(xT[:, 0, :, 1:P + 1]), proj_bank[:, 0:D].rearrange("p (c t) -> p c t", c=DC))\
                        .then_inc(proj_act.done("xt"), 1)
                if mix is not None:
                    act.wait_ge(mix_pe.sem, mix_pe.at("xt", mix))
                    copy(halved(xhT[:, 0, :, :]), mix_bank[0][:, 0:D].rearrange("p (c t) -> p c t", c=DC))\
                        .then_inc(mix_act.done("xt"), 1)
                if i.low in QKV_CUT:
                    cut_qkv(QKV_CUT[i.low], "kv", slice(E, 3 * E))
                if f is not None:
                    act.wait_ge(mlp_dve.sem, mlp_dve.at("x2", f))
                    act.activation(y_tanh, x2[:, :], ACT.Tanh, scale=0.5).then_inc(fin_act.done("tanh"), 1)
                if a is not None:
                    exps("a0", a)
                if proj is not None:
                    act.wait_ge(proj_pe.sem, proj_pe.at("q", proj))
                    copy(raw[:, 0:E], proj_bank[:, :]).then_inc(proj_act.done("q"), 1)
                if a is not None:
                    exps("a1", a)
                    exps("b0", a)
                if proj is not None:
                    act.wait_ge(proj_pe.sem, proj_pe.at("k", proj))
                    copy(raw[:, E:2 * E], proj_bank[:, :]).then_inc(proj_act.done("k"), 1)
                if m is not None:
                    act.wait_ge(mlp_pe.sem, mlp_pe.at("ht", m))
                    copy(hT_n[:, :, :], mlp_bank[1][:, 0:D].rearrange("p (c t) -> p c t", c=DC))\
                        .then_inc(mlp_act.done("ht"), 1)
                if proj is not None:
                    act.wait_ge(proj_act.sem, proj_act.at("k", proj))
                    act.activation(rot[:, :], raw[:, :], ACT.Square).then_inc(proj_act.done("square"), 1)
                if a is not None:
                    for k in range(2):
                        turned(f"a{k}", k, a, att_bank[k])
                if mix is not None:
                    act.wait_ge(mix_pool.sem, mix_pool.at("sub", mix))
                    act.activation(qk, qk, ACT.Exp).then_inc(mix_act.done("exp"), 1)
                if a is not None:
                    exps("b1", a)
                if mix is not None:
                    act.wait_ge(mix_dve.sem, mix_dve.at("p", mix))
                    act.activation(p_tanh, p_lin, ACT.Tanh, scale=0.5).then_inc(mix_act.done("tanh"), 1)
                if i.low in WO_CUT:
                    cut_wo(WO_CUT[i.low])
                if m is not None:
                    bias = b1_s[layer(m)]
                    if f is not None:
                        act.wait_ge(fin_dve.sem, fin_dve.at("u", window(f)))
                    act.wait_ge(mlp_pe.sem, mlp_pe.at("g0", m))
                    for j in range(4):
                        ins = act.activation(gel[:, j, :], mlp_bank[0][:, j * P:(j + 1) * P], ACT.Gelu,
                                             bias=bias[:, HC + j:HC + j + 1])
                    ins.then_inc(mlp_act.done("g0"), 1)
                if a is not None:
                    act.wait_ge(att_pe.sem, att_pe.at("pva", a))
                    copy(halved(oT[:, 0, 0:2, :]), att_bank[0][:, 0:2 * P].rearrange("p (b i) -> p b i", b=2))\
                        .then_inc(att_act.done("pva"), 1)
                if mix is not None:
                    act.wait_ge(mix_pe.sem, mix_pe.at("kt", mix))
                    if mix.low > 0:
                        copy(kT_raw[:, :, 0:1], kT_raw[:, :, P:P + 1]).then_inc(mix_act.done("halo"), 1)
                    else:
                        copy(kT_raw[:, :, 0:1], zero_col[:, :].unsqueeze(1).to_broadcast([P, MG, 1]))\
                            .then_inc(mix_act.done("halo"), 1)
                    act.wait_ge(mix_act.sem, mix_act.at("halo", mix))
                    copy(kT_raw[:, :, 1:P + 1], mix_bank[0][:, :].rearrange("p (g i) -> p g i", g=MG))\
                        .then_inc(mix_act.done("kt"), 1)
                if mix is not None:
                    act.wait_ge(mix_pe.sem, mix_pe.at("qt", mix))
                    copy(qT_mix[:, :, :], mix_bank[1][:, :].rearrange("p (g i) -> p g i", g=MG))\
                        .then_inc(mix_act.done("qt"), 1)
                if a is not None:
                    for k in range(2):
                        turned(f"b{k}", k, a, att_bank[1 + k])
                if m is not None and mix is None:
                    last_gates(m)
                if a is not None:
                    act.wait_ge(att_pe.sem, att_pe.at("pvb", a))
                    copy(halved(oT[:, 0, 2:4, :]), att_bank[0][:, 0:2 * P].rearrange("p (b i) -> p b i", b=2))\
                        .then_inc(att_act.done("pvb"), 1)
                if proj is not None:
                    act.wait_ge(proj_pe.sem, proj_pe.at("v", proj))
                    if a is not None:
                        act.wait_ge(att_pe.sem, att_pe.at("pvb", a))
                    copy(v_loc[:, proj.parity, :], proj_bank[:, :]).then_inc(proj_act.done("v"), 1)
                if proj is not None:
                    act.wait_ge(proj_pe.sem, proj_pe.at("qt", proj))
                    copy(halved(qT[:, 0, :, :]), turn_bank(proj, 0)[:, :].rearrange("p (g i) -> p g i", g=HP))\
                        .then_inc(proj_act.done("qt"), 1)
                if m is not None and mix is not None:
                    last_gates(m)
                if mix is not None:
                    act.wait_ge(mix_pe.sem, mix_pe.at("gt", mix))
                    copy(goT, mix_bank[0][:, :].rearrange("p (g i) -> p g i", g=MG))\
                        .then_inc(mix_act.done("gt"), 1)
                if proj is not None:
                    act.wait_ge(proj_pe.sem, proj_pe.at("kt", proj))
                    if window(proj).low == 0:
                        copy(halved(kT[:, :, :, 1 - proj.parity, :]),
                             zero_col[:, :].unsqueeze(1).unsqueeze(2).to_broadcast([P, 2, HP, P]))
                    copy(halved(kT[:, 0, :, proj.parity, :]), turn_bank(proj, 1)[:, :].rearrange("p (g i) -> p g i", g=HP))\
                        .then_inc(proj_act.done("kt"), 1)

            iterations(act, body)

        @block.vector
        def _(dve):
            spread = rot_other[:, 0:3 * DC * P].rearrange("p (n c t) -> p n c t", n=3, c=DC)

            def pace():
                dve.memset(paced[:, :], 0.0)

            def norm1(n):
                p = n.parity
                dve.wait_ge(x_loaded[p], 16 * (n.turn() + 1))
                dve.bn_stats(stats_x[:, :], x_s[:, p, :]).then_inc(norm_dve.done("stat"), 1)
                dve.wait_ge(norm_dve.sem, norm_dve.at("stat", n))
                pace()
                dve.bn_aggr(mv_x[:, :], stats_x[:, :]).then_inc(norm_dve.done("aggr"), 1)
                dve.wait_ge(norm_dve.sem, norm_dve.at("aggr", n))
                dve.tensor_scalar(small_x[:, 0:1], mv_x[:, 1:2], EPS, None, ALU.add)\
                   .then_inc(norm_dve.done("var"), 1)

            def norm2(n):
                p = n.parity
                dve.wait_ge(norm_pool.sem, norm_pool.at("rstd", n))
                if n.back(2).exists():
                    dve.wait_ge(att_dve.sem, att_dve.at("x1", n.back(2)))
                dve.tensor_scalar(xn[:, p, :], x_s[:, p, :], mv_x[:, 0:1], small_x[:, 1:2],
                                  ALU.subtract, ALU.mult).then_inc(norm_dve.done("xn"), 1)
                dve.tensor_scalar(small_x[:, 2:3], mv_x[:, 1:2], small_x[:, 1:2], small_x[:, 1:2],
                                  ALU.mult, ALU.mult).then_inc(norm_dve.done("sq"), 1)
                dve.wait_ge(norm_dve.sem, norm_dve.at("sq", n))
                dve.tensor_scalar(small_x[:, 2:3], small_x[:, 2:3], EPS, None, ALU.add)\
                   .then_inc(norm_dve.done("var2"), 1)

            def norm3(n):
                p = n.parity
                dve.wait_ge(norm_pool.sem, norm_pool.at("rstd2", n))
                if n.back(1).exists():
                    dve.wait_ge(mix_pe.sem, mix_pe.at("xt", n.back(1)))
                dve.tensor_scalar(xh[:, :], xn[:, p, :], small_x[:, 3:4], None, ALU.mult)\
                   .then_inc(norm_dve.done("xh"), 1)

            def scores(step, a, b):
                s = list(STEP_HEADS).index(step)
                at = (2 if window(a).low == 0 else a.parity) * P
                mask = masks[:, at:at + 2 * P]
                dve.wait_ge(att_pe.sem, att_pe.at("s" + step, a))
                pace()
                for j, h in enumerate(STEP_HEADS[step]):
                    c = 2 * s + j
                    ins = dve.tensor_tensor_reduce(prob[:, h, :], b[:, j * 2 * P:(j + 1) * 2 * P], mask,
                                                   inv_norm[:, a.parity, h:h + 1], -3e38, ALU.add, ALU.max,
                                                   row_max[:, c:c + 1])
                ins.then_inc(att_dve.done("s" + step), 1)
                dve.wait_ge(att_dve.sem, att_dve.at("s" + step, a))
                dve.tensor_scalar(neg_max[:, 2 * s:2 * s + 2], row_max[:, 2 * s:2 * s + 2], -QK_SCALE, None,
                                  ALU.mult).then_inc(att_dve.done("m" + step), 1)

            def weigh(step, a):
                s = list(STEP_HEADS).index(step)
                dve.wait_ge(att_act.sem, att_act.at("e" + step, a))
                dve.reciprocal(row_inv[:, 2 * s:2 * s + 2], row_sum[:, 2 * s:2 * s + 2])\
                   .then_inc(att_dve.done("r" + step), 1)
                dve.wait_ge(att_dve.sem, att_dve.at("r" + step, a))
                for j, h in enumerate(STEP_HEADS[step]):
                    c = 2 * s + j
                    ins = dve.tensor_scalar(prob[:, h, :], prob[:, h, :], row_inv[:, c:c + 1], None, ALU.mult)
                ins.then_inc(att_dve.done("n" + step), 1)

            def heads(ap):
                return ap.rearrange("p (h d) -> p h d", d=MD)

            def mix_read(mix, g):
                b = mix_bank[g // 2][:, 0:2 * MR * MV].rearrange("p (h d) -> p h d", d=MV)
                k = str(g // 2)
                den, rec = o_den[:, g // 2, :], o_rec[:, g // 2, :]
                cols = slice(g * P, (g + 2) * P)
                dve.wait_ge(mix_pe.sem, mix_pe.at("o" + k, mix))
                dve.scalar_tensor_tensor(den, b[:, :, MD], 2.0, q_eps[:, g * MR:(g + 2) * MR],
                                         ALU.mult, ALU.add).then_inc(mix_dve.done("den" + k), 1)
                dve.wait_ge(mix_dve.sem, mix_dve.at("den" + k, mix))
                dve.reciprocal(rec, den).then_inc(mix_dve.done("rec" + k), 1)
                dve.wait_ge(mix_dve.sem, mix_dve.at("rec" + k, mix))
                dve.tensor_tensor(heads(go[:, cols]), b[:, :, 0:MD],
                                  rec.unsqueeze(2).to_broadcast([P, 2 * MR, MD]), ALU.mult)\
                   .then_inc(mix_dve.done("o" + k), 1)
                dve.wait_ge(mix_dve.sem, mix_dve.at("o" + k, mix))
                dve.tensor_tensor(go[:, cols], go[:, cols], gate[:, cols], ALU.mult)\
                   .then_inc(mix_dve.done("go" + k), 1)

            def state_add(mix, g):
                k = str(g // 2)
                b = mix_bank[g // 2][:, 0:2 * MR * MV].rearrange("p (g c) -> p g c", g=2)
                dve.wait_ge(mix_pe.sem, mix_pe.at("st" + k, mix))
                dve.wait_ge(mix_pool.sem, mix_pool.at("sdec", mix))
                for r in range(MR):
                    rows, cols = slice(r * MD, (r + 1) * MD), slice(r * MV, (r + 1) * MV)
                    ins = dve.tensor_tensor(state[rows, g:g + 2, cols], b[rows, :, cols],
                                            state[rows, g:g + 2, cols], ALU.add)
                ins.then_inc(mix_dve.done("st" + k), 1)

            def decay_scores(mix, r):
                b = mix_bank[r % 2][:, :].rearrange("p (g i) -> p g i", g=MG)
                dve.wait_ge(mix_pe.sem, mix_pe.at(f"s{r}", mix))
                dve.tensor_tensor(att[:, r, 0:MG // 2, :], b[:, 0:MG // 2, :], decay[:, r, :, :], ALU.mult)
                dve.tensor_tensor(att[:, r, MG // 2:MG, :], b[:, MG // 2:MG, :],
                                  causal.unsqueeze(1).to_broadcast([P, MG // 2, P]), ALU.mult)\
                   .then_inc(mix_dve.done(f"s{r}"), 1)

            def hidden_tail(m):
                bias = b1_s[layer(m)]
                dve.wait_ge(mlp_act.sem, mlp_act.at("ga", m))
                for j in range(4, HC):
                    ins = dve.scalar_tensor_tensor(hid[:, j, :], mlp_bank[0][:, (j - 2) * P:(j - 1) * P],
                                                   bias[:, j:j + 1], gel[:, j, :], ALU.add, ALU.mult)
                ins.then_inc(mlp_dve.done("ga"), 1)

            def first_norm():
                norm1(Unit(0, 0, 0))
                norm2(Unit(0, 0, 0))
                norm3(Unit(0, 0, 0))

            first_norm()
            dve.wait_ge(setup_pe.sem, setup_pe.at("cols", ONCE))
            dve.tensor_copy(cols[:, 0:IN_ROWS], bank[4][:, 0:IN_ROWS]).then_inc(setup_dve.done("cols"), 1)
            dve.wait_ge(setup_dve.sem, setup_dve.at("cols", ONCE))
            for n in range(3):
                ins = dve.tensor_copy(spread[:, n, :, :],
                                      norm_cols(2 * n + 1).unsqueeze(2).to_broadcast([P, DC, P]))
            ins.then_inc(setup_dve.done("spread"), 1)
            dve.wait_ge(setup_pe.sem, setup_pe.at("vp", ONCE))
            dve.tensor_copy(bias_mix[:, 0, :], bank[0][:, :])
            dve.tensor_copy(bias_mix[:, 1, :], bank[1][:, :])
            dve.wait_ge(setup_pe.sem, setup_pe.at("k", ONCE))

            def low(w, w_in, c, scale):
                return dve.scalar_tensor_tensor(halved(w[:, 1, c, :]), w_in[:, 1, c, :], norm_cols(scale)[:, c:c + 1],
                                                w[:, 0, c, :], ALU.mult, ALU.subtract)

            dve.wait_ge(setup_act.sem, setup_act.at("mix_h", ONCE))
            for n, (w, w_in) in enumerate(((win_s, win_in), (wq_s, wq_in), (wk_s, wk_in))):
                for c in range(DC):
                    ins = low(w, w_in, c, 2 * n)
            ins.then_inc(setup_dve.done("mix_l"), 1)

            dve.wait_ge(small_loaded, 16 * SMALL_DMAS)
            dve.tensor_tensor(bias_mix[:, 2, :], bank[2][:, :], bias_mix[:, 2, :], ALU.add)
            dve.tensor_tensor(bias_mix[:, 3, :], bank[3][:, :], bias_mix[:, 3, :], ALU.add)\
               .then_inc(setup_dve.done("bias"), 1)
            for l in range(LAYERS):
                ins = dve.tensor_scalar(rot_scale[l][:, 2:4, 0, :], rot_scale[l][:, 0:2, 1, :], -1.0, None, ALU.mult)
            ins.then_inc(setup_dve.done("rneg"), 1)
            for l in range(LAYERS):
                ins = dve.tensor_copy(rot_scale[l][:, 2:4, 1, :], rot_scale[l][:, 0:2, 0, :])
            ins.then_inc(setup_dve.done("rcopy"), 1)
            dve.wait_ge(setup_act.sem, setup_act.at("smear", ONCE))
            dve.tensor_scalar(smear_s[:, :], smear_s[:, :], 1.0, None, ALU.add).then_inc(setup_dve.done("smear1"), 1)
            dve.wait_ge(setup_dve.sem, setup_dve.at("smear1", ONCE))
            dve.reciprocal(smear_s[:, :], smear_s[:, :]).then_inc(setup_dve.done("smear2"), 1)
            dve.wait_ge(setup_dve.sem, setup_dve.at("smear2", ONCE))
            dve.tensor_scalar(keep_s[:, :], smear_s[:, :], -1.0, 1.0, ALU.mult, ALU.add)\
               .then_inc(setup_dve.done("keep"), 1)
            dve.tensor_scalar(head_eps[:, :], head_scale[:, :], 2 * EPS, None, ALU.mult)\
               .then_inc(setup_dve.done("eps"), 1)
            dve.tensor_scalar(out_w_s[:, :], out_w_s[:, :], 0.5, None, ALU.mult)
            dve.tensor_scalar(out_b_s[:, :], out_b_s[:, :], 0.5, None, ALU.mult)\
               .then_inc(setup_dve.done("half"), 1)
            dve.wait_ge(setup_dve.sem, setup_dve.at("half", ONCE))
            dve.wait_ge(table_loaded, 16)

            dve.wait_ge(setup_pe.sem, setup_pe.at("mlp_cols", ONCE))
            dve.tensor_copy(cols[:, IN_ROWS:ROWS], bank[5][:, 0:ROWS - IN_ROWS]).then_inc(setup_dve.done("mlp_cols"), 1)
            dve.wait_ge(setup_dve.sem, setup_dve.at("mlp_cols", ONCE))

            def cut_qkv(l, name, cols):
                dve.wait_ge(setup_act.sem, setup_act.at(f"{name}_{l}", ONCE))
                dve.tensor_tensor(halved(wqkv_s[:, 1, :, cols]), wqkv_in[:, 1, :, cols], wqkv_s[:, 0, :, cols],
                                  ALU.subtract).then_inc(setup_dve.done(f"{name}_{l}"), 1)

            def cut_wo(l):
                dve.wait_ge(setup_act.sem, setup_act.at(f"wo_{l}", ONCE))
                dve.tensor_tensor(halved(wo_s[:, 1, :, :]), wo_in[:, 1, :, :], wo_s[:, 0, :, :], ALU.subtract)\
                   .then_inc(setup_dve.done(f"wo_{l}"), 1)

            def low_out(a, first, name, steps):
                dve.wait_ge(att_act.sem, att_act.at(name, a))
                dve.tensor_tensor(halved(oT[:, 1, first:first + 2, :]),
                                  att_bank[0][:, 0:2 * P].rearrange("p (b i) -> p b i", b=2),
                                  oT[:, 0, first:first + 2, :], ALU.subtract).then_inc(att_dve.done(steps), 1)

            def low_turned(u, name, done, halves, b):
                dve.wait_ge(proj_act.sem, proj_act.at(name, u))
                dve.tensor_tensor(halved(halves[:, 1]), b[:, :].rearrange("p (g i) -> p g i", g=HP), halves[:, 0],
                                  ALU.subtract).then_inc(proj_dve.done(done), 1)

            def low_x(xt, b):
                return dve.tensor_tensor(halved(xt[:, 1, :, :]), b[:, 0:D].rearrange("p (c t) -> p c t", c=DC),
                                         xt[:, 0, :, :], ALU.subtract)

            def fold(l):
                at = NORM_ROWS + l * 2 * HC
                dve.wait_ge(setup_pe.sem, setup_pe.at(f"b1_{l}", ONCE))
                dve.tensor_tensor(b1_s[l][:, :], proj_bank[:, 0:2 * HC], cols[:, at:at + 2 * HC], ALU.add)\
                   .then_inc(setup_dve.done(f"b1_{l}"), 1)
                for c in range(DC):
                    ins = dve.tensor_scalar(w1_s[:, c, :], w1_s[:, c, :], norm_cols(6 + 2 * l)[:, c:c + 1],
                                            None, ALU.mult)
                ins.then_inc(setup_dve.done(f"w1_{l}"), 1)

            def body(i):
                mix, u, a, m, f = streams(i)
                nxt = i.back(-1) if i.low + 1 < NW else None
                if i.low in QKV_CUT:
                    cut_qkv(QKV_CUT[i.low], "q", slice(0, E))
                if i.low in W1_FOLD:
                    fold(W1_FOLD[i.low])
                if u is not None:
                    dve.wait_ge(proj_act.sem, proj_act.at("xt", u))
                    low_x(xT[:, :, :, 1:P + 1], proj_bank).then_inc(proj_dve.done("xl"), 1)
                if mix is not None:
                    dve.wait_ge(mix_act.sem, mix_act.at("xt", mix))
                    low_x(xhT, mix_bank[0]).then_inc(mix_dve.done("xl"), 1)
                if i.low in QKV_CUT:
                    cut_qkv(QKV_CUT[i.low], "kv", slice(E, 3 * E))
                if 1 <= i.low <= NW:
                    y = i.back(1)
                    dve.wait_ge(mix_pool.sem, mix_pool.at("yrstd", y))
                    dve.tensor_scalar(y_n[:, :], mix_bank[1][:, 0:D], mv_y[:, 0:1], small_y[:, 1:2], ALU.subtract, ALU.mult)\
                       .then_inc(y_dve.done("yn"), 1)
                if a is not None:
                    scores("a0", a, att_bank[0])
                if m is not None:
                    dve.wait_ge(shifted[m.parity], 32 * (m.turn() + 1))
                    dve.bn_stats(stats_h[:, 0:6], x1[:, m.parity, 0:P])
                    dve.bn_stats(stats_h[:, 6:12], x1_shift[:, m.parity, :]).then_inc(mlp_dve.done("stat"), 1)
                    dve.wait_ge(mlp_dve.sem, mlp_dve.at("stat", m))
                    pace()
                    dve.bn_aggr(mv_h[:, :], stats_h[:, :]).then_inc(mlp_dve.done("aggr"), 1)
                    dve.wait_ge(mlp_dve.sem, mlp_dve.at("aggr", m))
                    dve.tensor_scalar(small_h[:, 0:1], mv_h[:, 1:2], EPS, None, ALU.add)\
                       .then_inc(mlp_dve.done("var"), 1)
                if a is not None:
                    scores("a1", a, att_bank[1])
                if m is not None:
                    dve.wait_ge(mlp_pool.sem, mlp_pool.at("rstd", m))
                    dve.tensor_scalar(h_n[:, 0:P], x1[:, m.parity, 0:P], mv_h[:, 0:1], small_h[:, 1:2],
                                      ALU.subtract, ALU.mult)
                    dve.tensor_scalar(h_n[:, P:D], x1_shift[:, m.parity, :], mv_h[:, 0:1], small_h[:, 1:2],
                                      ALU.subtract, ALU.mult).then_inc(mlp_dve.done("hn"), 1)
                if a is not None:
                    scores("b0", a, att_bank[2])
                    weigh("a0", a)
                if mix is not None:
                    dve.wait_ge(mix_pe.sem, mix_pe.at("q", mix))
                    dve.tensor_tensor(qk[:, 0:ME], mix_bank[0][:, :], bias_mix[:, 2, :], ALU.add)\
                       .then_inc(mix_dve.done("q"), 1)
                if a is not None:
                    weigh("a1", a)
                    weigh("b0", a)
                if a is not None and mix is None:
                    scores("b1", a, att_bank[2])
                if f is not None:
                    w = window(f)
                    dve.wait_ge(fin_act.sem, fin_act.at("tanh", w))
                    if w.back(1).exists():
                        dve.wait_ge(out_stored, 16 * w.number())
                    dve.scalar_tensor_tensor(y_out[:, :], y_tanh, 1.0, x2[:, :], ALU.add, ALU.mult)\
                       .then_inc(fin_dve.done("u"), 1)
                    dve.wait_ge(s_loaded, 16 * (w.number() + 1))
                    dve.wait_ge(fin_dve.sem, fin_dve.at("u", w))
                    dve.tensor_tensor(y_out[:, :], y_out[:, :], s_in[:, :], ALU.mult)\
                       .then_inc(fin_dve.done("us"), 1)
                    dve.wait_ge(xin_loaded, 16 * (w.number() + 1))
                    dve.wait_ge(fin_dve.sem, fin_dve.at("us", w))
                    dve.tensor_tensor(y_out[:, :], y_out[:, :], x_in[:, :], ALU.add)\
                       .then_inc(fin_dve.done("out"), 1)
                if mix is not None:
                    dve.wait_ge(mix_pe.sem, mix_pe.at("k", mix))
                    dve.tensor_tensor(qk[:, ME:2 * ME], mix_bank[1][:, :], bias_mix[:, 3, :], ALU.add)\
                       .then_inc(mix_dve.done("k"), 1)
                    dve.wait_ge(mix_dve.sem, mix_dve.at("k", mix))
                    dve.tensor_reduce(qk_max[:, :], heads(qk), AX_X, ALU.max).then_inc(mix_dve.done("max"), 1)
                if u is not None:
                    dve.wait_ge(proj_act.sem, proj_act.at("square", u))
                    dve.tensor_reduce(sq_sum[:, :], rot[:, :].rearrange("p (h d) -> p h d", d=HD), AX_X, ALU.add)\
                       .then_inc(proj_dve.done("sqsum"), 1)
                    dve.wait_ge(proj_dve.sem, proj_dve.at("sqsum", u))
                    dve.tensor_scalar(sq_clip[:, :], sq_sum[:, :], 1e-24, None, ALU.max)\
                       .then_inc(proj_dve.done("clip"), 1)
                if a is not None and mix is not None:
                    scores("b1", a, att_bank[2])
                if mix is not None:
                    dve.wait_ge(mix_pe.sem, mix_pe.at("p", mix))
                    dve.tensor_tensor(p_lin, mix_bank[1][:, :], bias_mix[:, 1, :], ALU.add)\
                       .then_inc(mix_dve.done("p"), 1)
                if mix is not None:
                    dve.wait_ge(mix_act.sem, mix_act.at("exp", mix))
                    dve.tensor_reduce(qk_sum[:, :], heads(qk), AX_X, ALU.add).then_inc(mix_dve.done("sum"), 1)
                    dve.wait_ge(mix_dve.sem, mix_dve.at("sum", mix))
                    dve.tensor_tensor(k_norm[:, :], qk_sum[:, MH:2 * MH], head_scale[:, :], ALU.mult)\
                       .then_inc(mix_dve.done("kscale"), 1)
                    dve.wait_ge(mix_dve.sem, mix_dve.at("kscale", mix))
                    dve.reciprocal(k_norm[:, :], k_norm[:, :]).then_inc(mix_dve.done("kinv"), 1)
                    dve.tensor_tensor(q_eps[:, :], qk_sum[:, 0:MH], head_eps[:, :], ALU.mult)\
                       .then_inc(mix_dve.done("qeps"), 1)
                if a is not None:
                    weigh("b1", a)
                if mix is not None:
                    dve.wait_ge(mix_pe.sem, mix_pe.at("v", mix))
                    dve.tensor_tensor(v_mix[:, :, 0:MD], heads(mix_bank[0][:, :]), heads(bias_mix[:, 0, :]),
                                      ALU.add).then_inc(mix_dve.done("v"), 1)
                if u is not None:
                    four = lambda ap: ap.rearrange("p (a h d) -> p a h d", a=2, h=H)
                    dve.wait_ge(proj_pool.sem, proj_pool.at("table", u))
                    dve.tensor_tensor(four(rot[:, :]), four(raw[:, :]),
                                      rot_t[:, 0:2, :, :].rearrange("p a s f -> p a (s f)").unsqueeze(2)
                                      .to_broadcast([P, 2, H, HD]), ALU.mult).then_inc(proj_dve.done("cos"), 1)
                if a is not None:
                    low_out(a, 0, "pva", "la")
                if u is not None:
                    dve.wait_ge(proj_pool.sem, proj_pool.at("other", u))
                    dve.wait_ge(proj_dve.sem, proj_dve.at("cos", u))
                    dve.tensor_tensor(rot[:, :], rot[:, :], rot_other[:, :], ALU.add)\
                       .then_inc(proj_dve.done("rot"), 1)
                if i.low in WO_CUT:
                    cut_wo(WO_CUT[i.low])
                if mix is not None:
                    dve.wait_ge(mix_pool.sem, mix_pool.at("kkeep", mix))
                    for g in range(MG):
                        ins = dve.scalar_tensor_tensor(kT_mix[:, g, :], kT_raw[:, g, 0:P], smear_s[:, g:g + 1],
                                                       kT_mix[:, g, :], ALU.mult, ALU.add)
                    ins.then_inc(mix_dve.done("ksmear"), 1)
                if u is not None:
                    k_h = rot[:, E:2 * E].rearrange("p (h d) -> p h d", d=HD)
                    dve.wait_ge(proj_pool.sem, proj_pool.at("inv", u))
                    dve.wait_ge(proj_dve.sem, proj_dve.at("rot", u))
                    dve.tensor_tensor(k_h, k_h, inv_norm[:, u.parity, H:2 * H].unsqueeze(2).to_broadcast([P, H, HD]),
                                      ALU.mult).then_inc(proj_dve.done("knorm"), 1)
                if m is not None:
                    bias = b1_s[layer(m)]
                    dve.wait_ge(mlp_pe.sem, mlp_pe.at("a0", m))
                    dve.wait_ge(mlp_act.sem, mlp_act.at("g0", m))
                    for j in range(4):
                        ins = dve.scalar_tensor_tensor(hid[:, j, :], mlp_bank[1][:, j * P:(j + 1) * P],
                                                       bias[:, j:j + 1], gel[:, j, :], ALU.add, ALU.mult)
                    ins.then_inc(mlp_dve.done("a0"), 1)
                if m is not None and mix is None:
                    hidden_tail(m)
                if mix is not None:
                    dve.wait_ge(mix_pe.sem, mix_pe.at("kb", mix))
                    dve.tensor_tensor(heads(k_dec[:, :]), heads(mix_bank[1][:, :]),
                                      key_decay.unsqueeze(2).to_broadcast([P, MH, MD]), ALU.mult)\
                       .then_inc(mix_dve.done("kdec"), 1)
                if mix is not None:
                    decay_scores(mix, 0)
                if mix is not None:
                    decay_scores(mix, 1)
                if u is not None:
                    low_turned(u, "qt", "ql", qT, turn_bank(u, 0))
                if a is not None:
                    low_out(a, 2, "pvb", "lb")
                if u is not None and mix is None:
                    low_turned(u, "kt", "kl", kT[:, :, :, u.parity, :], turn_bank(u, 1))
                if mix is not None:
                    dve.wait_ge(mix_pool.sem, mix_pool.at("gate", mix))
                    for r in range(2, MR):
                        decay_scores(mix, r)
                if m is not None and mix is not None:
                    hidden_tail(m)
                if nxt is not None:
                    norm1(nxt)
                if a is not None:
                    dve.wait_ge(att_pe.sem, att_pe.at("wo", a))
                    if layer(a) == 0:
                        res = xn
                    else:
                        res = x_res
                        dve.wait_ge(res_loaded[a.parity], 16 * (window(a).turn() + 1))
                    dve.tensor_tensor(x1[:, a.parity, :], att_bank[1][:, 0:D], res[:, a.parity, :], ALU.add)\
                       .then_inc(att_dve.done("x1"), 1)
                if mix is not None:
                    mix_read(mix, 0)
                if nxt is not None:
                    norm2(nxt)
                if mix is not None:
                    mix_read(mix, 2)
                if mix is not None:
                    state_add(mix, 0)
                if nxt is not None:
                    norm3(nxt)
                if mix is not None:
                    state_add(mix, 2)
                if u is not None and mix is not None:
                    low_turned(u, "kt", "kl", kT[:, :, :, u.parity, :], turn_bank(u, 1))
                if m is not None:
                    dve.wait_ge(mlp_pe.sem, mlp_pe.at("w2", m))
                    dve.wait_ge(att_pool.sem, att_pool.at("x1b", m))
                    if layer(m) == 1:
                        dve.wait_ge(x2_stored, 16 * NW)
                    elif m.back(1).exists():
                        dve.wait_ge(x2_stored, 16 * m.number())
                    dve.tensor_tensor(x2[:, :], mlp_bank[1][:, 0:D], x1b[:, m.parity, :], ALU.add)\
                       .then_inc(mlp_dve.done("x2"), 1)
                if mix is not None:
                    b = mix_bank[1][:, 0:D]
                    dve.wait_ge(mix_pe.sem, mix_pe.at("wout", mix))
                    dve.bn_stats(stats_y[:, :], b).then_inc(mix_dve.done("ystat"), 1)
                    dve.wait_ge(mix_dve.sem, mix_dve.at("ystat", mix))
                    pace()
                    dve.bn_aggr(mv_y[:, :], stats_y[:, :]).then_inc(mix_dve.done("yaggr"), 1)
                    dve.wait_ge(mix_dve.sem, mix_dve.at("yaggr", mix))
                    dve.tensor_scalar(small_y[:, 0:1], mv_y[:, 1:2], EPS, None, ALU.add)\
                       .then_inc(mix_dve.done("yvar"), 1)

            iterations(dve, body)

        @block.tensor
        def _(pe):
            def mm(out, lhsT, rhs, first, last):
                return pe.matmul(out, lhsT, rhs, start=first, stop=last)

            def mm3(out, left, right, first, last):
                for n, (a, b) in enumerate(((1, 0), (0, 1), (0, 0))):
                    ins = pe.matmul(out, halved(left[:, a]), halved(right[:, b]), start=first and n == 0,
                                    stop=last and n == 2)
                return ins

            def transposes(out, parts):
                for j, part in enumerate(parts):
                    ins = pe.transpose(out[:, j * P:(j + 1) * P], part, ident)
                return ins

            spread = rot_other[:, 0:3 * DC * P].rearrange("p (n c t) -> p n c t", n=3, c=DC)
            pe.wait_ge(rows_loaded, 16 * ROWS_DMAS)
            pe.wait_ge(table_loaded, 16)
            pe.transpose(bank[4][:, 0:IN_ROWS], rows_in, ident[0:IN_ROWS, 0:IN_ROWS])\
              .then_inc(setup_pe.done("cols"), 1)
            pe.wait_ge(setup_dve.sem, setup_dve.at("spread", ONCE))
            pe.wait_ge(mix_w_loaded, 16 * MIX_W_DMAS)
            for t in range(2):
                for c in range(DC):
                    ins = mm(bank[t][:, :], spread[:, 0, c, :], win_in[:, 1, c, t * ME:(t + 1) * ME], c == 0, c == DC - 1)
            ins.then_inc(setup_pe.done("vp"), 1)
            for n, (w, name) in enumerate(((wq_in, "q"), (wk_in, "k"))):
                for c in range(DC):
                    ins = mm(bank[2 + n][:, :], spread[:, 1 + n, c, :], w[:, 1, c, :], c == 0, c == DC - 1)
                ins.then_inc(setup_pe.done(name), 1)
            pe.wait_ge(mlp_rows_loaded, 16 * MLP_ROWS_DMAS)
            at = slice(32, 32 + ROWS - IN_ROWS)
            pe.transpose(bank[5][:, 0:ROWS - IN_ROWS], rows_mlp, ident[at, at]).then_inc(setup_pe.done("mlp_cols"), 1)
            pe.wait_ge(setup_dve.sem, setup_dve.at("bias", ONCE))
            pe.wait_ge(setup_pool, POOL_SETUP)

            def proj_bank_free(u):
                if u.low <= NW:
                    pe.wait_ge(proj_dve.sem, proj_dve.at("kl", u.back(1)))
                else:
                    pe.wait_ge(proj_act.sem, proj_act.at("v", u.back(1)))

            def fold(i, l):
                pe.wait_ge(w1_loaded, 16 * W1_DMAS * (l + 1))
                proj_bank_free(i)
                for j in range(2 * HC):
                    for c in range(DC):
                        ins = mm(proj_bank[:, j:j + 1], w1_s[:, c, j * P:(j + 1) * P],
                                 norm_cols(7 + 2 * l)[:, c:c + 1], c == 0, c == DC - 1)
                ins.then_inc(setup_pe.done(f"b1_{l}"), 1)
                pe.wait_ge(setup_dve.sem, setup_dve.at(f"b1_{l}", ONCE))

            def att_scores(step, a, b):
                for j, h in enumerate(STEP_HEADS[step]):
                    rows = slice(HD * (h % 2), HD * (h % 2) + HD)
                    ins = mm3(b[:, j * 2 * P:(j + 1) * 2 * P], qT[rows, :, h // 2, :],
                              kT[rows, :, h // 2, :, :].rearrange("p t s j -> p t (s j)"), True, True)
                ins.then_inc(att_pe.done("s" + step), 1)

            def att_turn(step, a, b):
                pe.wait_ge(att_dve.sem, att_dve.at("n" + step, a))
                parts = [prob[:, h, s * P:(s + 1) * P] for h in STEP_HEADS[step] for s in range(2)]
                transposes(b, parts).then_inc(att_pe.done("t" + step), 1)

            def att_values(half, a, b):
                for s in range(2):
                    for j, h in enumerate(STEP_HEADS[f"{half}{s}"]):
                        out = b[HD * (h % 2):HD * (h % 2) + HD, j * P:(j + 1) * P]
                        for slot in range(2):
                            ins = mm(out, v_loc[:, slot, h * HD:(h + 1) * HD], pT[:, s, 2 * j + slot, :],
                                     slot == 0, slot == 1)
                ins.then_inc(att_pe.done("pv" + half), 1)

            def mix_linear(mix, step, b, w, col):
                for c in range(DC):
                    ins = mm3(b[:, :], xhT[:, :, c, :], w[:, :, c, col:col + ME], c == 0, c == DC - 1)
                ins.then_inc(mix_pe.done(step), 1)

            def proj_linear(u, step, col):
                for c in range(DC):
                    ins = mm3(proj_bank[:, :], xT[:, :, c, 1 - c:1 - c + P], wqkv_s[:, :, c, col:col + E],
                              c == 0, c == DC - 1)
                ins.then_inc(proj_pe.done(step), 1)

            def hidden(m, b, at, first, count):
                for j in range(count):
                    for c in range(DC):
                        ins = mm(b[:, (at + j) * P:(at + j + 1) * P], w1_s[:, c, (first + j) * P:(first + j + 1) * P],
                                 hT_n[:, c, :], c == 0, c == DC - 1)
                return ins

            def out_projection(a):
                if window(a).low == 0:
                    pe.wait_ge(setup_dve.sem, setup_dve.at(f"wo_{layer(a)}", ONCE))
                pe.wait_ge(att_dve.sem, att_dve.at("lb", a))
                for g in range(HP):
                    ins = mm3(att_bank[1][:, 0:D], oT[:, :, g, :], wo_s[:, :, g, :], g == 0, g == HP - 1)
                ins.then_inc(att_pe.done("wo"), 1)

            def turn_q(u):
                if u.low < NW:
                    pe.wait_ge(proj_act.sem, proj_act.at("v", u))
                if u.low == NW:
                    pe.wait_ge(y_dve.sem, y_dve.at("yn", u.back(1)))
                pe.wait_ge(proj_dve.sem, proj_dve.at("rot", u))
                transposes(turn_bank(u, 0), [rot[:, g * P:(g + 1) * P] for g in range(HP)])\
                    .then_inc(proj_pe.done("qt"), 1)

            def turn_k(u):
                if u.low < NW:
                    pe.wait_ge(proj_dve.sem, proj_dve.at("ql", u))
                pe.wait_ge(proj_dve.sem, proj_dve.at("knorm", u))
                transposes(turn_bank(u, 1), [rot[:, E + g * P:E + (g + 1) * P] for g in range(HP)])\
                    .then_inc(proj_pe.done("kt"), 1)

            def project_q(u):
                if window(u).low == 0:
                    pe.wait_ge(setup_dve.sem, setup_dve.at(f"q_{layer(u)}", ONCE))
                pe.wait_ge(proj_dve.sem, proj_dve.at("xl", u))
                proj_linear(u, "q", 0)

            def first_gates(m):
                if window(m).low == 0:
                    pe.wait_ge(setup_dve.sem, setup_dve.at(f"w1_{layer(m)}", ONCE))
                pe.wait_ge(mlp_act.sem, mlp_act.at("ht", m))
                if m.back(1).exists():
                    pe.wait_ge(mlp_dve.sem, mlp_dve.at("ga", m.back(1)))
                hidden(m, mlp_bank[0], 0, HC, 4).then_inc(mlp_pe.done("g0"), 1)

            def state_sum(mix, k):
                pe.wait_ge(mix_dve.sem, mix_dve.at(f"o{k}", mix))
                for g in (2 * k, 2 * k + 1):
                    at = (g % 2) * MR * MV
                    ins = mm(mix_bank[k][:, at:at + MR * MV], k_dec[:, g * P:(g + 1) * P],
                             v_mix[:, g * MR:(g + 1) * MR, :].rearrange("p h d -> p (h d)"), True, True)
                ins.then_inc(mix_pe.done(f"st{k}"), 1)

            def mlp_out(m, first, last):
                if first == 0:
                    if window(m).low == 0:
                        pe.wait_ge(w2_loaded, 16 * W2_DMAS * (layer(m) + 1))
                    pe.wait_ge(mlp_dve.sem, mlp_dve.at("a0", m))
                if last > 4:
                    pe.wait_ge(mlp_dve.sem, mlp_dve.at("ga", m))
                for j in range(first, last):
                    ins = mm(mlp_bank[1][:, 0:D], hid[:, j, :], w2_s[:, j, :], j == 0, j == HC - 1)
                if last == HC:
                    ins.then_inc(mlp_pe.done("w2"), 1)

            def mix_scores(mix, r):
                steps, name = [(mix_act, "kt"), (mix_dve, "kdec"), (mix_dve, "s0"), (mix_dve, "s1")][r]
                pe.wait_ge(steps.sem, steps.at(name, mix))
                rows = slice(r * MD, (r + 1) * MD)
                for g in range(MG):
                    ins = mm(mix_bank[r % 2][:, g * P:(g + 1) * P], kT_mix[rows, g, :], qT_mix[rows, g, :],
                             True, True)
                ins.then_inc(mix_pe.done(f"s{r}"), 1)

            def mix_out(mix, g):
                q_g = qT_dec[:, g, :] if g < MG // 2 else qT_mix[:, g, :]
                at = (g % 2) * MR * MV
                mm(mix_bank[g // 2][:, at:at + MR * MV], q_g, state[:, g, :], True, False)
                for r in range(MR):
                    ins = mm(mix_bank[g // 2][:, at + r * MV:at + (r + 1) * MV], att[:, r, g, :],
                             v_mix[:, g * MR + r, :], False, r == MR - 1)
                if g % 2 == 1:
                    ins.then_inc(mix_pe.done(f"o{g // 2}"), 1)

            def body(i):
                mix, u, a, m, f = streams(i)
                if i.low in W1_FOLD:
                    fold(i, W1_FOLD[i.low])
                if u is not None:
                    if layer(u) == 0:
                        pe.wait_ge(norm_dve.sem, norm_dve.at("xn", u))
                        src = xn
                    else:
                        pe.wait_ge(x_loaded[u.parity], 16 * (u.turn() + 1))
                        src = x_s
                    if u.back(1).exists():
                        proj_bank_free(u)
                    transposes(proj_bank, [src[:, u.parity, c * P:(c + 1) * P] for c in range(DC)])\
                        .then_inc(proj_pe.done("xt"), 1)
                if mix is not None:
                    pe.wait_ge(norm_dve.sem, norm_dve.at("xh", mix))
                    if mix.back(1).exists():
                        pe.wait_ge(mix_act.sem, mix_act.at("gt", mix.back(1)))
                    transposes(mix_bank[0], [xh[:, c * P:(c + 1) * P] for c in range(DC)])\
                        .then_inc(mix_pe.done("xt"), 1)
                if a is not None:
                    pe.wait_ge(proj_dve.sem, proj_dve.at("kl", a))
                    if a.back(1).exists():
                        pe.wait_ge(att_dve.sem, att_dve.at("lb", a.back(1)))
                    att_scores("a0", a, att_bank[0])
                if a is not None:
                    if a.back(1).exists():
                        pe.wait_ge(att_dve.sem, att_dve.at("x1", a.back(1)))
                    att_scores("a1", a, att_bank[1])
                if u is not None and mix is None:
                    project_q(u)
                if a is not None:
                    if a.back(1).exists():
                        pe.wait_ge(att_act.sem, att_act.at("tb1", a.back(1)))
                    att_scores("b0", a, att_bank[2])
                if u is not None and mix is not None:
                    project_q(u)
                if mix is not None:
                    pe.wait_ge(mix_dve.sem, mix_dve.at("xl", mix))
                    mix_linear(mix, "q", mix_bank[0], wq_s, 0)
                if mix is not None:
                    if mix.back(1).exists():
                        pe.wait_ge(y_dve.sem, y_dve.at("yn", mix.back(1)))
                    mix_linear(mix, "k", mix_bank[1], wk_s, 0)
                if u is not None:
                    if window(u).low == 0:
                        pe.wait_ge(setup_dve.sem, setup_dve.at(f"kv_{layer(u)}", ONCE))
                    pe.wait_ge(proj_act.sem, proj_act.at("q", u))
                    proj_linear(u, "k", E)
                if m is not None:
                    pe.wait_ge(mlp_dve.sem, mlp_dve.at("hn", m))
                    if m.back(1).exists():
                        pe.wait_ge(mlp_dve.sem, mlp_dve.at("x2", m.back(1)))
                    transposes(mlp_bank[1], [h_n[:, c * P:(c + 1) * P] for c in range(DC)])\
                        .then_inc(mlp_pe.done("ht"), 1)
                if a is not None:
                    pe.wait_ge(att_dve.sem, att_dve.at("sb0", a))
                    att_scores("b1", a, att_bank[2])
                if a is not None:
                    att_turn("a0", a, att_bank[0])
                if mix is not None:
                    pe.wait_ge(mix_dve.sem, mix_dve.at("q", mix))
                    mix_linear(mix, "v", mix_bank[0], win_s, 0)
                if a is not None:
                    att_turn("a1", a, att_bank[1])
                if mix is not None:
                    pe.wait_ge(mix_dve.sem, mix_dve.at("k", mix))
                    mix_linear(mix, "p", mix_bank[1], win_s, ME)
                if m is not None:
                    first_gates(m)
                if a is not None:
                    pe.wait_ge(att_act.sem, att_act.at("ta1", a))
                    pe.wait_ge(proj_act.sem, proj_act.at("v", a))
                    att_values("a", a, att_bank[0])
                if m is not None:
                    hidden(m, mlp_bank[1], 0, 0, 4).then_inc(mlp_pe.done("a0"), 1)
                if mix is not None:
                    pe.wait_ge(mix_act.sem, mix_act.at("exp", mix))
                    pe.wait_ge(mix_dve.sem, mix_dve.at("p", mix))
                    transposes(mix_bank[1], [qk[:, g * P:(g + 1) * P] for g in range(MG)])\
                        .then_inc(mix_pe.done("qt"), 1)
                if a is not None:
                    att_turn("b0", a, att_bank[1])
                if u is not None and mix is None:
                    pe.wait_ge(proj_act.sem, proj_act.at("k", u))
                    proj_linear(u, "v", 2 * E)
                if a is not None:
                    att_turn("b1", a, att_bank[2])
                if mix is not None:
                    pe.wait_ge(mix_pool.sem, mix_pool.at("kn", mix))
                    pe.wait_ge(mix_dve.sem, mix_dve.at("v", mix))
                    transposes(mix_bank[0], [qk[:, ME + g * P:ME + (g + 1) * P] for g in range(MG)])\
                        .then_inc(mix_pe.done("kt"), 1)
                if m is not None:
                    pe.wait_ge(mlp_act.sem, mlp_act.at("g0", m))
                    hidden(m, mlp_bank[0], 0, HC + 4, 2)
                if m is not None and mix is None:
                    hidden(m, mlp_bank[0], 2, 4, 2).then_inc(mlp_pe.done("ga"), 1)
                if u is not None and mix is not None:
                    pe.wait_ge(proj_act.sem, proj_act.at("k", u))
                    proj_linear(u, "v", 2 * E)
                if a is not None:
                    pe.wait_ge(att_act.sem, att_act.at("tb1", a))
                    pe.wait_ge(att_dve.sem, att_dve.at("la", a))
                    att_values("b", a, att_bank[0])
                if mix is not None:
                    pe.wait_ge(mix_dve.sem, mix_dve.at("ksmear", mix))
                    pe.wait_ge(mix_act.sem, mix_act.at("qt", mix))
                    transposes(mix_bank[1], [kT_mix[:, g, :] for g in range(MG)]).then_inc(mix_pe.done("kb"), 1)
                if mix is not None:
                    mix_scores(mix, 0)
                if u is not None:
                    turn_q(u)
                if m is not None and mix is None:
                    mlp_out(m, 0, 4)
                if mix is not None:
                    mix_scores(mix, 1)
                if u is not None and mix is None:
                    turn_k(u)
                if m is not None and mix is not None:
                    hidden(m, mlp_bank[0], 2, 4, 2).then_inc(mlp_pe.done("ga"), 1)
                if mix is not None:
                    for r in range(MR // 2, MR):
                        mix_scores(mix, r)
                if a is not None:
                    out_projection(a)
                if mix is not None:
                    pe.wait_ge(mix_pool.sem, mix_pool.at("qdec", mix))
                    if mix.back(1).exists():
                        pe.wait_ge(mix_dve.sem, mix_dve.at("st1", mix.back(1)))
                    pe.wait_ge(mix_dve.sem, mix_dve.at("s3", mix))
                    for g in range(MG):
                        mix_out(mix, g)
                        if m is not None:
                            mlp_out(m, g, g + 1)
                if mix is not None:
                    state_sum(mix, 0)
                if m is not None:
                    mlp_out(m, 4, 5)
                if mix is not None:
                    state_sum(mix, 1)
                if mix is not None:
                    pe.wait_ge(mix_dve.sem, mix_dve.at("st0", mix))
                    pe.wait_ge(mix_dve.sem, mix_dve.at("go1", mix))
                    transposes(mix_bank[0], [go[:, g * P:(g + 1) * P] for g in range(MG)])\
                        .then_inc(mix_pe.done("gt"), 1)
                if m is not None:
                    mlp_out(m, 5, HC)
                if u is not None and mix is not None:
                    turn_k(u)
                if mix is not None:
                    pe.wait_ge(mix_act.sem, mix_act.at("gt", mix))
                    pe.wait_ge(mix_dve.sem, mix_dve.at("st1", mix))
                    if mix.low == 0:
                        pe.wait_ge(wout_loaded, 16)
                    for g in range(MG):
                        ins = mm(mix_bank[1][:, 0:D], goT[:, g, :], wout_s[:, g, :], g == 0, g == MG - 1)
                    ins.then_inc(mix_pe.done("wout"), 1)

            iterations(pe, body)


_INS = ["x", "in_ln_w", "in_ln_b", "q_ln_w", "q_ln_b", "k_ln_w", "k_ln_b", "out_ln_w", "out_ln_b",
        "W_in", "W_out", "Wq", "bq", "Wk", "bk", "smear_factor", "log_scale"]
_FFN = ["wqkv", "q_scale", "k_scale", "wo", "ln_g", "ln_b", "w1", "b1", "w2", "b2"]


def kernel(**inputs):
    import concourse.bacc as _bacc
    from concourse.bass_utils import run_bass_kernel_spmd as _run

    nc = _bacc.Bacc("TRN2", target_bir_lowering=False, num_devices=1)
    table, table_at, rotary = constants()
    arrays, args = {}, []
    named = [(f"L0_attn_{n}", None) for n in _INS] + [(f"L0_ffn_{n}", None) for n in _FFN]
    named += [("table", table), ("rotary", rotary)]
    for name, a in named:
        a = np.ascontiguousarray(inputs[name] if a is None else a)
        arrays[f"in_{name}"] = a
        args.append(nc.dram_tensor(f"in_{name}", a.shape, mybir.dt.from_np(a.dtype), kind="ExternalInput").ap())
    out = nc.dram_tensor("out_0", [1, TOKENS, D], F32, kind="ExternalOutput").ap()
    build(nc, *args, table_at, out)
    r = _run(nc, [arrays], core_ids=[0])
    return r.results[0]["out_0"]
```
